# Optimizing a Trainium2 kernel written in Bass

```python
import numpy as np
import jax
import jax.numpy as jnp

def _softmax(x, axis=-1):
    return jax.nn.softmax(x, axis=axis)

def _gelu(x):
    return jax.nn.gelu(x, approximate=True)

def _silu(x):
    return jax.nn.silu(x)

def _sigmoid(x):
    return jax.nn.sigmoid(x)

def _layernorm(x, axis=-1, eps=1e-05):
    m = jnp.mean(x, axis=axis, keepdims=True)
    v = jnp.var(x, axis=axis, keepdims=True)
    return (x - m) / jnp.sqrt(v + eps)

def _scatter_add(tgt, idx, src, axis=0):
    return tgt.at[idx].add(src)

def _segment_sum(src, seg, n):
    return jax.ops.segment_sum(src, seg, n)
kernel_name = 'mk_audio_tower_d2_tok_audfeat512_r4_7aa64f'

def setup_inputs(seed: int=0):
    np.random.seed(seed)
    _w = jnp.asarray

    def _rec_inputs():
        import jax
        import jax.numpy as jnp
        _rk = jax.random.key(seed)
        x = 7.22013e-05 + 1.00017 * jax.random.normal(jax.random.fold_in(_rk, 1), (32, 512, 128), jnp.float32)
        return x
    x = _rec_inputs()

    def _L0_tok_setup():
        import jax, jax.numpy as jnp
        import numpy as np
        H = 8
        TOP_FRAC = 0.2
        EPS = 1e-05

        def _layernorm(x, g, b):
            mu = jnp.mean(x, axis=-1, keepdims=True)
            var = jnp.mean((x - mu) ** 2, axis=-1, keepdims=True)
            return (x - mu) * jax.lax.rsqrt(var + EPS) * g + b
        key = jax.random.key(seed)
        ks = jax.random.split(key, 8)
        B, L, D, F = (8, 512, 128, 512)
        s = 0.02
        return {'x': jax.random.normal(ks[0], (B, L, D), jnp.float32), 'q_w': jax.random.normal(ks[1], (D, D), jnp.float32) * s, 'q_b': jnp.zeros((D,), jnp.float32), 'k_w': jax.random.normal(ks[2], (D, D), jnp.float32) * s, 'k_b': jnp.zeros((D,), jnp.float32), 'v_w': jax.random.normal(ks[3], (D, D), jnp.float32) * s, 'v_b': jnp.zeros((D,), jnp.float32), 'o_w': jax.random.normal(ks[4], (D, D), jnp.float32) * s, 'o_b': jnp.zeros((D,), jnp.float32), 'ln1_g': jnp.ones((D,), jnp.float32), 'ln1_b': jnp.zeros((D,), jnp.float32), 'f1_w': jax.random.normal(ks[5], (D, F), jnp.float32) * s, 'f1_b': jnp.zeros((F,), jnp.float32), 'f2_w': jax.random.normal(ks[6], (F, D), jnp.float32) * s, 'f2_b': jnp.zeros((D,), jnp.float32), 'ln2_g': jnp.ones((D,), jnp.float32), 'ln2_b': jnp.zeros((D,), jnp.float32), 'conv_w': jax.random.normal(ks[7], (D, D, 3), jnp.float32) * s, 'conv_b': jnp.zeros((D,), jnp.float32)}
    _L0_tok_all = _L0_tok_setup()
    _L0_tok_in = {k: v for k, v in _L0_tok_all.items() if k in ('q_w', 'q_b', 'k_w', 'k_b', 'v_w', 'v_b', 'o_w', 'o_b', 'ln1_g', 'ln1_b', 'f1_w', 'f1_b', 'f2_w', 'f2_b', 'ln2_g', 'ln2_b', 'conv_w', 'conv_b')}
    del _L0_tok_all

    def _L0_attn_setup():
        import jax, jax.numpy as jnp
        import numpy as np
        B, T, D, H, C, WIN = (2, 512, 128, 8, 64, 128)
        EPS = 1e-06

        def _rms_norm(x, w):
            norm = jax.lax.rsqrt(jnp.mean(x * x, axis=-1, keepdims=True) + EPS)
            return x * norm * w

        def _apply_rope(x, cos_p, sin_p):
            half = x.shape[-1] // 2
            x1, x2 = (x[..., :half], x[..., half:])
            rotated = jnp.concatenate([-x2, x1], axis=-1)
            return x * cos_p + rotated * sin_p
        key = jax.random.key(seed)
        ks = jax.random.split(key, 5)
        h = jax.random.normal(ks[0], (B, T, D), dtype=jnp.float32)
        inv_freq = 1.0 / 10000.0 ** (jnp.arange(0, C, 2, dtype=jnp.float32) / C)
        pos = jnp.arange(T, dtype=jnp.float32)
        freqs = pos[:, None] * inv_freq[None, :]
        emb = jnp.concatenate([freqs, freqs], axis=-1)
        rope_cos = jnp.cos(emb)
        rope_sin = jnp.sin(emb)
        scale = 0.02
        W_q = jax.random.normal(ks[1], (D, H * C), dtype=jnp.float32) * scale
        W_k = jax.random.normal(ks[2], (D, H * C), dtype=jnp.float32) * scale
        W_v = jax.random.normal(ks[3], (D, H * C), dtype=jnp.float32) * scale
        W_o = jax.random.normal(ks[4], (H * C, D), dtype=jnp.float32) * scale
        q_norm_w = jnp.ones((C,), dtype=jnp.float32)
        k_norm_w = jnp.ones((C,), dtype=jnp.float32)
        return {'h': h, 'rope_cos': rope_cos, 'rope_sin': rope_sin, 'W_q': W_q, 'W_k': W_k, 'W_v': W_v, 'W_o': W_o, 'q_norm_w': q_norm_w, 'k_norm_w': k_norm_w}
    _L0_attn_all = _L0_attn_setup()
    _L0_attn_in = {k: v for k, v in _L0_attn_all.items() if k in ('rope_cos', 'rope_sin', 'W_q', 'W_k', 'W_v', 'W_o', 'q_norm_w', 'k_norm_w')}
    del _L0_attn_all

    def _L0_ffn_setup():
        import jax, jax.numpy as jnp
        import numpy as np
        NUM_EXPERTS = 32
        GROUP_SIZE = 4
        NUM_GROUPS = NUM_EXPERTS // GROUP_SIZE
        C_CAP = 1.0
        key = jax.random.key(seed)
        ks = jax.random.split(key, 5)
        B, S, H = (16, 512, 128)
        D_FF = int(H * 4 * (2.0 / 3.0))
        x = jax.random.normal(ks[0], (B, S, H), dtype=jnp.float32)
        W_router = jax.random.normal(ks[1], (H, NUM_EXPERTS), dtype=jnp.float32) * (1.0 / np.sqrt(H))
        b_router = jnp.zeros((NUM_EXPERTS,), dtype=jnp.float32)
        W_up = jax.random.normal(ks[2], (NUM_GROUPS, H, D_FF), dtype=jnp.float32) * (1.0 / np.sqrt(H))
        b_up = jnp.zeros((NUM_GROUPS, D_FF), dtype=jnp.float32)
        W_down = jax.random.normal(ks[3], (NUM_EXPERTS, D_FF, H), dtype=jnp.float32) * (1.0 / np.sqrt(D_FF))
        b_down = jnp.zeros((NUM_EXPERTS, H), dtype=jnp.float32)
        return {'x': x, 'W_router': W_router, 'b_router': b_router, 'W_up': W_up, 'b_up': b_up, 'W_down': W_down, 'b_down': b_down}
    _L0_ffn_all = _L0_ffn_setup()
    _L0_ffn_in = {k: v for k, v in _L0_ffn_all.items() if k in ('W_router', 'b_router', 'W_up', 'b_up', 'W_down', 'b_down')}
    del _L0_ffn_all

    def _L1_attn_setup():
        import jax, jax.numpy as jnp
        import numpy as np
        B, L, D = (4, 512, 128)
        CHUNK = 64
        EPS = 1e-05

        def _gated_delta_scan(k, v, q, lam, beta):
            b, l, d = k.shape
            nc = l // CHUNK

            def to_scan(t):
                return t.transpose(1, 0, 2).reshape(nc, CHUNK, b, d)
            ks, vs, qs = (to_scan(k), to_scan(v), to_scan(q))

            def step(S, inp):
                k_t, v_t, q_t = inp
                S = lam * S
                v_err = beta * (v_t - jnp.einsum('bk,bkv->bv', k_t, S))
                S = S + k_t[:, :, None] * v_err[:, None, :]
                o_t = jnp.einsum('bk,bkv->bv', q_t, S)
                return (S, o_t)

            def chunk_body(S, ch):
                return jax.lax.scan(step, S, ch)
            S0 = jnp.zeros((b, d, d), k.dtype)
            _, o = jax.lax.scan(chunk_body, S0, (ks, vs, qs))
            return o.reshape(l, b, d).transpose(1, 0, 2)
        key = jax.random.key(seed)
        kx, kw = jax.random.split(key)
        x = jax.random.normal(kx, (B, L, D), dtype=jnp.float32)
        W = jax.random.normal(kw, (D, D), dtype=jnp.float32) / np.float32(np.sqrt(D))
        return {'x': x, 'W': W, 'eta': jnp.asarray(0.01, jnp.float32), 'lam_logit': jnp.asarray(np.log(0.99 / 0.01), jnp.float32), 'ln_gamma': jnp.ones((D,), jnp.float32), 'ln_beta': jnp.zeros((D,), jnp.float32)}
    _L1_attn_all = _L1_attn_setup()
    _L1_attn_in = {k: v for k, v in _L1_attn_all.items() if k in ('W', 'eta', 'lam_logit', 'ln_gamma', 'ln_beta')}
    del _L1_attn_all

    def _L1_ffn_setup():
        import jax, jax.numpy as jnp
        import numpy as np
        DIM = 128
        INTER = 64
        SHARED_INTER = 256
        N_EXPERTS = 64
        TOP_K = 6
        key = jax.random.key(seed)
        ks = jax.random.split(key, 8)
        s = 0.05
        return {'x': jax.random.normal(ks[0], (2, 128, DIM), jnp.float32), 'w_gate': jax.random.normal(ks[1], (N_EXPERTS, DIM), jnp.float32) * s, 'w1': jax.random.normal(ks[2], (N_EXPERTS, INTER, DIM), jnp.float32) * s, 'w2': jax.random.normal(ks[3], (N_EXPERTS, INTER, DIM), jnp.float32) * s, 'w3': jax.random.normal(ks[4], (N_EXPERTS, INTER, DIM), jnp.float32) * s, 'w_sg': jax.random.normal(ks[5], (SHARED_INTER, DIM), jnp.float32) * s, 'w_su': jax.random.normal(ks[6], (SHARED_INTER, DIM), jnp.float32) * s, 'w_sd': jax.random.normal(ks[7], (DIM, SHARED_INTER), jnp.float32) * s}
    _L1_ffn_all = _L1_ffn_setup()
    _L1_ffn_in = {k: v for k, v in _L1_ffn_all.items() if k in ('w_gate', 'w1', 'w2', 'w3', 'w_sg', 'w_su', 'w_sd')}
    del _L1_ffn_all
    return {'x': x, 'L0_tok_q_w': _L0_tok_in['q_w'], 'L0_tok_q_b': _L0_tok_in['q_b'], 'L0_tok_k_w': _L0_tok_in['k_w'], 'L0_tok_k_b': _L0_tok_in['k_b'], 'L0_tok_v_w': _L0_tok_in['v_w'], 'L0_tok_v_b': _L0_tok_in['v_b'], 'L0_tok_o_w': _L0_tok_in['o_w'], 'L0_tok_o_b': _L0_tok_in['o_b'], 'L0_tok_ln1_g': _L0_tok_in['ln1_g'], 'L0_tok_ln1_b': _L0_tok_in['ln1_b'], 'L0_tok_f1_w': _L0_tok_in['f1_w'], 'L0_tok_f1_b': _L0_tok_in['f1_b'], 'L0_tok_f2_w': _L0_tok_in['f2_w'], 'L0_tok_f2_b': _L0_tok_in['f2_b'], 'L0_tok_ln2_g': _L0_tok_in['ln2_g'], 'L0_tok_ln2_b': _L0_tok_in['ln2_b'], 'L0_tok_conv_w': _L0_tok_in['conv_w'], 'L0_tok_conv_b': _L0_tok_in['conv_b'], 'L0_attn_rope_cos': _L0_attn_in['rope_cos'], 'L0_attn_rope_sin': _L0_attn_in['rope_sin'], 'L0_attn_W_q': _L0_attn_in['W_q'], 'L0_attn_W_k': _L0_attn_in['W_k'], 'L0_attn_W_v': _L0_attn_in['W_v'], 'L0_attn_W_o': _L0_attn_in['W_o'], 'L0_attn_q_norm_w': _L0_attn_in['q_norm_w'], 'L0_attn_k_norm_w': _L0_attn_in['k_norm_w'], 'L0_ffn_W_router': _L0_ffn_in['W_router'], 'L0_ffn_b_router': _L0_ffn_in['b_router'], 'L0_ffn_W_up': _L0_ffn_in['W_up'], 'L0_ffn_b_up': _L0_ffn_in['b_up'], 'L0_ffn_W_down': _L0_ffn_in['W_down'], 'L0_ffn_b_down': _L0_ffn_in['b_down'], 'L1_attn_W': _L1_attn_in['W'], 'L1_attn_eta': _L1_attn_in['eta'], 'L1_attn_lam_logit': _L1_attn_in['lam_logit'], 'L1_attn_ln_gamma': _L1_attn_in['ln_gamma'], 'L1_attn_ln_beta': _L1_attn_in['ln_beta'], 'L1_ffn_w_gate': _L1_ffn_in['w_gate'], 'L1_ffn_w1': _L1_ffn_in['w1'], 'L1_ffn_w2': _L1_ffn_in['w2'], 'L1_ffn_w3': _L1_ffn_in['w3'], 'L1_ffn_w_sg': _L1_ffn_in['w_sg'], 'L1_ffn_w_su': _L1_ffn_in['w_su'], 'L1_ffn_w_sd': _L1_ffn_in['w_sd']}

def reference(x, L0_tok_q_w, L0_tok_q_b, L0_tok_k_w, L0_tok_k_b, L0_tok_v_w, L0_tok_v_b, L0_tok_o_w, L0_tok_o_b, L0_tok_ln1_g, L0_tok_ln1_b, L0_tok_f1_w, L0_tok_f1_b, L0_tok_f2_w, L0_tok_f2_b, L0_tok_ln2_g, L0_tok_ln2_b, L0_tok_conv_w, L0_tok_conv_b, L0_attn_rope_cos, L0_attn_rope_sin, L0_attn_W_q, L0_attn_W_k, L0_attn_W_v, L0_attn_W_o, L0_attn_q_norm_w, L0_attn_k_norm_w, L0_ffn_W_router, L0_ffn_b_router, L0_ffn_W_up, L0_ffn_b_up, L0_ffn_W_down, L0_ffn_b_down, L1_attn_W, L1_attn_eta, L1_attn_lam_logit, L1_attn_ln_gamma, L1_attn_ln_beta, L1_ffn_w_gate, L1_ffn_w1, L1_ffn_w2, L1_ffn_w3, L1_ffn_w_sg, L1_ffn_w_su, L1_ffn_w_sd):
    import jax
    import jax.numpy as jnp

    def _L0_tok_ref(x, q_w, q_b, k_w, k_b, v_w, v_b, o_w, o_b, ln1_g, ln1_b, f1_w, f1_b, f2_w, f2_b, ln2_g, ln2_b, conv_w, conv_b):
        import jax, jax.numpy as jnp
        import numpy as np
        H = 8
        TOP_FRAC = 0.2
        EPS = 1e-05

        def _layernorm(x, g, b):
            mu = jnp.mean(x, axis=-1, keepdims=True)
            var = jnp.mean((x - mu) ** 2, axis=-1, keepdims=True)
            return (x - mu) * jax.lax.rsqrt(var + EPS) * g + b
        B, L, D = x.shape
        hd = D // H
        scale = hd ** (-0.5)
        k_top = max(1, int(L * TOP_FRAC))

        def split_heads(t):
            return t.reshape(B, L, H, hd).transpose(0, 2, 1, 3)
        q = split_heads(x @ q_w + q_b)
        k = split_heads(x @ k_w + k_b)
        v = split_heads(x @ v_w + v_b)
        q_norm = jnp.sum(q * q, axis=-1)
        _, top_idx = jax.lax.top_k(q_norm, k_top)
        bi = jnp.arange(B)[:, None, None]
        hi = jnp.arange(H)[None, :, None]
        mask = jnp.zeros((B, H, L), bool).at[bi, hi, top_idx].set(True)
        q = q * mask[..., None]
        scores = jnp.einsum('bhld,bhmd->bhlm', q, k) * scale
        probs = jax.nn.softmax(scores, axis=-1)
        attn = jnp.einsum('bhlm,bhmd->bhld', probs, v)
        attn = attn.transpose(0, 2, 1, 3).reshape(B, L, D)
        attn_out = attn @ o_w + o_b
        h1 = _layernorm(x + attn_out, ln1_g, ln1_b)
        ff = jax.nn.relu(h1 @ f1_w + f1_b) @ f2_w + f2_b
        h2 = _layernorm(h1 + ff, ln2_g, ln2_b)
        fused = h2 + attn_out
        y = fused.transpose(0, 2, 1)
        y = jax.lax.conv_general_dilated(y, conv_w, window_strides=(1,), padding=[(1, 1)], dimension_numbers=('NCH', 'OIH', 'NCH')) + conv_b[None, :, None]
        y = jax.nn.relu(y)
        y = y.reshape(B, D, L // 2, 2).max(axis=-1)
        return y.transpose(0, 2, 1)

    def _L0_attn_ref(h, rope_cos, rope_sin, W_q, W_k, W_v, W_o, q_norm_w, k_norm_w):
        import jax, jax.numpy as jnp
        import numpy as np
        B, T, D, H, C, WIN = (2, 512, 128, 8, 64, 128)
        EPS = 1e-06

        def _rms_norm(x, w):
            norm = jax.lax.rsqrt(jnp.mean(x * x, axis=-1, keepdims=True) + EPS)
            return x * norm * w

        def _apply_rope(x, cos_p, sin_p):
            half = x.shape[-1] // 2
            x1, x2 = (x[..., :half], x[..., half:])
            rotated = jnp.concatenate([-x2, x1], axis=-1)
            return x * cos_p + rotated * sin_p
        Bx, Tx, _ = h.shape
        q = (h @ W_q).reshape(Bx, Tx, H, C)
        k = (h @ W_k).reshape(Bx, Tx, H, C)
        v = (h @ W_v).reshape(Bx, Tx, H, C)
        q = _rms_norm(q, q_norm_w)
        k = _rms_norm(k, k_norm_w)
        positions = jnp.arange(Tx)
        cos_p = rope_cos[positions]
        sin_p = rope_sin[positions]
        q = _apply_rope(q.transpose(0, 2, 1, 3), cos_p, sin_p).transpose(0, 2, 1, 3)
        k = _apply_rope(k.transpose(0, 2, 1, 3), cos_p, sin_p).transpose(0, 2, 1, 3)
        i = positions[:, None]
        j = positions[None, :]
        sw_mask = (j <= i) & (j > i - WIN)
        logits = jnp.einsum('bthc,bshc->bhts', q, k) / np.sqrt(C).astype(np.float32)
        logits = jnp.where(sw_mask[None, None], logits, jnp.float32(-jnp.inf))
        attn = jax.nn.softmax(logits, axis=-1)
        out = jnp.einsum('bhts,bshc->bthc', attn, v).reshape(Bx, Tx, H * C)
        return out @ W_o

    def _L0_ffn_ref(x, W_router, b_router, W_up, b_up, W_down, b_down):
        import jax, jax.numpy as jnp
        import numpy as np
        NUM_EXPERTS = 32
        GROUP_SIZE = 4
        NUM_GROUPS = NUM_EXPERTS // GROUP_SIZE
        C_CAP = 1.0
        B, S, H = x.shape
        bs = B * S
        E = NUM_EXPERTS
        k = min(int(bs * C_CAP) // E, bs)
        xf = x.reshape(bs, H)
        h = xf @ W_router + b_router
        Sm = jax.nn.softmax(h, axis=-1)
        G_ek, idx_ek = jax.lax.top_k(Sm.T, k)
        tokens = xf[idx_ek]
        D_FF = W_up.shape[-1]
        tok_g = tokens.reshape(NUM_GROUPS, GROUP_SIZE, k, H)
        up = jnp.einsum('gjkh,ghf->gjkf', tok_g, W_up) + b_up[:, None, None, :]
        act = jax.nn.silu(up).reshape(E, k, D_FF)
        Eout = jnp.einsum('ekf,efh->ekh', act, W_down) + b_down[:, None, :]
        weighted = G_ek[..., None] * Eout
        y = jnp.zeros((bs, H), dtype=x.dtype).at[idx_ek.reshape(-1)].add(weighted.reshape(-1, H))
        return y.reshape(B, S, H)

    def _L1_attn_ref(x, W, eta, lam_logit, ln_gamma, ln_beta):
        import jax, jax.numpy as jnp
        import numpy as np
        B, L, D = (4, 512, 128)
        CHUNK = 64
        EPS = 1e-05

        def _gated_delta_scan(k, v, q, lam, beta):
            b, l, d = k.shape
            nc = l // CHUNK

            def to_scan(t):
                return t.transpose(1, 0, 2).reshape(nc, CHUNK, b, d)
            ks, vs, qs = (to_scan(k), to_scan(v), to_scan(q))

            def step(S, inp):
                k_t, v_t, q_t = inp
                S = lam * S
                v_err = beta * (v_t - jnp.einsum('bk,bkv->bv', k_t, S))
                S = S + k_t[:, :, None] * v_err[:, None, :]
                o_t = jnp.einsum('bk,bkv->bv', q_t, S)
                return (S, o_t)

            def chunk_body(S, ch):
                return jax.lax.scan(step, S, ch)
            S0 = jnp.zeros((b, d, d), k.dtype)
            _, o = jax.lax.scan(chunk_body, S0, (ks, vs, qs))
            return o.reshape(l, b, d).transpose(1, 0, 2)
        lam = jax.nn.sigmoid(lam_logit)
        x_act = jnp.tanh(x)
        static_out = jnp.einsum('bld,ed->ble', x_act, W)
        o_dyn = _gated_delta_scan(x_act, static_out, x_act, lam, eta)
        y = static_out + o_dyn
        mu = jnp.mean(y, axis=-1, keepdims=True)
        var = jnp.var(y, axis=-1, keepdims=True)
        return (y - mu) * jax.lax.rsqrt(var + EPS) * ln_gamma + ln_beta

    def _L1_ffn_ref(x, w_gate, w1, w2, w3, w_sg, w_su, w_sd):
        import jax, jax.numpy as jnp
        import numpy as np
        DIM = 128
        INTER = 64
        SHARED_INTER = 256
        N_EXPERTS = 64
        TOP_K = 6
        orig_shape = x.shape
        xf = x.reshape(-1, x.shape[-1])
        T = xf.shape[0]
        scores = xf @ w_gate.T
        top_vals, top_idx = jax.lax.top_k(scores, TOP_K)
        expert_weights = jax.nn.softmax(top_vals, axis=-1)
        comb = jnp.zeros(scores.shape, xf.dtype).at[jnp.arange(T)[:, None], top_idx].set(expert_weights)
        x1 = jax.nn.silu(jnp.einsum('td,eid->tei', xf, w1))
        x3 = jnp.einsum('td,eid->tei', xf, w3)
        y = jnp.einsum('tei,eid->ted', x1 * x3, w2)
        routed = jnp.einsum('ted,te->td', y, comb)
        shared = jax.nn.silu(xf @ w_sg.T) * (xf @ w_su.T) @ w_sd.T
        return (routed + shared).reshape(orig_shape)
    h = _L0_tok_ref(x, L0_tok_q_w, L0_tok_q_b, L0_tok_k_w, L0_tok_k_b, L0_tok_v_w, L0_tok_v_b, L0_tok_o_w, L0_tok_o_b, L0_tok_ln1_g, L0_tok_ln1_b, L0_tok_f1_w, L0_tok_f1_b, L0_tok_f2_w, L0_tok_f2_b, L0_tok_ln2_g, L0_tok_ln2_b, L0_tok_conv_w, L0_tok_conv_b)
    h = h + _L0_attn_ref(_layernorm(h, axis=-1), L0_attn_rope_cos, L0_attn_rope_sin, L0_attn_W_q, L0_attn_W_k, L0_attn_W_v, L0_attn_W_o, L0_attn_q_norm_w, L0_attn_k_norm_w)
    h = h + _L0_ffn_ref(_layernorm(h, axis=-1), L0_ffn_W_router, L0_ffn_b_router, L0_ffn_W_up, L0_ffn_b_up, L0_ffn_W_down, L0_ffn_b_down)
    h = h + _L1_attn_ref(_layernorm(h, axis=-1), L1_attn_W, L1_attn_eta, L1_attn_lam_logit, L1_attn_ln_gamma, L1_attn_ln_beta)
    h = h + _L1_ffn_ref(_layernorm(h, axis=-1), L1_ffn_w_gate, L1_ffn_w1, L1_ffn_w2, L1_ffn_w3, L1_ffn_w_sg, L1_ffn_w_su, L1_ffn_w_sd)
    return h

_drawn_inputs = setup_inputs


def setup_inputs(seed=0):
    import zlib

    import numpy as np

    out = dict(_drawn_inputs(seed))
    spreads = {'L0_tok_q_b': (0.0, 0.8),
     'L0_tok_k_b': (0.0, 0.8),
     'L0_tok_v_b': (0.0, 0.1),
     'L0_tok_o_b': (0.0, 0.1),
     'L0_tok_ln1_g': (1.0, 0.2),
     'L0_tok_ln1_b': (0.0, 0.1),
     'L0_tok_f1_b': (0.0, 0.1),
     'L0_tok_f2_b': (0.0, 0.1),
     'L0_tok_ln2_g': (1.0, 0.2),
     'L0_tok_ln2_b': (0.0, 0.1),
     'L0_tok_conv_b': (0.0, 0.1),
     'L0_attn_q_norm_w': (1.0, 0.2),
     'L0_attn_k_norm_w': (1.0, 0.2),
     'L0_ffn_b_router': (0.0, 0.1),
     'L0_ffn_b_up': (0.0, 0.1),
     'L0_ffn_b_down': (0.0, 0.1),
     'L1_attn_ln_gamma': (1.0, 0.2),
     'L1_attn_ln_beta': (0.0, 0.1)}
    factors = {'L0_tok_q_w': 8.0, 'L0_tok_k_w': 8.0}
    for name, (base, spread) in spreads.items():
        noise = np.random.default_rng([zlib.crc32(name.encode()), seed]).standard_normal(out[name].shape)
        drawn = base * np.exp(spread * noise) if base else spread * noise
        out[name] = jnp.asarray(drawn.astype(out[name].dtype))
    for name, factor in factors.items():
        out[name] = (out[name] * factor).astype(out[name].dtype)
    return out
```

```python
from contextlib import ExitStack

import concourse.bass as bass
from concourse import mybir

ALU = mybir.AluOpType
ACT = mybir.ActivationFunctionType
F32 = mybir.dt.float32
BF16 = mybir.dt.bfloat16
F16 = mybir.dt.float16
I32 = mybir.dt.int32
U32 = mybir.dt.uint32
AX = mybir.AxisListType

P = 128
B, L, D = 32, 512, 128
LT = L // P
H0, HD0 = 8, 16
TOP = int(L * 0.2)
LN_EPS = 1e-5
START = 1
PAIRS = B // 2


def stand_alone(eng, seen):
    eng.sem_inc(seen, 1)


def start_counts(nc, sems):
    with nc.Block() as block:
        @block.sync
        def _(sp):
            for s in sems:
                sp.sem_inc(s, START)
    nc.all_engine_barrier()


def make_identity(nc, pool, ident, zeroed, ready):
    nc.gpsimd.memset(ident[:, :], 0.0).then_inc(zeroed, 1)
    pool.wait_ge(zeroed, 1)
    nc.gpsimd.affine_select(out=ident[:, :], in_=ident[:, :], compare_op=ALU.not_equal, fill=1.0, base=0,
                            pattern=[[-1, P]], channel_multiplier=1).then_inc(ready, 1)


def select_queries(nc, dram, keep):
    GROUPS = 2
    GB = B // GROUPS
    ROUNDS = -(-TOP // 8)
    sems = []
    with ExitStack() as ctx:
        def sb(name, shape, dt=F32):
            return ctx.enter_context(nc.sbuf_tensor(name, shape, dt))

        def two(name, shape, dt=F32):
            return [sb(f"{name}{u}", shape, dt) for u in range(2)]

        def ps(name, shape):
            return ctx.enter_context(nc.psum_tensor(name, shape, F32))

        def sem(name):
            sems.append(nc.alloc_semaphore("q_" + name))
            return sems[-1]

        def sem2(name):
            return [sem(f"{name}{u}") for u in range(2)]

        xT = two("q1_xT", [P, L])
        q_sb = two("q1_q", [P, LT, D])
        sq = two("q1_sq", [P, LT, H0, HD0])
        wq = sb("q1_wq", [P, D])
        qb = sb("q1_qb", [P, D])
        norms = sb("q1_norms", [P, LT, B, H0])
        rows = two("q1_rows", [P, L])
        best = two("q1_best", [P, 8])
        found = two("q1_found", [P, ROUNDS * 8], U32)
        found_f = two("q1_found_f", [P, ROUNDS * 8])
        base = sb("q1_base", [P, B, H0], I32)
        base_f = sb("q1_base_f", [P, B * H0])
        psT = [ps(f"q1_psT{u}", [P, L]) for u in range(2)]
        psQ = [ps(f"q1_psQ{u}", [P, LT, D]) for u in range(2)]
        psR = [ps(f"q1_psR{u}", [P, L]) for u in range(2)]

        weights = sem("weights")
        xT_loaded = sem2("xT_loaded")
        q_done = sem2("q_done")
        q_ready = sem2("q_ready")
        q_squared = sem2("q_squared")
        q_stored = sem2("q_stored")
        norms_ready = sem2("norms_ready")
        rows_turned = sem("rows_turned")
        rows_ready = sem("rows_ready")
        best_ready = sem2("best_ready")
        found_ready = sem2("found_ready")
        row_marked = sem2("row_marked")
        found_cast = sem("found_cast")
        found_turned = sem("found_turned")
        top_ready = sem("top_ready")
        spare_ready = sem("spare_ready")
        base_ready = sem("base_ready")
        base_cast = sem("base_cast")

        q_d = dram["q_rows"].rearrange("(b t p h) c -> b p t (h c)", b=B, t=LT, h=H0)

        start_counts(nc, [*q_ready, *norms_ready, *q_stored, *q_squared])

        with nc.Block() as block:
            @block.sync
            def _(sp):
                sp.dma_start(wq[:, :], dram["q_w"]).then_inc(weights, 16)
                sp.dma_start(qb[:, :], dram["q_b"].partition_broadcast(P)).then_inc(weights, 16)
                for u in range(2):
                    sp.dma_start(xT[u][:, :], dram["xT"][u]).then_inc(xT_loaded[u], 16)
                with sp.Fori(0, PAIRS - 1) as p:
                    for u in range(2):
                        sp.wait_ge(q_done[u], p + 1)
                        sp.dma_start(xT[u][:, :], dram["xT"][2 * p + 2 + u]).then_inc(xT_loaded[u], 16)
                        sp.wait_ge(q_ready[u], START + p + 1)
                        sp.dma_start(q_d[2 * p + u], q_sb[u][:, :, :]).then_inc(q_stored[u], 16)
                for u in range(2):
                    sp.wait_ge(q_ready[u], START + PAIRS)
                    sp.dma_start(q_d[2 * (PAIRS - 1) + u], q_sb[u][:, :, :]).then_inc(q_stored[u], 16)
                for u in range(2):
                    sp.wait_ge(q_stored[u], START + 16 * PAIRS)

            @block.gpsimd
            def _(pool):
                nc.gpsimd.memset(keep.top_row[0:TOP, B * H0:], 0).then_inc(spare_ready, 1)
                nc.gpsimd.iota(base[:, :, :], pattern=[[L * H0, B], [1, H0]], base=0,
                               channel_multiplier=0).then_inc(base_ready, 1)

            @block.tensor
            def _(pe):
                pe.wait_ge(weights, 32)
                with pe.Fori(0, PAIRS) as p:
                    for u in range(2):
                        pe.wait_ge(xT_loaded[u], 16 * p + 16)
                        pe.wait_ge(q_ready[u], START + p)
                        for t in range(LT):
                            ins = nc.tensor.matmul(psQ[u][:, t, :], xT[u][:, t * P:(t + 1) * P], wq[:, :],
                                                   start=True, stop=True)
                        ins.then_inc(q_done[u], 1)
                for u in range(2):
                    pe.wait_ge(norms_ready[u], START + PAIRS)
                for g in range(GROUPS):
                    for t in range(LT):
                        ins = nc.tensor.transpose(psR[g][:, t * P:(t + 1) * P],
                                                  norms[:, t, g * GB:(g + 1) * GB, :].rearrange("p b h -> p (b h)"),
                                                  keep.ident[:, :])
                    ins.then_inc(rows_turned, 1)
                for g in range(GROUPS):
                    pe.wait_ge(found_cast, g + 1)
                    nc.tensor.transpose(psT[g][0:TOP, 0:P], found_f[g][:, 0:TOP],
                                        keep.ident[:, :]).then_inc(found_turned, 1)

            @block.scalar
            def _(act):
                with act.Fori(0, PAIRS) as p:
                    for u in range(2):
                        act.wait_ge(q_ready[u], START + p + 1)
                        act.wait_ge(norms_ready[u], START + p)
                        nc.scalar.activation(sq[u][:, :, :, :].rearrange("p t h c -> p (t h c)"),
                                             q_sb[u][:, :, :].rearrange("p t d -> p (t d)"),
                                             ACT.Square).then_inc(q_squared[u], 1)

            @block.vector
            def _(dve):
                dve.wait_ge(weights, 32)
                with dve.Fori(0, PAIRS) as p:
                    for u in range(2):
                        dve.wait_ge(q_done[u], p + 1)
                        dve.wait_ge(q_stored[u], START + 16 * p)
                        dve.wait_ge(q_squared[u], START + p)
                        nc.vector.tensor_tensor(q_sb[u][:, :, :], psQ[u][:, :, :],
                                                qb[:, :].unsqueeze(1).broadcast_to([P, LT, D]),
                                                ALU.add).then_inc(q_ready[u], 1)
                    for u in range(2):
                        dve.wait_ge(q_squared[u], START + p + 1)
                        nc.vector.tensor_reduce(norms[:, :, 2 * p + u, :], sq[u][:, :, :, :], AX.X,
                                                ALU.add).then_inc(norms_ready[u], 1)
                for g in range(GROUPS):
                    dve.wait_ge(rows_turned, g + 1)
                    nc.vector.tensor_copy(rows[g][:, :], psR[g][:, :]).then_inc(rows_ready, 1)
                for r in range(ROUNDS):
                    for g in range(GROUPS):
                        if r == 0:
                            dve.wait_ge(rows_ready, g + 1)
                        else:
                            dve.wait_ge(row_marked[g], r)
                        nc.vector.max(best[g][:, :], rows[g][:, :]).then_inc(best_ready[g], 1)
                    for g in range(GROUPS):
                        dve.wait_ge(best_ready[g], r + 1)
                        nc.vector.max_index(found[g][:, 8 * r:8 * r + 8], best[g][:, :],
                                            rows[g][:, :]).then_inc(found_ready[g], 1)
                    for g in range(GROUPS):
                        dve.wait_ge(found_ready[g], r + 1)
                        nc.vector.match_replace(rows[g][:, :], best[g][:, :], rows[g][:, :],
                                                -1.0).then_inc(row_marked[g], 1)
                for g in range(GROUPS):
                    dve.wait_ge(found_ready[g], ROUNDS)
                    nc.vector.tensor_copy(found_f[g][:, :], found[g][:, :]).then_inc(found_cast, 1)
                dve.wait_ge(base_ready, 1)
                nc.vector.tensor_copy(base_f[:, :], base[:, :, :].rearrange("p b h -> p (b h)"))\
                    .then_inc(base_cast, 1)
                dve.wait_ge(base_cast, 1)
                for g in range(GROUPS):
                    dve.wait_ge(found_turned, g + 1)
                    cols = slice(g * P, (g + 1) * P)
                    nc.vector.tensor_copy(keep.top_f32[0:TOP, cols], psT[g][0:TOP, 0:P]).then_inc(top_ready, 1)
                    dve.wait_ge(top_ready, 2 * g + 1)
                    nc.vector.scalar_tensor_tensor(out=keep.top_row[0:TOP, cols], in0=keep.top_f32[0:TOP, cols],
                                                   scalar=float(H0), in1=base_f[0:TOP, cols], op0=ALU.mult,
                                                   op1=ALU.add).then_inc(top_ready, 1)
        nc.clear_and_free_semaphores(sems)
        nc.all_engine_barrier()


LP = L // 2
PT = LP // P
FF = 512
FC = FF // P


def token_layer(nc, dram, keep):
    sems = []
    with ExitStack() as ctx:
        def sb(name, shape, dt=F32):
            return ctx.enter_context(nc.sbuf_tensor("t_" + name, shape, dt))

        def two(name, shape, dt=F32):
            return [sb(f"{name}{u}", shape, dt) for u in range(2)]

        def sem(name):
            sems.append(nc.alloc_semaphore("t_" + name))
            return sems[-1]

        def sem2(name):
            return [sem(f"{name}{u}") for u in range(2)]

        w_small = {n: sb(n, [P, D]) for n in ("k_w", "v_w", "o_w")}
        rows = {n: sb(n, [P, D]) for n in ("v_b", "o_b", "ln1_g", "ln1_b", "ln2_g", "ln2_b", "f2_b")}
        cols = {n: sb(n, [P, 1]) for n in ("k_b", "conv_b")}
        f1_w = sb("f1_w", [P, FF])
        f1_b = sb("f1_b", [P, FC])
        f2_w = sb("f2_w", [P, FC, D])
        conv_w = sb("conv_w", [P, 3, D])
        out_shift = sb("out_shift", [P, D])
        head_mask = sb("head_mask", [P, H0])
        mean_w = sb("mean_w", [P, P])
        half_neg = sb("half_neg", [P, LT])
        eps = sb("eps", [P, LT])
        iota_i = sb("iota_i", [P, L], I32)
        iota_h = sb("iota_h", [P, L], F16)

        x_sb = two("x", [P, LT, D])
        x_shift = two("x_shift", [P, LT, D])
        xT = two("xT", [P, L])
        kT = two("kT", [P, L])
        v1 = two("v1", [P, LT, H0, HD0 + 1])
        top_col = two("top_col", [P, H0], I32)
        q_top = two("q_top", [P, D])
        q_diag = two("q_diag", [P, H0, TOP])
        v_mean = two("v_mean", [P, D])
        low = two("low", [P, H0])
        probs = two("probs", [P, 2, L])
        probsT = two("probsT", [P, 2, LT, TOP])
        place = two("place", [P, H0, L], BF16)
        o_scale = two("o_scale", [P, H0])
        o_top = two("o_top", [P, H0, HD0])
        o_rest = two("o_rest", [P, H0, HD0])
        o_part = two("o_part", [P, 3, D], BF16)
        attn = two("attn", [P, LT, D])
        attnT = two("attnT", [P, L])
        ao_shift = two("ao_shift", [P, LT, D])
        z = two("z", [P, LT, D])
        stats = two("stats", [P, LT, 6])
        mean_var = two("mean_var", [P, LT, 2])
        rstd = two("rstd", [P, LT])
        h1 = two("h1", [P, LT, D])
        h1T = two("h1T", [P, L])
        ff = two("ff", [P, FC, L])
        fusedT = two("fusedT", [P, L + 2])
        pooled = two("pooled", [P, LP])
        yT = two("yT", [P, LP])

        bank = [[ctx.enter_context(nc.psum_tensor(f"t_bank{u}{k}", [P, 512], F32)) for k in range(4)]
                for u in range(2)]

        def tiles(ap, n=LT):
            return ap.rearrange("p (t d) -> p t d", t=n)

        def per_tile(row, n=LT):
            return row[:, :].unsqueeze(1).broadcast_to([P, n, D])

        weights = sem("weights")
        const = sem("const")
        dve_seen = sem("dve_seen")
        pool_seen = sem("pool_seen")
        shift_ready = sem("shift_ready")
        iota_ready = sem("iota_ready")
        x_loaded, xT_loaded, x_shifted = map(sem2, ("x_loaded", "xT_loaded", "x_shifted"))
        kT_done, kT_ready, v_done, v_ready = map(sem2, ("kT_done", "kT_ready", "v_done", "v_ready"))
        col_ready, q_gathered, qT_done, q_diag_ready = map(
            sem2, ("col_ready", "q_gathered", "qT_done", "q_diag_ready"))
        mean_done, mean_ready, place_ready = map(sem2, ("mean_done", "mean_ready", "place_ready"))
        scores_done, low_ready, probs_ready = map(sem2, ("scores_done", "low_ready", "probs_ready"))
        probs_turned, probsT_ready, o_done = map(sem2, ("probs_turned", "probsT_ready", "o_done"))
        o_rest_ready = sem2("o_rest_ready")
        o_step, o_placed, attn_ready, attn_turned, attnT_ready = map(
            sem2, ("o_step", "o_placed", "attn_ready", "attn_turned", "attnT_ready"))
        ao_done, ao_ready, z_ready = map(sem2, ("ao_done", "ao_ready", "z_ready"))
        ln_stats, ln_var, ln_eps, ln_root, ln_norm, ln_gain = map(
            sem2, ("ln_stats", "ln_var", "ln_eps", "ln_root", "ln_norm", "ln_gain"))
        h1_ready, h1_turned, h1T_ready, h1_shifted = map(sem2, ("h1_ready", "h1_turned", "h1T_ready", "h1_shifted"))
        ff_done, ff_act, ff_dve, y_done, z2_ready = map(sem2, ("ff_done", "ff_act", "ff_dve", "y_done", "z2_ready"))
        fused_ready, fused_turned, fusedT_ready = map(sem2, ("fused_ready", "fused_turned", "fusedT_ready"))
        conv_done, pooled_ready, yT_ready, y_turned, h_ready = map(
            sem2, ("conv_done", "pooled_ready", "yT_ready", "y_turned", "h_ready"))

        x_d = dram["x"].rearrange("b (t p) d -> b p t d", p=P)
        top_f32 = keep.top_f32[:, :].rearrange("p (b h) -> p b h", h=H0)
        top_row = keep.top_row[:, :].rearrange("p (b h) -> p b h", h=H0)

        loads = [(w_small[n][:, :], dram[n]) for n in w_small]
        loads += [(rows[n][:, :], dram[n].partition_broadcast(P)) for n in rows]
        loads += [(cols[n][:, :], dram[n].unsqueeze(1)) for n in cols]
        loads += [(f1_w[:, :], dram["f1_w"]),
                  (f1_b[:, :], dram["f1_b"]),
                  (f2_w[:, :, :], dram["f2_w"].rearrange("(c p) d -> p c d", p=P)),
                  (conv_w[:, :, :], dram["conv_w"])]
        ALL_WEIGHTS = 16 * len(loads)
        CONSTS = 10

        start_counts(nc, [*z_ready, *h_ready, *probs_ready, *probsT_ready, *probs_turned, *o_done,
                          *fused_ready, *fused_turned])

        FF_BANK = (0, 2, 3, 1)
        TURN_H1, FF_LOW, FF_HIGH, FF_DOWN, ADD_H1, NORM2_STATS, NORM2 = 1, 2, 3, 4, 5, 6, 7

        def turns(eng, turn):
            turn((0, 0), None)
            turn((1, 0), (0, 0))
            with eng.Fori(0, PAIRS - 1) as p:
                turn((0, p + 1), (1, p))
                turn((1, p + 1), (0, p + 1))
            turn(None, (1, PAIRS - 1))

        with nc.Block() as block:
            @block.sync
            def _(sp):
                for dst, src in loads:
                    sp.dma_start(dst, src).then_inc(weights, 16)
                for u in range(2):
                    sp.dma_start(xT[u][:, :], dram["xT"][u]).then_inc(xT_loaded[u], 16)
                    sp.dma_start(x_sb[u][:, :, :], x_d[u]).then_inc(x_loaded[u], 16)
                with sp.Fori(0, PAIRS - 1) as p:
                    for u in range(2):
                        sp.wait_ge(v_done[u], p + 1)
                        sp.dma_start(xT[u][:, :], dram["xT"][2 * p + 2 + u]).then_inc(xT_loaded[u], 16)
                        sp.wait_ge(x_shifted[u], p + 1)
                        sp.dma_start(x_sb[u][:, :, :], x_d[2 * p + 2 + u]).then_inc(x_loaded[u], 16)

            @block.gpsimd
            def _(pool):
                nc.gpsimd.memset(mean_w[:, :], 1.0 / L).then_inc(const, 1)
                nc.gpsimd.memset(half_neg[:, :], -0.5).then_inc(const, 1)
                nc.gpsimd.memset(eps[:, :], LN_EPS).then_inc(const, 1)
                for u in range(2):
                    nc.gpsimd.memset(v1[u][:, :, :, HD0:HD0 + 1], 1.0).then_inc(const, 1)
                    nc.gpsimd.memset(fusedT[u][:, 0:L + 2:L + 1], 0.0).then_inc(const, 1)
                nc.gpsimd.iota(iota_i[:, :], pattern=[[1, L]], base=0, channel_multiplier=0)\
                    .then_inc(iota_ready, 1)
                nc.gpsimd.memset(head_mask[:, :], -(float(HD0) ** -0.5)).then_inc(const, 1)
                pool.wait_ge(const, 8)
                nc.gpsimd.affine_select(out=head_mask[:, :], in_=head_mask[:, :], compare_op=ALU.is_ge,
                                        fill=0.0, base=0, pattern=[[-HD0, H0]],
                                        channel_multiplier=1).then_inc(const, 1)
                pool.wait_ge(const, 9)
                nc.gpsimd.affine_select(out=head_mask[:, :], in_=head_mask[:, :], compare_op=ALU.is_ge,
                                        fill=0.0, base=HD0 - 1, pattern=[[HD0, H0]],
                                        channel_multiplier=-1).then_inc(const, 1)
                pool.wait_ge(weights, ALL_WEIGHTS)
                nc.gpsimd.tensor_tensor(out_shift[:, :], rows["o_b"][:, :], rows["ln2_b"][:, :],
                                        ALU.add).then_inc(shift_ready, 1)

                def gather(u):
                    for h in range(H0):
                        pool.indirect_dma_start(
                            out=q_top[u][0:TOP, h * HD0:(h + 1) * HD0], out_offset=None, in_=dram["q_rows"],
                            in_offset=bass.IndirectOffsetOnAxis(ap=top_col[u][0:TOP, h:h + 1], axis=0),
                        ).then_inc(q_gathered[u], 16)

                def inverse_root(u, n):
                    pool.wait_ge(ln_var[u], LT * (n + 1))
                    nc.gpsimd.tensor_tensor(rstd[u][:, :], mean_var[u][:, :, 1], eps[:, :],
                                            ALU.add).then_inc(ln_eps[u], 1)
                    pool.wait_ge(ln_eps[u], n + 1)
                    nc.gpsimd.tensor_tensor(rstd[u][:, :], rstd[u][:, :], half_neg[:, :],
                                            ALU.pow).then_inc(ln_root[u], 1)

                def shift_x(u, p):
                    pool.wait_ge(x_loaded[u], 16 * p + 16)
                    pool.wait_ge(z_ready[u], START + p)
                    nc.gpsimd.tensor_tensor(x_shift[u][:, :, :], x_sb[u][:, :, :], per_tile(rows["o_b"]),
                                            ALU.add).then_inc(x_shifted[u], 1)

                def gather_next(u, p):
                    pool.wait_ge(q_gathered[u], 16 * H0 * (p + 1))
                    nc.gpsimd.tensor_copy(top_col[u][0:TOP, :], top_row[0:TOP, 2 * p + 2 + u, :])\
                        .then_inc(col_ready[u], 1)
                    pool.wait_ge(qT_done[u], p + 1)
                    pool.wait_ge(col_ready[u], p + 2)
                    stand_alone(pool, pool_seen)
                    gather(u)

                def gain_shift_1(u, p):
                    pool.wait_ge(ln_norm[u], LT * (2 * p + 1))
                    nc.gpsimd.tensor_tensor(h1[u][:, :, :], h1[u][:, :, :], per_tile(rows["ln1_g"]),
                                            ALU.mult).then_inc(ln_gain[u], 1)
                    pool.wait_ge(ln_gain[u], 2 * p + 1)
                    nc.gpsimd.tensor_tensor(h1[u][:, :, :], h1[u][:, :, :], per_tile(rows["ln1_b"]),
                                            ALU.add).then_inc(h1_ready[u], 1)

                def shift_h1(u, p):
                    pool.wait_ge(h1_ready[u], p + 1)
                    nc.gpsimd.tensor_tensor(z[u][:, :, :], h1[u][:, :, :], per_tile(rows["f2_b"]),
                                            ALU.add).then_inc(h1_shifted[u], 1)

                def gain_shift_2(u, p):
                    pool.wait_ge(ln_norm[u], LT * (2 * p + 2))
                    pool.wait_ge(h1_turned[u], p + 1)
                    nc.gpsimd.tensor_tensor(h1[u][:, :, :], h1[u][:, :, :], per_tile(rows["ln2_g"]),
                                            ALU.mult).then_inc(ln_gain[u], 1)
                    pool.wait_ge(ln_gain[u], 2 * p + 2)
                    nc.gpsimd.tensor_tensor(h1[u][:, :, :], h1[u][:, :, :], ao_shift[u][:, :, :],
                                            ALU.add).then_inc(fused_ready[u], 1)

                def turn(a, b):
                    if a:
                        shift_x(*a)
                    if b:
                        inverse_root(b[0], 2 * b[1])
                        gain_shift_1(*b)
                        shift_h1(*b)
                    if a:
                        gather_next(*a)
                    if b:
                        inverse_root(b[0], 2 * b[1] + 1)
                        gain_shift_2(*b)

                for u in range(2):
                    nc.gpsimd.tensor_copy(top_col[u][0:TOP, :], top_row[0:TOP, u, :]).then_inc(col_ready[u], 1)
                for u in range(2):
                    pool.wait_ge(col_ready[u], 1)
                    gather(u)
                turns(pool, turn)
                for u in range(2):
                    pool.wait_ge(q_gathered[u], 16 * H0 * (PAIRS + 1))

            @block.tensor
            def _(pe):
                def transpose(dst, src, n=LT):
                    for t in range(n):
                        ins = nc.tensor.transpose(dst[:, t * P:(t + 1) * P], src[:, t, :], keep.ident[:, :])
                    return ins

                def project(u, p):
                    pe.wait_ge(xT_loaded[u], 16 * p + 16)
                    nc.tensor.matmul(bank[u][1][:, :], w_small["k_w"][:, :], xT[u][:, :], start=True,
                                     stop=True).then_inc(kT_done[u], 1)
                    for t in range(LT):
                        ins = nc.tensor.matmul(bank[u][2][:, t * P:(t + 1) * P], xT[u][:, t * P:(t + 1) * P],
                                               w_small["v_w"][:, :], start=True, stop=True)
                    ins.then_inc(v_done[u], 1)

                def turn_queries(u, p):
                    pe.wait_ge(q_gathered[u], 16 * H0 * (p + 1))
                    nc.tensor.transpose(bank[u][0][:, 0:TOP], q_top[u][0:TOP, :],
                                        keep.ident[0:TOP, 0:TOP]).then_inc(qT_done[u], 1)

                def mean_value(u, p):
                    pe.wait_ge(v_ready[u], p + 1)
                    pe.wait_ge(h_ready[u], START + p)
                    for t in range(LT):
                        ins = nc.tensor.matmul(bank[u][3][:, 0:D], mean_w[:, :], v1[u][:, t, :, 0:HD0],
                                               start=(t == 0), stop=(t == LT - 1))
                    ins.then_inc(mean_done[u], 1)

                def score(u, p, h):
                    if h == 0:
                        pe.wait_ge(q_diag_ready[u], p + 1)
                        pe.wait_ge(kT_ready[u], p + 1)
                    if h >= 2:
                        pe.wait_ge(probs_ready[u], START + H0 * p + h - 1)
                    nc.tensor.matmul(bank[u][h % 2][0:TOP, :], q_diag[u][:, h, :], kT[u][:, :],
                                     start=True, stop=True).then_inc(scores_done[u], 1)

                def turn_probs(u, p, h):
                    pe.wait_ge(probs_ready[u], START + H0 * p + h + 1)
                    if h:
                        pe.wait_ge(probsT_ready[u], START + H0 * p + h)
                    for t in range(LT):
                        ins = nc.tensor.transpose(bank[u][2][:, t * TOP:(t + 1) * TOP],
                                                  probs[u][0:TOP, h % 2, t * P:(t + 1) * P],
                                                  keep.ident[0:TOP, 0:TOP])
                    ins.then_inc(probs_turned[u], 1)

                def sum_values(u, p, h):
                    if h == 0:
                        pe.wait_ge(mean_ready[u], p + 1)
                    pe.wait_ge(probsT_ready[u], START + H0 * p + h + 1)
                    for t in range(LT):
                        ins = nc.tensor.matmul(bank[u][3][0:TOP, h * (HD0 + 1):(h + 1) * (HD0 + 1)],
                                               probsT[u][:, h % 2, t, :], v1[u][:, t, h, :],
                                               start=(t == 0), stop=(t == LT - 1))
                    ins.then_inc(o_done[u], 1)

                def place_outputs(u, p):
                    pe.wait_ge(place_ready[u], H0 * (p + 1))
                    pe.wait_ge(o_step[u], 6 * (p + 1))
                    for t in range(LT):
                        for h in range(H0):
                            for k in range(3):
                                ins = nc.tensor.matmul(
                                    bank[u][0][:, t * P + h * HD0:t * P + (h + 1) * HD0],
                                    place[u][0:TOP, h, t * P:(t + 1) * P],
                                    o_part[u][0:TOP, k, h * HD0:(h + 1) * HD0], start=(k == 0), stop=(k == 2))
                    ins.then_inc(o_placed[u], 1)

                def turn_attention(u, p):
                    pe.wait_ge(attn_ready[u], p + 1)
                    transpose(bank[u][1], attn[u]).then_inc(attn_turned[u], 1)

                def project_out(u, p):
                    pe.wait_ge(attnT_ready[u], p + 1)
                    for t in range(LT):
                        ins = nc.tensor.matmul(bank[u][2][:, t * P:(t + 1) * P], attnT[u][:, t * P:(t + 1) * P],
                                               w_small["o_w"][:, :], start=True, stop=True)
                    ins.then_inc(ao_done[u], 1)

                def turn_h1(u, p):
                    pe.wait_ge(h1_ready[u], p + 1)
                    transpose(bank[u][1], h1[u]).then_inc(h1_turned[u], 1)

                def up(u, p, chunks):
                    pe.wait_ge(h1T_ready[u], p + 1)
                    for c in chunks:
                        nc.tensor.matmul(bank[u][FF_BANK[c]][:, :], f1_w[:, c * P:(c + 1) * P], h1T[u][:, :],
                                         start=True, stop=True).then_inc(ff_done[u], 1)

                def down(u, p):
                    pe.wait_ge(ff_act[u], 2 * p + 2)
                    pe.wait_ge(ff_dve[u], 2 * p + 2)
                    for t in range(LT):
                        for c in range(FC):
                            ins = nc.tensor.matmul(bank[u][0][:, t * P:(t + 1) * P],
                                                   ff[u][:, c, t * P:(t + 1) * P], f2_w[:, c, :],
                                                   start=(c == 0), stop=(c == FC - 1))
                    ins.then_inc(y_done[u], 1)

                def turn_fused(u, p):
                    pe.wait_ge(fused_ready[u], START + p + 1)
                    transpose(bank[u][2], h1[u]).then_inc(fused_turned[u], 1)

                def convolve(u, p):
                    pe.wait_ge(fusedT_ready[u], p + 1)
                    for k in range(3):
                        ins = nc.tensor.matmul(bank[u][3][:, :], conv_w[:, k, :], fusedT[u][:, k:k + L],
                                               start=(k == 0), stop=(k == 2))
                    ins.then_inc(conv_done[u], 1)

                def turn_pooled(u, p):
                    pe.wait_ge(yT_ready[u], p + 1)
                    for t in range(PT):
                        ins = nc.tensor.transpose(bank[u][3][:, t * P:(t + 1) * P],
                                                  yT[u][:, t * P:(t + 1) * P], keep.ident[:, :])
                    ins.then_inc(y_turned[u], 1)

                def turn(a, b):
                    if a:
                        turn_queries(*a)
                        project(*a)
                    for s in range(H0 + 2):
                        if a and s < H0:
                            score(*a, s)
                        if a and s == 0:
                            mean_value(*a)
                        if a and 1 <= s <= H0:
                            turn_probs(*a, s - 1)
                        if a and s >= 2:
                            sum_values(*a, s - 2)
                        if b and s == TURN_H1:
                            turn_h1(*b)
                        if b and s == FF_LOW:
                            up(*b, (0, 1))
                        if b and s == FF_HIGH:
                            up(*b, (2, 3))
                        if b and s == FF_DOWN:
                            down(*b)
                    if b:
                        turn_fused(*b)
                    if a:
                        place_outputs(*a)
                    if b:
                        convolve(*b)
                    if a:
                        turn_attention(*a)
                        project_out(*a)
                    if b:
                        turn_pooled(*b)

                pe.wait_ge(weights, ALL_WEIGHTS)
                pe.wait_ge(const, CONSTS)
                turns(pe, turn)

            @block.scalar
            def _(act):
                def copy_kT(u, p):
                    act.wait_ge(kT_done[u], p + 1)
                    nc.scalar.activation(kT[u][:, :], bank[u][1][:, :], ACT.Identity,
                                         bias=cols["k_b"][:, 0:1]).then_inc(kT_ready[u], 1)

                def copy_mean(u, p):
                    act.wait_ge(mean_done[u], p + 1)
                    nc.scalar.copy(v_mean[u][:, :], bank[u][3][:, 0:D]).then_inc(mean_ready[u], 1)

                def raise_scores(u, p, h):
                    act.wait_ge(low_ready[u], H0 * p + h + 1)
                    if h >= 2:
                        act.wait_ge(probs_turned[u], START + H0 * p + h - 1)
                    nc.scalar.activation(probs[u][0:TOP, h % 2, :], bank[u][h % 2][0:TOP, :], ACT.Exp,
                                         bias=low[u][0:TOP, h:h + 1], scale=-1.0).then_inc(probs_ready[u], 1)

                def copy_probsT(u, p, h):
                    act.wait_ge(probs_turned[u], START + H0 * p + h + 1)
                    if h >= 2:
                        act.wait_ge(o_done[u], START + H0 * p + h - 1)
                    nc.scalar.copy(probsT[u][:, h % 2, :, :].rearrange("p t r -> p (t r)"),
                                   bank[u][2][:, 0:LT * TOP]).then_inc(probsT_ready[u], 1)

                def copy_attnT(u, p):
                    act.wait_ge(attn_turned[u], p + 1)
                    nc.scalar.copy(attnT[u][:, :], bank[u][1][:, :]).then_inc(attnT_ready[u], 1)

                def copy_h1T(u, p):
                    act.wait_ge(h1_turned[u], p + 1)
                    nc.scalar.copy(h1T[u][:, :], bank[u][1][:, :]).then_inc(h1T_ready[u], 1)

                def rectify(u, p, c):
                    act.wait_ge(ff_done[u], FC * p + c + 1)
                    nc.scalar.activation(ff[u][:, c, :], bank[u][FF_BANK[c]][:, :], ACT.Relu,
                                         bias=f1_b[:, c:c + 1]).then_inc(ff_act[u], 1)

                def copy_fusedT(u, p):
                    act.wait_ge(fused_turned[u], START + p + 1)
                    nc.scalar.copy(fusedT[u][:, 1:L + 1], bank[u][2][:, :]).then_inc(fusedT_ready[u], 1)

                def rectify_pooled(u, p):
                    act.wait_ge(pooled_ready[u], p + 1)
                    nc.scalar.activation(yT[u][:, :], pooled[u][:, :], ACT.Relu,
                                         bias=cols["conv_b"][:, 0:1]).then_inc(yT_ready[u], 1)

                def copy_h(u, p):
                    act.wait_ge(y_turned[u], p + 1)
                    nc.scalar.copy(keep.h[:, 2 * p + u, :, :].rearrange("p t d -> p (t d)"),
                                   bank[u][3][:, 0:LP]).then_inc(h_ready[u], 1)

                def turn(a, b):
                    if a:
                        copy_kT(*a)
                    for s in range(H0 + 1):
                        if a and s < H0:
                            raise_scores(*a, s)
                        if a and s == 0:
                            copy_mean(*a)
                        if a and s % 2 == 1:
                            copy_probsT(*a, s - 1)
                        if b and s == TURN_H1:
                            copy_h1T(*b)
                        if b and s == FF_LOW:
                            rectify(*b, 0)
                        if b and s == FF_HIGH:
                            rectify(*b, 2)
                    if b:
                        copy_fusedT(*b)
                    if a:
                        copy_attnT(*a)
                    if b:
                        rectify_pooled(*b)
                        copy_h(*b)

                act.wait_ge(weights, ALL_WEIGHTS)
                turns(act, turn)

            @block.vector
            def _(dve):
                def statistics(u, n):
                    for t in range(LT):
                        nc.vector.bn_stats(stats[u][:, t, :], z[u][:, t, :]).then_inc(ln_stats[u], 1)

                def mean_variance(u, n):
                    dve.wait_ge(ln_stats[u], LT * (n + 1))
                    stand_alone(dve, dve_seen)
                    for t in range(LT):
                        nc.vector.bn_aggr(mean_var[u][:, t, :], stats[u][:, t, :]).then_inc(ln_var[u], 1)

                def normalize(u, n):
                    dve.wait_ge(ln_root[u], n + 1)
                    for t in range(LT):
                        nc.vector.tensor_scalar(h1[u][:, t, :], z[u][:, t, :], mean_var[u][:, t, 0:1],
                                                rstd[u][:, t:t + 1], ALU.subtract, ALU.mult)\
                            .then_inc(ln_norm[u], 1)

                def mark_place(u, p, h):
                    nc.vector.tensor_scalar(place[u][0:TOP, h, :], iota_h[0:TOP, :],
                                            top_f32[0:TOP, 2 * p + u, h:h + 1], None,
                                            ALU.is_equal).then_inc(place_ready[u], 1)

                def shift_v(u, p):
                    dve.wait_ge(v_done[u], p + 1)
                    nc.vector.tensor_tensor(
                        v1[u][:, :, :, 0:HD0],
                        bank[u][2][:, :].rearrange("p (t h c) -> p t h c", t=LT, h=H0),
                        rows["v_b"][:, :].rearrange("p (h c) -> p h c", h=H0).unsqueeze(1)
                        .broadcast_to([P, LT, H0, HD0]), ALU.add).then_inc(v_ready[u], 1)

                def spread_queries(u, p):
                    dve.wait_ge(qT_done[u], p + 1)
                    nc.vector.tensor_tensor(
                        q_diag[u][:, :, :], bank[u][0][:, 0:TOP].unsqueeze(1).broadcast_to([P, H0, TOP]),
                        head_mask[:, :].unsqueeze(2).broadcast_to([P, H0, TOP]),
                        ALU.mult).then_inc(q_diag_ready[u], 1)

                def least_score(u, p, h):
                    dve.wait_ge(scores_done[u], H0 * p + h + 1)
                    nc.vector.tensor_reduce(low[u][0:TOP, h:h + 1], bank[u][h % 2][0:TOP, :], AX.X,
                                            ALU.min).then_inc(low_ready[u], 1)

                def copy_probsT(u, p, h):
                    dve.wait_ge(probs_turned[u], START + H0 * p + h + 1)
                    if h >= 2:
                        dve.wait_ge(o_done[u], START + H0 * p + h - 1)
                    nc.vector.tensor_copy(probsT[u][:, h % 2, :, :].rearrange("p t r -> p (t r)"),
                                          bank[u][2][:, 0:LT * TOP]).then_inc(probsT_ready[u], 1)

                def divide(u, p):
                    sums = bank[u][3][0:TOP, 0:H0 * (HD0 + 1)].rearrange("p (h c) -> p h c", h=H0)
                    top3 = o_top[u][0:TOP, :, :]
                    rest3 = o_rest[u][0:TOP, :, :]

                    def part(k):
                        return o_part[u][0:TOP, k, :].rearrange("p (h c) -> p h c", h=H0)

                    dve.wait_ge(o_done[u], START + H0 * (p + 1))
                    nc.vector.reciprocal(o_scale[u][0:TOP, :], sums[:, :, HD0]).then_inc(o_step[u], 1)
                    dve.wait_ge(o_step[u], 6 * p + 1)
                    nc.vector.tensor_tensor(top3, sums[:, :, 0:HD0],
                                            o_scale[u][0:TOP, :].unsqueeze(2).broadcast_to([TOP, H0, HD0]),
                                            ALU.mult).then_inc(o_step[u], 1)
                    dve.wait_ge(o_step[u], 6 * p + 2)
                    dve.wait_ge(mean_ready[u], p + 1)
                    nc.vector.tensor_tensor(top3, top3,
                                            v_mean[u][0:TOP, :].rearrange("p (h c) -> p h c", h=H0),
                                            ALU.subtract).then_inc(o_step[u], 1)
                    dve.wait_ge(o_step[u], 6 * p + 3)
                    nc.vector.tensor_copy(part(0), top3).then_inc(o_step[u], 1)
                    dve.wait_ge(o_step[u], 6 * p + 4)
                    nc.vector.tensor_tensor(rest3, top3, part(0), ALU.subtract).then_inc(o_rest_ready[u], 1)
                    dve.wait_ge(o_rest_ready[u], p + 1)
                    nc.vector.tensor_copy(part(1), rest3).then_inc(o_step[u], 1)
                    dve.wait_ge(o_step[u], 6 * p + 5)
                    nc.vector.tensor_tensor(part(2), rest3, part(1), ALU.subtract).then_inc(o_step[u], 1)

                def add_mean(u, p):
                    dve.wait_ge(o_placed[u], p + 1)
                    nc.vector.tensor_tensor(attn[u][:, :, :], tiles(bank[u][0][:, :]), per_tile(v_mean[u]),
                                            ALU.add).then_inc(attn_ready[u], 1)

                def add_x(u, p):
                    dve.wait_ge(ao_done[u], p + 1)
                    dve.wait_ge(x_shifted[u], p + 1)
                    nc.vector.tensor_tensor(z[u][:, :, :], tiles(bank[u][2][:, :]), x_shift[u][:, :, :],
                                            ALU.add).then_inc(z_ready[u], 1)
                    dve.wait_ge(fused_ready[u], START + p)
                    nc.vector.tensor_tensor(ao_shift[u][:, :, :], tiles(bank[u][2][:, :]), per_tile(out_shift),
                                            ALU.add).then_inc(ao_ready[u], 1)

                def rectify(u, p, c):
                    dve.wait_ge(ff_done[u], FC * p + c + 1)
                    nc.vector.tensor_scalar(ff[u][:, c, :], bank[u][FF_BANK[c]][:, :], f1_b[:, c:c + 1], 0.0,
                                            ALU.add, ALU.max).then_inc(ff_dve[u], 1)

                def add_h1(u, p):
                    dve.wait_ge(y_done[u], p + 1)
                    dve.wait_ge(h1_shifted[u], p + 1)
                    nc.vector.tensor_tensor(z[u][:, :, :], tiles(bank[u][0][:, :]), z[u][:, :, :],
                                            ALU.add).then_inc(z2_ready[u], 1)

                def pool_pairs(u, p):
                    dve.wait_ge(conv_done[u], p + 1)
                    nc.vector.tensor_reduce(pooled[u][:, :], bank[u][3][:, :].rearrange("p (l a) -> p l a", a=2),
                                            AX.X, ALU.max).then_inc(pooled_ready[u], 1)

                def turn(a, b):
                    if b:
                        dve.wait_ge(z_ready[b[0]], START + b[1] + 1)
                        statistics(b[0], 2 * b[1])
                        mean_variance(b[0], 2 * b[1])
                    if a:
                        spread_queries(*a)
                        shift_v(*a)
                    if b:
                        dve.wait_ge(fused_turned[b[0]], START + b[1])
                        normalize(b[0], 2 * b[1])
                    for s in range(H0 + 1):
                        if a and s < H0:
                            least_score(*a, s)
                            mark_place(*a, s)
                        if a and s >= 2 and s % 2 == 0:
                            copy_probsT(*a, s - 1)
                        if b and s == FF_LOW:
                            rectify(*b, 1)
                        if b and s == FF_HIGH:
                            rectify(*b, 3)
                        if b and s == ADD_H1:
                            add_h1(*b)
                        if b and s == NORM2_STATS:
                            dve.wait_ge(z2_ready[b[0]], b[1] + 1)
                            statistics(b[0], 2 * b[1] + 1)
                            mean_variance(b[0], 2 * b[1] + 1)
                        if b and s == NORM2:
                            normalize(b[0], 2 * b[1] + 1)
                    if a:
                        divide(*a)
                        add_mean(*a)
                    if b:
                        pool_pairs(*b)
                    if a:
                        add_x(*a)

                dve.wait_ge(iota_ready, 1)
                nc.vector.tensor_copy(iota_h[:, :], iota_i[:, :]).then_inc(iota_ready, 1)
                dve.wait_ge(iota_ready, 2)
                dve.wait_ge(weights, ALL_WEIGHTS)
                dve.wait_ge(shift_ready, 1)
                dve.wait_ge(const, CONSTS)
                turns(dve, turn)
        nc.clear_and_free_semaphores(sems)
        nc.all_engine_barrier()


H1, HD1 = 8, 64
HALF = HD1 // 2
W1 = H1 * HD1
WC = W1 // P
WIN = 128
RMS_EPS = 1e-6
MASKED = -1e30
LEAST = -3e38


def windowed_attention(nc, dram, keep):
    sems = []
    with ExitStack() as ctx:
        def sb(name, shape, dt=F32):
            return ctx.enter_context(nc.sbuf_tensor("w_" + name, shape, dt))

        def two(name, shape, dt=F32):
            return [sb(f"{name}{u}", shape, dt) for u in range(2)]

        def sem(name):
            sems.append(nc.alloc_semaphore("w_" + name))
            return sems[-1]

        def sem2(name):
            return [sem(f"{name}{u}") for u in range(2)]

        w_qkv = [sb(n, [P, W1]) for n in ("W_q", "W_k", "W_v")]
        w_out = sb("W_o", [P, WC, D])
        rope = sb("rope", [P, 2, PT, HD1])
        norm_w = sb("norm_w", [P, 2, HD1])
        cos_w = sb("cos_w", [P, 2, PT, HD1])
        sin_w = sb("sin_w", [P, 2, PT, HD1])
        win_mask = sb("win_mask", [P, 3 * P])
        half_neg = sb("half_neg", [P, 4 * H1])
        eps = sb("eps", [P, PT])
        rms_eps = sb("rms_eps", [P, 4 * H1])

        stats = two("stats", [P, PT, 6])
        mean_var = two("mean_var", [P, PT, 2])
        rstd = two("rstd", [P, PT])
        hn = two("hn", [P, PT, D])
        hnT = two("hnT", [P, LP])
        v_sb = two("v", [P, PT, W1])
        squares = two("squares", [P, 2, H1, HD1])
        sum_sq = two("sum_sq", [P, PT, 2, H1])
        root = two("root", [P, PT, 2, H1])
        t1 = two("t1", [P, 2, H1, HD1])
        t2 = two("t2", [P, 2, H1, HD1])
        qk = two("qk", [P, PT, 2, W1])
        qkT = two("qkT", [P, 2, WC, LP])
        masked = two("masked", [P, 2, 3 * P])
        top = two("top", [P, H1, PT])
        bias = two("bias", [P, H1, PT])
        probs = two("probs", [P, 2, 3 * P])
        probsT = two("probsT", [P, 2, 3 * P])
        total = two("total", [P, PT, H1])
        scale = two("scale", [P, PT, H1])
        o_sb = two("o", [P, PT, W1])
        oT = two("oT", [P, PT, WC, P])

        bank = [[ctx.enter_context(nc.psum_tensor(f"w_bank{u}{k}", [P, 512], F32)) for k in range(4)]
                for u in range(2)]

        weights = sem("weights")
        const = sem("const")
        dve_seen = sem("dve_seen")
        pool_seen = sem("pool_seen")
        tables = sem("tables")
        ln_stats, ln_var, ln_eps, ln_root, hn_ready = map(
            sem2, ("ln_stats", "ln_var", "ln_eps", "ln_root", "hn_ready"))
        hn_turned, hnT_ready, qkv_done, v_copied = map(sem2, ("hn_turned", "hnT_ready", "qkv_done", "v_copied"))
        squared, summed, rotated, added, root_eps, root_ready, k_scaled = map(
            sem2, ("squared", "summed", "rotated", "added", "root_eps", "root_ready", "k_scaled"))
        qk_turned, qkT_ready = map(sem2, ("qk_turned", "qkT_ready"))
        scores_done, masked_ready, bias_ready, probs_ready = map(
            sem2, ("scores_done", "masked_ready", "bias_ready", "probs_ready"))
        probs_turned, probsT_ready, o_done = map(sem2, ("probs_turned", "probsT_ready", "o_done"))
        scale_ready, o_ready, o_turned, oT_ready, out_done, h_ready = map(
            sem2, ("scale_ready", "o_ready", "o_turned", "oT_ready", "out_done", "h_ready"))

        loads = [(w[:, :], dram[n]) for w, n in zip(w_qkv, ("W_q", "W_k", "W_v"))]
        loads += [(w_out[:, :, :], dram["W_o"].rearrange("(c p) d -> p c d", p=P))]
        loads += [(rope[:, i, :, :], dram[n][0:LP, :].rearrange("(t p) c -> p t c", p=P))
                  for i, n in enumerate(("rope_cos", "rope_sin"))]
        loads += [(norm_w[:, i, :], dram[n].partition_broadcast(P))
                  for i, n in enumerate(("q_norm_w", "k_norm_w"))]
        ALL_WEIGHTS = 16 * len(loads)
        CONSTS = 7
        TABLES = 7
        PRODUCTS = ((0, 0, 1), (0, 1, 2), (0, 2, 3), (1, 0, 0), (1, 1, 1), (1, 2, 2))
        QK = [(n, t, w, k) for n, (t, w, k) in enumerate(PRODUCTS) if w < 2]

        start_counts(nc, [*h_ready, *masked_ready, *probsT_ready, *summed, *probs_turned, *o_done, *added,
                          *probs_ready])

        with nc.Block() as block:
            @block.sync
            def _(sp):
                for dst, src in loads:
                    sp.dma_start(dst, src).then_inc(weights, 16)
                sp.wait_ge(weights, ALL_WEIGHTS)

            @block.gpsimd
            def _(pool):
                nc.gpsimd.memset(half_neg[:, :], -0.5).then_inc(const, 1)
                nc.gpsimd.memset(eps[:, :], LN_EPS).then_inc(const, 1)
                nc.gpsimd.memset(rms_eps[:, :], HD1 * RMS_EPS).then_inc(const, 1)
                nc.gpsimd.memset(win_mask[:, :], 0.0).then_inc(const, 1)
                pool.wait_ge(const, 4)
                nc.gpsimd.affine_select(out=win_mask[:, 0:P], in_=win_mask[:, 0:P], compare_op=ALU.is_ge,
                                        fill=MASKED, base=0, pattern=[[-1, P]],
                                        channel_multiplier=1).then_inc(const, 1)
                nc.gpsimd.affine_select(out=win_mask[:, P:], in_=win_mask[:, P:], compare_op=ALU.is_ge,
                                        fill=MASKED, base=P, pattern=[[-1, 2 * P]],
                                        channel_multiplier=1).then_inc(const, 1)
                pool.wait_ge(const, 6)
                nc.gpsimd.affine_select(out=win_mask[:, P:], in_=win_mask[:, P:], compare_op=ALU.is_ge,
                                        fill=MASKED, base=WIN - 1 - P, pattern=[[1, 2 * P]],
                                        channel_multiplier=-1).then_inc(const, 1)
                pool.wait_ge(weights, ALL_WEIGHTS)
                nc.gpsimd.tensor_scalar(norm_w[:, 1, :], norm_w[:, 1, :], float(HD1) ** 0.5, 1.0, ALU.mult,
                                        ALU.mult).then_inc(tables, 1)
                pool.wait_ge(tables, 1)
                for i in range(2):
                    def over_tiles(lo, hi):
                        return norm_w[:, i, lo:hi].unsqueeze(1).broadcast_to([P, PT, hi - lo])

                    nc.gpsimd.tensor_tensor(cos_w[:, i, :, :], rope[:, 0, :, :], over_tiles(0, HD1),
                                            ALU.mult).then_inc(tables, 1)
                    nc.gpsimd.tensor_tensor(sin_w[:, i, :, 0:HALF], rope[:, 1, :, 0:HALF], over_tiles(HALF, HD1),
                                            ALU.mult).then_inc(tables, 1)
                    nc.gpsimd.tensor_tensor(sin_w[:, i, :, HALF:], rope[:, 1, :, HALF:], over_tiles(0, HALF),
                                            ALU.mult).then_inc(tables, 1)
                pool.wait_ge(tables, TABLES)
                nc.gpsimd.tensor_scalar(sin_w[:, :, :, 0:HALF], sin_w[:, :, :, 0:HALF], -1.0, 1.0, ALU.mult,
                                        ALU.mult).then_inc(tables, 1)
                with pool.Fori(0, PAIRS) as p:
                    for u in range(2):
                        pool.wait_ge(ln_var[u], PT * (p + 1))
                        nc.gpsimd.tensor_tensor(rstd[u][:, :], mean_var[u][:, :, 1], eps[:, :],
                                                ALU.add).then_inc(ln_eps[u], 1)
                        pool.wait_ge(ln_eps[u], p + 1)
                        nc.gpsimd.tensor_tensor(rstd[u][:, :], rstd[u][:, :], half_neg[:, 0:PT],
                                                ALU.pow).then_inc(ln_root[u], 1)
                    for i, (_, t, w, _) in enumerate(QK):
                        for u in range(2):
                            pool.wait_ge(rotated[u], 12 * p + 3 * i + 3)
                            nc.gpsimd.tensor_tensor(
                                qk[u][:, t, w, :], t1[u][:, i % 2, :, :].rearrange("p h c -> p (h c)"),
                                t2[u][:, i % 2, :, :].rearrange("p h c -> p (h c)"), ALU.add)\
                                .then_inc(added[u], 1)
                    for u in range(2):
                        pool.wait_ge(summed[u], START + 4 * (p + 1))
                        nc.gpsimd.tensor_tensor(
                            root[u][:, :, :, :].rearrange("p t w h -> p (t w h)"),
                            sum_sq[u][:, :, :, :].rearrange("p t w h -> p (t w h)"), rms_eps[:, :],
                            ALU.add).then_inc(root_eps[u], 1)
                        pool.wait_ge(root_eps[u], p + 1)
                        nc.gpsimd.tensor_tensor(
                            root[u][:, :, :, :].rearrange("p t w h -> p (t w h)"),
                            root[u][:, :, :, :].rearrange("p t w h -> p (t w h)"), half_neg[:, :],
                            ALU.pow).then_inc(root_ready[u], 1)

            @block.tensor
            def _(pe):
                pe.wait_ge(weights, ALL_WEIGHTS)
                with pe.Fori(0, PAIRS) as p:
                    for u in range(2):
                        pe.wait_ge(hn_ready[u], PT * (p + 1))
                        for t in range(PT):
                            ins = nc.tensor.transpose(bank[u][0][:, t * P:(t + 1) * P], hn[u][:, t, :],
                                                      keep.ident[:, :])
                        ins.then_inc(hn_turned[u], 1)
                    for n, (t, w, k) in enumerate(PRODUCTS):
                        for u in range(2):
                            if n == 0:
                                pe.wait_ge(hnT_ready[u], p + 1)
                                pe.wait_ge(h_ready[u], START + p)
                            if n == 4:
                                pe.wait_ge(rotated[u], 12 * p + 3)
                                pe.wait_ge(squared[u], 4 * p + 1)
                            if n == 5:
                                pe.wait_ge(rotated[u], 12 * p + 6)
                                pe.wait_ge(squared[u], 4 * p + 2)
                            nc.tensor.matmul(bank[u][k][:, :], hnT[u][:, t * P:(t + 1) * P], w_qkv[w][:, :],
                                             start=True, stop=True).then_inc(qkv_done[u], 1)
                    for i in range(4):
                        t, w = i % 2, i // 2
                        for u in range(2):
                            if i == 0:
                                pe.wait_ge(added[u], START + 4 * (p + 1))
                                pe.wait_ge(squared[u], 4 * (p + 1))
                                pe.wait_ge(v_copied[u], 2 * (p + 1))
                            if w == 1:
                                pe.wait_ge(k_scaled[u], 2 * p + t + 1)
                            for c in range(WC):
                                ins = nc.tensor.transpose(bank[u][i][:, c * P:(c + 1) * P],
                                                          qk[u][:, t, w, c * P:(c + 1) * P], keep.ident[:, :])
                            ins.then_inc(qk_turned[u], 1)
                    for s in range(H1 + 2):
                        for u in range(2):
                            if s < H1:
                                if s == 0:
                                    pe.wait_ge(qkT_ready[u], 4 * (p + 1))
                                else:
                                    pe.wait_ge(masked_ready[u], START + 2 * (H1 * p + s))
                                c, lo = s // 2, HD1 * (s % 2)
                                q, k = (qkT[u][lo:lo + HD1, w, c, :] for w in range(2))
                                nc.tensor.matmul(bank[u][0][:, 0:P], q[:, 0:P], k[:, 0:P], start=True, stop=True)
                                nc.tensor.matmul(bank[u][0][:, P:3 * P], q[:, P:], k[:, :], start=True,
                                                 stop=True).then_inc(scores_done[u], 1)
                            if 1 <= s <= H1:
                                h = s - 1
                                pe.wait_ge(probs_ready[u], START + 2 * (H1 * p + h + 1))
                                if h:
                                    pe.wait_ge(probsT_ready[u], START + H1 * p + h)
                                for j in range(3):
                                    ins = nc.tensor.transpose(bank[u][1][:, j * P:(j + 1) * P],
                                                              probs[u][:, h % 2, j * P:(j + 1) * P],
                                                              keep.ident[:, :])
                                ins.then_inc(probs_turned[u], 1)
                            if s >= 2:
                                h = s - 2
                                pe.wait_ge(probsT_ready[u], START + H1 * p + h + 1)
                                cols = slice(h * HD1, (h + 1) * HD1)
                                for j, (t, kt) in enumerate(((0, 0), (1, 0), (1, 1))):
                                    ins = nc.tensor.matmul(bank[u][2 + t][:, cols],
                                                           probsT[u][:, h % 2, j * P:(j + 1) * P],
                                                           v_sb[u][:, kt, cols], start=(kt == 0), stop=(j != 1))
                                ins.then_inc(o_done[u], 1)
                    for t in range(PT):
                        for u in range(2):
                            pe.wait_ge(o_ready[u], PT * p + t + 1)
                            for c in range(WC):
                                ins = nc.tensor.transpose(bank[u][t][:, c * P:(c + 1) * P],
                                                          o_sb[u][:, t, c * P:(c + 1) * P], keep.ident[:, :])
                            ins.then_inc(o_turned[u], 1)
                    for u in range(2):
                        pe.wait_ge(oT_ready[u], PT * (p + 1))
                        for t in range(PT):
                            for c in range(WC):
                                ins = nc.tensor.matmul(bank[u][2][:, t * P:(t + 1) * P], oT[u][:, t, c, :],
                                                       w_out[:, c, :], start=(c == 0), stop=(c == WC - 1))
                        ins.then_inc(out_done[u], 1)

            @block.scalar
            def _(act):
                act.wait_ge(weights, ALL_WEIGHTS)
                with act.Fori(0, PAIRS) as p:
                    for u in range(2):
                        act.wait_ge(hn_turned[u], p + 1)
                        nc.scalar.copy(hnT[u][:, :], bank[u][0][:, 0:LP]).then_inc(hnT_ready[u], 1)
                    i = 0
                    for n, (t, w, k) in enumerate(PRODUCTS):
                        for u in range(2):
                            act.wait_ge(qkv_done[u], 6 * p + n + 1)
                            if w == 2:
                                nc.scalar.copy(v_sb[u][:, t, :], bank[u][k][:, :]).then_inc(v_copied[u], 1)
                            else:
                                if i >= 2:
                                    act.wait_ge(summed[u], START + 4 * p + i - 1)
                                nc.scalar.activation(squares[u][:, i % 2, :, :].rearrange("p h c -> p (h c)"),
                                                     bank[u][k][:, :], ACT.Square).then_inc(squared[u], 1)
                        i += w < 2
                    for i in range(4):
                        t, w = i % 2, i // 2
                        for u in range(2):
                            act.wait_ge(qk_turned[u], 4 * p + i + 1)
                            nc.scalar.copy(qkT[u][:, w, :, t * P:(t + 1) * P],
                                           bank[u][i][:, :].rearrange("p (c l) -> p c l", c=WC))\
                                .then_inc(qkT_ready[u], 1)
                    for s in range(H1 + 1):
                        for u in range(2):
                            if s < H1:
                                act.wait_ge(bias_ready[u], H1 * p + s + 1)
                                if s >= 2:
                                    act.wait_ge(probs_turned[u], START + H1 * p + s - 1)
                                for t, cols in enumerate((slice(0, P), slice(P, 3 * P))):
                                    nc.scalar.activation(probs[u][:, s % 2, cols], masked[u][:, s % 2, cols],
                                                         ACT.Exp, bias=bias[u][:, s, t:t + 1],
                                                         scale=root[u][:, t, 0, s:s + 1],
                                                         accum_out=total[u][:, t, s:s + 1])\
                                        .then_inc(probs_ready[u], 1)
                            if s % 2 == 1:
                                h = s - 1
                                act.wait_ge(probs_turned[u], START + H1 * p + h + 1)
                                if h >= 2:
                                    act.wait_ge(o_done[u], START + H1 * p + h - 1)
                                nc.scalar.copy(probsT[u][:, h % 2, :], bank[u][1][:, 0:3 * P])\
                                    .then_inc(probsT_ready[u], 1)
                    for t in range(PT):
                        for u in range(2):
                            act.wait_ge(o_turned[u], PT * p + t + 1)
                            nc.scalar.copy(oT[u][:, t, :, :].rearrange("p c l -> p (c l)"),
                                           bank[u][t][:, :]).then_inc(oT_ready[u], 1)

            @block.vector
            def _(dve):
                dve.wait_ge(tables, TABLES + 1)
                dve.wait_ge(const, CONSTS)
                with dve.Fori(0, PAIRS) as p:
                    for u in range(2):
                        for t in range(PT):
                            nc.vector.bn_stats(stats[u][:, t, :], keep.h[:, 2 * p + u, t, :])\
                                .then_inc(ln_stats[u], 1)
                        dve.wait_ge(ln_stats[u], PT * (p + 1))
                        stand_alone(dve, dve_seen)
                        for t in range(PT):
                            nc.vector.bn_aggr(mean_var[u][:, t, :], stats[u][:, t, :]).then_inc(ln_var[u], 1)
                    for u in range(2):
                        dve.wait_ge(ln_root[u], p + 1)
                        for t in range(PT):
                            nc.vector.tensor_scalar(hn[u][:, t, :], keep.h[:, 2 * p + u, t, :],
                                                    mean_var[u][:, t, 0:1], rstd[u][:, t:t + 1],
                                                    ALU.subtract, ALU.mult).then_inc(hn_ready[u], 1)
                    for i, (n, t, w, k) in enumerate(QK):
                        for u in range(2):
                            x = bank[u][k][:, :].rearrange("p (h c) -> p h c", h=H1)

                            def over_heads(table, lo, hi):
                                return table[:, w, t, lo:hi].unsqueeze(1).broadcast_to([P, H1, hi - lo])

                            dve.wait_ge(squared[u], 4 * p + i + 1)
                            if i >= 2:
                                dve.wait_ge(added[u], START + 4 * p + i - 1)
                            nc.vector.tensor_tensor(t1[u][:, i % 2, :, :], x, over_heads(cos_w, 0, HD1),
                                                    ALU.mult).then_inc(rotated[u], 1)
                            nc.vector.tensor_tensor(t2[u][:, i % 2, :, 0:HALF], x[:, :, HALF:],
                                                    over_heads(sin_w, 0, HALF), ALU.mult).then_inc(rotated[u], 1)
                            nc.vector.tensor_tensor(t2[u][:, i % 2, :, HALF:], x[:, :, 0:HALF],
                                                    over_heads(sin_w, HALF, HD1), ALU.mult)\
                                .then_inc(rotated[u], 1)
                            nc.vector.tensor_reduce(sum_sq[u][:, t, w, :], squares[u][:, i % 2, :, :], AX.X,
                                                    ALU.add).then_inc(summed[u], 1)
                    for u in range(2):
                        dve.wait_ge(root_ready[u], p + 1)
                        dve.wait_ge(added[u], START + 4 * (p + 1))
                        for t in range(PT):
                            k3 = qk[u][:, t, 1, :].rearrange("p (h c) -> p h c", h=H1)
                            nc.vector.tensor_tensor(k3, k3, root[u][:, t, 1, :].unsqueeze(2)
                                                    .broadcast_to([P, H1, HD1]), ALU.mult)\
                                .then_inc(k_scaled[u], 1)
                    for s in range(H1 + 1):
                        for u in range(2):
                            if s < H1:
                                dve.wait_ge(scores_done[u], H1 * p + s + 1)
                                if s >= 2:
                                    dve.wait_ge(probs_ready[u], START + 2 * (H1 * p + s - 1))
                                stand_alone(dve, dve_seen)
                                for t, cols in enumerate((slice(0, P), slice(P, 3 * P))):
                                    nc.vector.tensor_tensor_reduce(
                                        masked[u][:, s % 2, cols], bank[u][0][:, cols], win_mask[:, cols], 1.0,
                                        LEAST, ALU.add, ALU.max, top[u][:, s, t:t + 1])\
                                        .then_inc(masked_ready[u], 1)
                                dve.wait_ge(masked_ready[u], START + 2 * (H1 * p + s + 1))
                                nc.vector.scalar_tensor_tensor(out=bias[u][:, s, :], in0=top[u][:, s, :],
                                                               scalar=-1.0, in1=root[u][:, :, 0, s],
                                                               op0=ALU.mult, op1=ALU.mult)\
                                    .then_inc(bias_ready[u], 1)
                            if s >= 2 and s % 2 == 0:
                                h = s - 1
                                dve.wait_ge(probs_turned[u], START + H1 * p + h + 1)
                                if h >= 2:
                                    dve.wait_ge(o_done[u], START + H1 * p + h - 1)
                                nc.vector.tensor_copy(probsT[u][:, h % 2, :], bank[u][1][:, 0:3 * P])\
                                    .then_inc(probsT_ready[u], 1)
                    for u in range(2):
                        dve.wait_ge(probs_ready[u], START + 2 * H1 * (p + 1))
                        nc.vector.reciprocal(scale[u][:, :, :], total[u][:, :, :]).then_inc(scale_ready[u], 1)
                    for t in range(PT):
                        for u in range(2):
                            dve.wait_ge(scale_ready[u], p + 1)
                            dve.wait_ge(o_done[u], START + H1 * (p + 1))
                            nc.vector.tensor_tensor(
                                o_sb[u][:, t, :].rearrange("p (h c) -> p h c", h=H1),
                                bank[u][2 + t][:, :].rearrange("p (h c) -> p h c", h=H1),
                                scale[u][:, t, :].unsqueeze(2).broadcast_to([P, H1, HD1]),
                                ALU.mult).then_inc(o_ready[u], 1)
                    for u in range(2):
                        dve.wait_ge(out_done[u], p + 1)
                        nc.vector.tensor_tensor(keep.h[:, 2 * p + u, :, :], keep.h[:, 2 * p + u, :, :],
                                                bank[u][2][:, 0:LP].rearrange("p (t d) -> p t d", t=PT),
                                                ALU.add).then_inc(h_ready[u], 1)
        nc.clear_and_free_semaphores(sems)
        nc.all_engine_barrier()


E0 = 32
NT = B * PT
TOK = NT * P
CAP = TOK // E0
CT = CAP // P
ROW = D + E0
TG = P // E0
NG = NT // TG
DIGIT = 16
EG = P // DIGIT
LISTS = E0 // EG


def route(nc, dram, keep):
    sems = []
    with ExitStack() as ctx:
        def sb(name, shape, dt=F32):
            return ctx.enter_context(nc.sbuf_tensor("r_" + name, shape, dt))

        def two(name, shape, dt=F32):
            return [sb(f"{name}{u}", shape, dt) for u in range(2)]

        def sem(name):
            sems.append(nc.alloc_semaphore("r_" + name))
            return sems[-1]

        def sem2(name):
            return [sem(f"{name}{u}") for u in range(2)]

        w_router = sb("w_router", [P, E0])
        b_router = sb("b_router", [P, E0])
        half_neg = sb("half_neg", [P, PT])
        eps = sb("eps", [P, PT])
        ident_h = sb("ident_h", [P, P], BF16)
        before = sb("before", [P, P], BF16)
        ones = sb("ones", [P, P], BF16)
        same_expert = sb("same_expert", [P, P])
        own_list = sb("own_list", [P, EG])
        digits_i = sb("digits_i", [P, DIGIT], I32)
        digits = sb("digits", [P, DIGIT], BF16)
        lane_i = sb("lane_i", [P, 1], I32)
        lane = sb("lane", [P, 1])
        not_first = sb("not_first", [P, E0, NT])

        stats = two("stats", [P, PT, 6])
        mean_var = two("mean_var", [P, PT, 2])
        rstd = two("rstd", [P, PT])
        hn = two("hn", [P, PT, D])
        hnT = two("hnT", [P, LP])
        prob = sb("prob", [P, NT, E0])
        high = sb("high", [P, NT])
        total = sb("total", [P, NT])
        probT = sb("probT", [P, NG, P])
        hits = sb("hits", [P, NG * P], BF16)
        count = sb("count", [P, 1])
        bit = sb("bit", [P, 1], I32)
        least = sb("least", [P, 1], I32)
        tried = sb("tried", [P, 1], I32)
        gain = sb("gain", [P, 1], I32)
        aboveT = sb("aboveT", [P, NG, P], BF16)
        levelT = sb("levelT", [P, NG, P], BF16)
        above = sb("above", [P, NT, E0], BF16)
        level = sb("level", [P, NT, E0], BF16)
        chosen = sb("chosen", [P, NT, E0], BF16)
        inside = sb("inside", [P, NT, E0])
        per_tile = sb("per_tile", [P, E0, NT])
        upto = sb("upto", [P, E0, NT])
        wanted = sb("wanted", [P, E0])
        pos_i = sb("pos_i", [P, NT, E0], I32)
        digit_i = sb("digit_i", [P, NT, E0], I32)
        digit_a = sb("digit_a", [P, NT, E0], BF16)
        digit_b = sb("digit_b", [P, NT, E0], BF16)
        hot_a = [sb(f"hot_a{k}", [P, E0, DIGIT], BF16) for k in range(2)]
        hot_b = [sb(f"hot_b{k}", [P, E0, DIGIT], BF16) for k in range(2)]
        tile_b = [sb(f"tile_b{k}", [P, E0, DIGIT], BF16) for k in range(2)]
        lane_b = [sb(f"lane_b{k}", [P, E0, DIGIT], BF16) for k in range(2)]
        picked = sb("picked", [P, EG, DIGIT])
        half = sb("half", [P, LISTS, 2, DIGIT])
        lists = sb("lists", [P, LISTS, DIGIT])
        lists_r = sb("lists_r", [E0 * CT, P])

        bank = [ctx.enter_context(nc.psum_tensor(f"r_bank{k}", [P, 512], F32)) for k in range(8)]

        weights = sem("weights")
        const = sem("const")
        dve_seen = sem("dve_seen")
        cast = sem("cast")
        ln_stats, ln_var, ln_eps, ln_root, hn_ready = map(
            sem2, ("ln_stats", "ln_var", "ln_eps", "ln_root", "hn_ready"))
        hn_turned, hnT_ready, logits_done, logits_ready, row_stored = map(
            sem2, ("hn_turned", "hnT_ready", "logits_done", "logits_ready", "row_stored"))
        softmax_step, exp_done, prob_stored = sem("softmax_step"), sem("exp_done"), sem("prob_stored")
        prob_turned, probT_ready = sem("prob_turned"), sem("probT_ready")
        start_ready, tried_ready, counted, summed, gained, least_ready, bit_ready = map(
            sem, ("start_ready", "tried_ready", "counted", "summed", "gained", "least_ready", "bit_ready"))
        markT_ready, mark_turned, mark_ready = map(sem, ("markT_ready", "mark_turned", "mark_ready"))
        inside_done, inside_ready, tiles_done, tiles_ready = map(
            sem, ("inside_done", "inside_ready", "tiles_done", "tiles_ready"))
        step = sem("step")
        listed = sem("listed")
        a_ready, b_ready, tile_b_ready, lane_b_ready = map(sem, ("a_ready", "b_ready", "tile_b_ready", "lane_b_ready"))
        half_ready, lists_ready = sem("half_ready"), sem("lists_ready")
        list_step, list_stored, list_loaded, list_turned, tokens_ready = map(
            sem, ("list_step", "list_stored", "list_loaded", "list_turned", "tokens_ready"))

        rows_d = dram["token_rows"]
        feat_d = rows_d[:, 0:D].rearrange("(n t p) d -> n p t d", t=PT, p=P)
        prob_d = rows_d[:, D:ROW].rearrange("(t p) e -> p t e", p=P)
        CONSTS = 12

        start_counts(nc, [*logits_ready, tiles_ready, *row_stored, *hn_turned, least_ready, bit_ready])

        with nc.Block() as block:
            @block.sync
            def _(sp):
                sp.dma_start(w_router[:, :], dram["W_router"]).then_inc(weights, 16)
                sp.dma_start(b_router[:, :], dram["b_router"].partition_broadcast(P)).then_inc(weights, 16)
                with sp.Fori(0, PAIRS) as p:
                    for u in range(2):
                        sp.wait_ge(hn_ready[u], PT * (p + 1))
                        sp.dma_start(feat_d[2 * p + u], hn[u][:, :, :]).then_inc(row_stored[u], 16)
                sp.wait_ge(softmax_step, 5)
                sp.dma_start(prob_d, prob[:, :, :]).then_inc(prob_stored, 16)
                sp.wait_ge(lists_ready, LISTS)
                flat = dram["lists"]
                sp.dma_start(flat.rearrange("(g p b) -> p g b", g=LISTS, p=P), lists[:, :, :])\
                    .then_inc(list_stored, 16)
                sp.wait_ge(list_stored, 16)
                sp.dma_start(lists_r[:, :], flat.rearrange("(c r) -> c r", r=P)).then_inc(list_loaded, 16)
                for u in range(2):
                    sp.wait_ge(row_stored[u], START + 16 * PAIRS)
                sp.wait_ge(prob_stored, 16)

            @block.gpsimd
            def _(pool):
                nc.gpsimd.memset(half_neg[:, :], -0.5).then_inc(const, 1)
                nc.gpsimd.memset(eps[:, :], LN_EPS).then_inc(const, 1)
                nc.gpsimd.memset(before[:, :], 1.0).then_inc(const, 1)
                nc.gpsimd.memset(ones[:, :], 1.0).then_inc(const, 1)
                nc.gpsimd.memset(same_expert[:, :], 0.0).then_inc(const, 1)
                nc.gpsimd.memset(own_list[:, :], 1.0).then_inc(const, 1)
                nc.gpsimd.memset(not_first[:, :, :], 1.0).then_inc(const, 1)
                nc.gpsimd.iota(digits_i[:, :], pattern=[[1, DIGIT]], base=0, channel_multiplier=0)\
                    .then_inc(const, 1)
                nc.gpsimd.iota(lane_i[:, :], pattern=[[1, 1]], base=0, channel_multiplier=1).then_inc(const, 1)
                pool.wait_ge(const, 9)
                nc.gpsimd.memset(not_first[:, :, 0:1], 0.0).then_inc(const, 1)
                nc.gpsimd.affine_select(out=before[:, :], in_=before[:, :], compare_op=ALU.is_ge, fill=0.0,
                                        base=-1, pattern=[[1, P]], channel_multiplier=-1).then_inc(const, 1)
                nc.gpsimd.affine_select(out=own_list[:, :], in_=own_list[:, :], compare_op=ALU.is_ge, fill=0.0,
                                        base=0, pattern=[[-DIGIT, EG]], channel_multiplier=1).then_inc(const, 1)
                pool.wait_ge(const, 12)
                nc.gpsimd.affine_select(out=own_list[:, :], in_=own_list[:, :], compare_op=ALU.is_ge, fill=0.0,
                                        base=DIGIT - 1, pattern=[[DIGIT, EG]], channel_multiplier=-1)\
                    .then_inc(cast, 1)
                for n, off in enumerate(range(-P + E0, P, E0)):
                    pool.wait_ge(cast, 1 + n)
                    nc.gpsimd.affine_select(out=same_expert[:, :], in_=same_expert[:, :],
                                            compare_op=ALU.not_equal, fill=1.0, base=off, pattern=[[-1, P]],
                                            channel_multiplier=1).then_inc(cast, 1)
                pool.wait_ge(cast, 2 * TG)
                nc.gpsimd.tensor_copy(ident_h[:, :], keep.ident[:, :]).then_inc(cast, 1)
                nc.gpsimd.tensor_copy(digits[:, :], digits_i[:, :]).then_inc(cast, 1)
                nc.gpsimd.tensor_copy(lane[:, :], lane_i[:, :]).then_inc(cast, 1)
                with pool.Fori(0, PAIRS) as p:
                    for u in range(2):
                        pool.wait_ge(ln_var[u], PT * (p + 1))
                        nc.gpsimd.tensor_tensor(rstd[u][:, :], mean_var[u][:, :, 1], eps[:, :],
                                                ALU.add).then_inc(ln_eps[u], 1)
                        pool.wait_ge(ln_eps[u], p + 1)
                        nc.gpsimd.tensor_tensor(rstd[u][:, :], rstd[u][:, :], half_neg[:, :],
                                                ALU.pow).then_inc(ln_root[u], 1)

            CASTS = 2 * TG + 3

            @block.tensor
            def _(pe):
                pe.wait_ge(weights, 32)
                with pe.Fori(0, PAIRS) as p:
                    for u in range(2):
                        pe.wait_ge(hn_ready[u], PT * (p + 1))
                        for t in range(PT):
                            ins = nc.tensor.transpose(bank[u][:, t * P:(t + 1) * P], hn[u][:, t, :],
                                                      keep.ident[:, :])
                        ins.then_inc(hn_turned[u], 1)
                    for u in range(2):
                        pe.wait_ge(hnT_ready[u], p + 1)
                        pe.wait_ge(logits_ready[u], START + p)
                        for t in range(PT):
                            ins = nc.tensor.matmul(bank[2 + u][:, t * E0:(t + 1) * E0],
                                                   hnT[u][:, t * P:(t + 1) * P], w_router[:, :], start=True,
                                                   stop=True)
                        ins.then_inc(logits_done[u], 1)
                pe.wait_ge(softmax_step, 5)
                for g in range(NG):
                    k = 4 + g % 4
                    if g >= 4:
                        pe.wait_ge(probT_ready, g - 3)
                    nc.tensor.transpose(bank[k][:, 0:P],
                                        prob[:, TG * g:TG * (g + 1), :].rearrange("p t e -> p (t e)"),
                                        keep.ident[:, :]).then_inc(prob_turned, 1)
                pe.wait_ge(cast, CASTS)
                with pe.Fori(0, 30) as r:
                    pe.wait_ge(counted, r + 1)
                    nc.tensor.matmul(bank[0][:, 0:1], same_expert[:, :], count[:, :], start=True, stop=True)\
                        .then_inc(summed, 1)
                for n, src in enumerate((aboveT, levelT)):
                    pe.wait_ge(markT_ready, n + 1)
                    for q in range(4):
                        k = 4 * n + q
                        dst = bank[k][:, :].bitcast(BF16)
                        for j in range(4):
                            ins = nc.tensor.transpose(dst[:, j * P:(j + 1) * P], src[:, 4 * q + j, :],
                                                      ident_h[:, :])
                        ins.then_inc(mark_turned, 1)
                for n, src in enumerate((above, level, chosen)):
                    flat = src[:, :, :].rearrange("p t e -> p (t e)")
                    if n < 2:
                        pe.wait_ge(mark_ready, 8)
                    else:
                        pe.wait_ge(step, 8)
                    if n != 0:
                        for q in range(4):
                            if n == 2:
                                pe.wait_ge(inside_ready, 4)
                            ins = nc.tensor.matmul(bank[q][:, :], before[:, :], flat[:, 512 * q:512 * q + 512],
                                                   start=True, stop=True)
                            ins.then_inc(inside_done, 1)
                    if n:
                        pe.wait_ge(tiles_ready, START + 4 * n)
                    for q in range(4):
                        nc.tensor.matmul(bank[4 + q][:, :], ones[:, :], flat[:, 512 * q:512 * q + 512],
                                         start=True, stop=True).then_inc(tiles_done, 1)
                pe.wait_ge(tiles_ready, START + 12)
                pe.wait_ge(inside_ready, 8)
                for t in range(NT):
                    pe.wait_ge(a_ready, t + 1)
                    pe.wait_ge(tile_b_ready, t + 1)
                    pe.wait_ge(lane_b_ready, t + 1)
                    for g in range(LISTS):
                        cols = slice(g * EG, (g + 1) * EG)
                        for f, src in enumerate((tile_b, lane_b)):
                            ins = nc.tensor.matmul(
                                bank[g][:, f * P:(f + 1) * P],
                                hot_a[t % 2][:, cols, :].rearrange("p e a -> p (e a)"),
                                src[t % 2][:, cols, :].rearrange("p e b -> p (e b)"),
                                start=(t == 0 and f == 0), stop=(t == NT - 1), skip_group_check=True)
                    ins.then_inc(listed, 1)
                pe.wait_ge(list_loaded, 16)
                nc.tensor.transpose(bank[4][:, 0:E0 * CT], lists_r[:, :], keep.ident[0:E0 * CT, 0:E0 * CT])\
                    .then_inc(list_turned, 1)

            @block.scalar
            def _(act):
                with act.Fori(0, PAIRS) as p:
                    for u in range(2):
                        act.wait_ge(hn_turned[u], START + p + 1)
                        nc.scalar.copy(hnT[u][:, :], bank[u][:, 0:LP]).then_inc(hnT_ready[u], 1)
                act.wait_ge(softmax_step, 2)
                nc.scalar.activation(prob[:, :, :].rearrange("p t e -> p (t e)"),
                                     prob[:, :, :].rearrange("p t e -> p (t e)"), ACT.Exp).then_inc(exp_done, 1)
                for g in range(NG):
                    act.wait_ge(prob_turned, g + 1)
                    nc.scalar.copy(probT[:, g, :], bank[4 + g % 4][:, 0:P]).then_inc(probT_ready, 1)
                for t in range(NT):
                    act.wait_ge(b_ready, t + 1)
                    if t >= 2:
                        act.wait_ge(listed, t - 1)
                    nc.scalar.mul(tile_b[t % 2][:, :, :].rearrange("p e b -> p (e b)"),
                                  hot_b[t % 2][:, :, :].rearrange("p e b -> p (e b)"), float(t))\
                        .then_inc(tile_b_ready, 1)

            @block.vector
            def _(dve):
                with dve.Fori(0, PAIRS) as p:
                    for u in range(2):
                        for t in range(PT):
                            nc.vector.bn_stats(stats[u][:, t, :], keep.h[:, 2 * p + u, t, :])\
                                .then_inc(ln_stats[u], 1)
                        dve.wait_ge(ln_stats[u], PT * (p + 1))
                        stand_alone(dve, dve_seen)
                        for t in range(PT):
                            nc.vector.bn_aggr(mean_var[u][:, t, :], stats[u][:, t, :]).then_inc(ln_var[u], 1)
                    for u in range(2):
                        dve.wait_ge(ln_root[u], p + 1)
                        dve.wait_ge(row_stored[u], START + 16 * p)
                        dve.wait_ge(hn_turned[u], START + p)
                        for t in range(PT):
                            nc.vector.tensor_scalar(hn[u][:, t, :], keep.h[:, 2 * p + u, t, :],
                                                    mean_var[u][:, t, 0:1], rstd[u][:, t:t + 1],
                                                    ALU.subtract, ALU.mult).then_inc(hn_ready[u], 1)
                    for u in range(2):
                        dve.wait_ge(logits_done[u], p + 1)
                        if u == 0:
                            dve.wait_ge(weights, 32)
                        nc.vector.tensor_tensor(
                            prob[:, :, :].rearrange("p (n t) e -> p n t e", t=PT)[:, 2 * p + u, :, :],
                            bank[2 + u][:, 0:PT * E0].rearrange("p (t e) -> p t e", t=PT),
                            b_router[:, :].unsqueeze(1).broadcast_to([P, PT, E0]), ALU.add)\
                            .then_inc(logits_ready[u], 1)
                for u in range(2):
                    dve.wait_ge(logits_ready[u], START + PAIRS)

                def over_experts(x):
                    return x[:, :].unsqueeze(2).broadcast_to([P, NT, E0])

                nc.vector.tensor_reduce(high[:, :], prob[:, :, :], AX.X, ALU.max).then_inc(softmax_step, 1)
                dve.wait_ge(softmax_step, 1)
                nc.vector.tensor_tensor(prob[:, :, :], prob[:, :, :], over_experts(high), ALU.subtract)\
                    .then_inc(softmax_step, 1)
                dve.wait_ge(exp_done, 1)
                nc.vector.tensor_reduce(total[:, :], prob[:, :, :], AX.X, ALU.add).then_inc(softmax_step, 1)
                dve.wait_ge(softmax_step, 3)
                nc.vector.reciprocal(total[:, :], total[:, :]).then_inc(softmax_step, 1)
                dve.wait_ge(softmax_step, 4)
                nc.vector.tensor_tensor(prob[:, :, :], prob[:, :, :], over_experts(total), ALU.mult)\
                    .then_inc(softmax_step, 1)

                nc.vector.memset(least[:, :], 0).then_inc(start_ready, 1)
                nc.vector.memset(bit[:, :], 1 << 29).then_inc(start_ready, 1)
                dve.wait_ge(start_ready, 2)
                dve.wait_ge(probT_ready, NG)
                with dve.Fori(0, 30) as r:
                    dve.wait_ge(least_ready, START + r)
                    dve.wait_ge(bit_ready, START + r)
                    nc.vector.tensor_tensor(tried[:, :], least[:, :], bit[:, :], ALU.bitwise_or)\
                        .then_inc(tried_ready, 1)
                    dve.wait_ge(tried_ready, r + 1)
                    nc.vector.tensor_scalar(hits[:, :], probT[:, :, :].rearrange("p g l -> p (g l)"),
                                            tried[:, :].bitcast(F32), None, ALU.is_ge, ALU.add,
                                            accum_out=count[:, :]).then_inc(counted, 1)
                    dve.wait_ge(summed, r + 1)
                    nc.vector.scalar_tensor_tensor(out=gain[:, :], in0=bank[0][:, 0:1], scalar=float(CAP),
                                                   in1=bit[:, :], op0=ALU.is_ge, op1=ALU.mult)\
                        .then_inc(gained, 1)
                    dve.wait_ge(gained, r + 1)
                    nc.vector.tensor_tensor(least[:, :], least[:, :], gain[:, :], ALU.bitwise_or)\
                        .then_inc(least_ready, 1)
                    nc.vector.tensor_scalar(bit[:, :], bit[:, :], 1, None, ALU.logical_shift_right)\
                        .then_inc(bit_ready, 1)
                dve.wait_ge(least_ready, START + 30)
                limit = least[:, :].bitcast(F32)
                flatT = probT[:, :, :].rearrange("p g l -> p (g l)")
                nc.vector.tensor_scalar(aboveT[:, :, :].rearrange("p g l -> p (g l)"), flatT, limit, None,
                                        ALU.is_gt).then_inc(markT_ready, 1)
                nc.vector.tensor_scalar(levelT[:, :, :].rearrange("p g l -> p (g l)"), flatT, limit, None,
                                        ALU.is_equal).then_inc(markT_ready, 1)
                for n, dst in enumerate((above, level)):
                    for q in range(4):
                        dve.wait_ge(mark_turned, 4 * n + q + 1)
                        nc.vector.tensor_copy(
                            dst[:, 16 * q:16 * q + 16, :].rearrange("p t e -> p (t e)"),
                            bank[4 * n + q][:, :].bitcast(BF16)[:, 0:512]).then_inc(mark_ready, 1)

                def take_tiles(n):
                    for q in range(4):
                        dve.wait_ge(tiles_done, 4 * n + q + 1)
                        nc.vector.tensor_copy(per_tile[:, :, 16 * q:16 * q + 16],
                                              bank[4 + q][:, :].rearrange("p (t e) -> p e t", e=E0))\
                            .then_inc(tiles_ready, 1)

                def take_inside(n):
                    for q in range(4):
                        dve.wait_ge(inside_done, 4 * n + q + 1)
                        nc.vector.tensor_copy(inside[:, 16 * q:16 * q + 16, :].rearrange("p t e -> p (t e)"),
                                              bank[q][:, :]).then_inc(inside_ready, 1)

                def flat(x):
                    return x[:, :, :].rearrange("p a b -> p (a b)")

                def scan():
                    nc.vector.tensor_tensor_scan(flat(upto), flat(not_first), flat(per_tile), 0.0, ALU.mult,
                                                 ALU.add).then_inc(step, 1)

                by_tile = upto[:, :, :].rearrange("p e t -> p t e")
                take_tiles(0)
                dve.wait_ge(tiles_ready, START + 4)
                dve.wait_ge(cast, CASTS)
                scan()
                dve.wait_ge(step, 1)
                nc.vector.tensor_scalar(wanted[:, :], upto[:, :, NT - 1], -1.0, float(CAP), ALU.mult, ALU.add)\
                    .then_inc(step, 1)
                take_inside(0)
                take_tiles(1)
                dve.wait_ge(tiles_ready, START + 8)
                dve.wait_ge(step, 2)
                scan()
                dve.wait_ge(step, 3)
                nc.vector.tensor_tensor(flat(upto), flat(upto), flat(per_tile), ALU.subtract).then_inc(step, 1)
                dve.wait_ge(step, 4)
                dve.wait_ge(inside_ready, 4)
                nc.vector.tensor_tensor(inside[:, :, :], inside[:, :, :], by_tile, ALU.add).then_inc(step, 1)
                dve.wait_ge(step, 5)
                nc.vector.tensor_tensor(inside[:, :, :], inside[:, :, :],
                                        wanted[:, :].unsqueeze(1).broadcast_to([P, NT, E0]), ALU.is_lt)\
                    .then_inc(step, 1)
                dve.wait_ge(step, 6)
                nc.vector.tensor_tensor(flat(chosen), flat(inside), flat(level), ALU.mult).then_inc(step, 1)
                dve.wait_ge(step, 7)
                nc.vector.tensor_tensor(flat(chosen), flat(chosen), flat(above), ALU.add).then_inc(step, 1)
                take_inside(1)
                take_tiles(2)
                dve.wait_ge(tiles_ready, START + 12)
                scan()
                dve.wait_ge(step, 9)
                nc.vector.tensor_tensor(flat(upto), flat(upto), flat(per_tile), ALU.subtract).then_inc(step, 1)
                dve.wait_ge(step, 10)
                dve.wait_ge(inside_ready, 8)
                nc.vector.tensor_tensor(inside[:, :, :], inside[:, :, :], by_tile, ALU.add).then_inc(step, 1)
                dve.wait_ge(step, 11)
                nc.vector.scalar_tensor_tensor(out=flat(inside), in0=flat(chosen), scalar=-4096.0,
                                               in1=flat(inside), op0=ALU.mult, op1=ALU.add).then_inc(step, 1)
                dve.wait_ge(step, 12)
                nc.vector.tensor_scalar(flat(pos_i), flat(inside), 4096.0, None, ALU.add).then_inc(step, 1)
                dve.wait_ge(step, 13)
                nc.vector.tensor_scalar(flat(digit_i), flat(pos_i), 4, None, ALU.logical_shift_right)\
                    .then_inc(step, 1)
                dve.wait_ge(step, 14)
                nc.vector.tensor_copy(flat(digit_a), flat(digit_i)).then_inc(step, 1)
                dve.wait_ge(step, 15)
                nc.vector.tensor_scalar(flat(digit_i), flat(pos_i), DIGIT - 1, None, ALU.bitwise_and)\
                    .then_inc(step, 1)
                dve.wait_ge(step, 16)
                nc.vector.tensor_copy(flat(digit_b), flat(digit_i)).then_inc(step, 1)
                dve.wait_ge(step, 17)
                for t in range(NT):
                    if t >= 2:
                        dve.wait_ge(listed, t - 1)
                        dve.wait_ge(tile_b_ready, t - 1)
                    every = digits[:, :].unsqueeze(1).broadcast_to([P, E0, DIGIT])
                    nc.vector.tensor_tensor(hot_b[t % 2][:, :, :], every,
                                            digit_b[:, t, :].unsqueeze(2).broadcast_to([P, E0, DIGIT]),
                                            ALU.is_equal).then_inc(b_ready, 1)
                    nc.vector.tensor_tensor(hot_a[t % 2][:, :, :], every,
                                            digit_a[:, t, :].unsqueeze(2).broadcast_to([P, E0, DIGIT]),
                                            ALU.is_equal).then_inc(a_ready, 1)
                    dve.wait_ge(b_ready, t + 1)
                    nc.vector.tensor_scalar(flat(lane_b[t % 2]), flat(hot_b[t % 2]), lane[:, 0:1], None,
                                            ALU.mult).then_inc(lane_b_ready, 1)
                dve.wait_ge(listed, NT)
                for g in range(LISTS):
                    for f in range(2):
                        block_f = bank[g][:, f * P:(f + 1) * P].rearrange("p (e b) -> p e b", e=EG)
                        if g or f:
                            dve.wait_ge(half_ready, 2 * g + f)
                        nc.vector.tensor_tensor(picked[:, :, :], block_f,
                                                own_list[:, :].unsqueeze(2).broadcast_to([P, EG, DIGIT]),
                                                ALU.mult).then_inc(list_step, 1)
                        dve.wait_ge(list_step, 2 * g + f + 1)
                        nc.vector.tensor_reduce(half[:, g, f, :], picked[:, :, :].rearrange("p e b -> p b e"),
                                                AX.X, ALU.add).then_inc(half_ready, 1)
                    dve.wait_ge(half_ready, 2 * g + 2)
                    nc.vector.scalar_tensor_tensor(out=lists[:, g, :], in0=half[:, g, 0, :], scalar=float(P),
                                                   in1=half[:, g, 1, :], op0=ALU.mult, op1=ALU.add)\
                        .then_inc(lists_ready, 1)
                dve.wait_ge(list_turned, 1)
                nc.vector.tensor_copy(keep.tokens[:, 0:E0 * CT], bank[4][:, 0:E0 * CT]).then_inc(tokens_ready, 1)
        nc.clear_and_free_semaphores(sems)
        nc.all_engine_barrier()


GROUP = 4
F0 = 341
CHUNKS = [(c * P, min(P, F0 - c * P)) for c in range(-(-F0 // P))]


def experts(nc, dram, keep):
    sems = []
    with ExitStack() as ctx:
        def sb(name, shape, dt=F32):
            return ctx.enter_context(nc.sbuf_tensor("e_" + name, shape, dt))

        def two(name, shape, dt=F32):
            return [sb(f"{name}{u}", shape, dt) for u in range(2)]

        def sem(name):
            sems.append(nc.alloc_semaphore("e_" + name))
            return sems[-1]

        def sem2(name):
            return [sem(f"{name}{u}") for u in range(2)]

        NCH = len(CHUNKS)
        w_up = two("w_up", [P, F0])
        b_up = sb("b_up", [P, NCH, E0 // GROUP])
        w_down = two("w_down", [P, NCH, D])
        b_down = two("b_down", [1, D])
        ones = sb("ones", [1, P])
        zeros = sb("zeros", [P, PT * D])
        token_col = two("token_col", [P, CT], I32)
        rows = two("rows", [P, CT, ROW])
        xT = two("xT", [P, CAP])
        bias = two("bias", [P, NCH])
        hidden = two("hidden", [P, NCH, CAP])
        y = two("y", [P, CT, D])
        add_up = two("add_up", [P, PT, D])

        bank = [[ctx.enter_context(nc.psum_tensor(f"e_bank{u}{k}", [P, 512], F32)) for k in range(4)]
                for u in range(2)]

        weights = sem("weights")
        const = sem("const")
        pool_seen = sem("pool_seen")
        dve_seen = sem("dve_seen")
        h_stored, zero_stored = sem("h_stored"), sem("zero_stored")
        col_ready, gathered, w_loaded, turned, xT_ready, up_done, hidden_ready = map(
            sem2, ("col_ready", "gathered", "w_loaded", "turned", "xT_ready", "up_done", "hidden_ready"))
        down_done, y_ready, scattered, bias_ready = map(sem2, ("down_done", "y_ready", "scattered", "bias_ready"))
        added_loaded, added = sem2("added_loaded"), sem2("added")

        tokens = keep.tokens[:, :].rearrange("p (e j) -> p e j", j=CT)
        sum_d = [dram[f"sum{u}"].rearrange("(n t p) d -> n p t d", t=PT, p=P) for u in range(2)]
        up_d = dram["W_up"]
        down_d = dram["W_down"]

        start_counts(nc, [*down_done, *added, *y_ready, *hidden_ready])

        with nc.Block() as block:
            @block.sync
            def _(sp):
                for c, (lo, n) in enumerate(CHUNKS):
                    sp.dma_start(b_up[0:n, c, :], dram["b_upT"][lo:lo + n, :]).then_inc(weights, 16)
                sp.wait_ge(const, 2)
                with sp.Fori(0, B) as b:
                    sp.dma_start(sum_d[0][b], keep.h[:, b, :, :]).then_inc(h_stored, 16)
                    sp.dma_start(sum_d[1][b], zeros[:, :].rearrange("p (t d) -> p t d", t=PT))\
                        .then_inc(zero_stored, 16)
                with sp.Fori(0, E0 // 2) as p:
                    for u in range(2):
                        sp.wait_ge(down_done[u], START + p)
                        sp.dma_start(w_up[u][:, :], up_d[p // (GROUP // 2)]).then_inc(w_loaded[u], 16)
                        for c, (lo, n) in enumerate(CHUNKS):
                            sp.dma_start(w_down[u][0:n, c, :], down_d[2 * p + u, lo:lo + n, :])\
                                .then_inc(w_loaded[u], 16)
                        sp.dma_start(b_down[u][:, :], dram["b_down"][bass.ds(2 * p + u, 1), :])\
                            .then_inc(w_loaded[u], 16)
                for u in range(2):
                    sp.wait_ge(scattered[u], 16 * CT * (E0 // 2))
                with sp.Fori(0, PAIRS) as p:
                    for u in range(2):
                        sp.wait_ge(added[u], START + p)
                        sp.dma_start(keep.h[:, 2 * p + u, :, :], sum_d[0][2 * p + u]).then_inc(added_loaded[u], 16)
                        sp.dma_start(add_up[u][:, :, :], sum_d[1][2 * p + u]).then_inc(added_loaded[u], 16)

            @block.gpsimd
            def _(pool):
                nc.gpsimd.memset(ones[:, :], 1.0).then_inc(const, 1)
                nc.gpsimd.memset(zeros[:, :], 0.0).then_inc(const, 1)
                for u in range(2):
                    nc.gpsimd.tensor_copy(token_col[u][:, :], tokens[:, u, :]).then_inc(col_ready[u], 1)

                def gather(u):
                    for j in range(CT):
                        pool.indirect_dma_start(
                            out=rows[u][:, j, :], out_offset=None, in_=dram["token_rows"],
                            in_offset=bass.IndirectOffsetOnAxis(ap=token_col[u][:, j:j + 1], axis=0),
                        ).then_inc(gathered[u], 16)

                for u in range(2):
                    pool.wait_ge(col_ready[u], 1)
                    gather(u)
                pool.wait_ge(h_stored, 16 * B)
                pool.wait_ge(zero_stored, 16 * B)
                with pool.Fori(0, E0 // 2) as p:
                    for u in range(2):
                        pool.wait_ge(y_ready[u], START + CT * (p + 1))
                        stand_alone(pool, pool_seen)
                        for j in range(CT):
                            pool.indirect_dma_start(
                                out=dram[f"sum{u}"],
                                out_offset=bass.IndirectOffsetOnAxis(ap=token_col[u][:, j:j + 1], axis=0),
                                in_=y[u][:, j, :], in_offset=None, compute_op=ALU.add,
                            ).then_inc(scattered[u], 16)
                        pool.wait_ge(scattered[u], 16 * CT * (p + 1))
                        nc.gpsimd.tensor_copy(token_col[u][:, :], tokens[:, 2 * p + 2 + u, :])\
                            .then_inc(col_ready[u], 1)
                        pool.wait_ge(col_ready[u], p + 2)
                        stand_alone(pool, pool_seen)
                        gather(u)
                for u in range(2):
                    pool.wait_ge(gathered[u], 16 * CT * (E0 // 2 + 1))

            @block.tensor
            def _(pe):
                pe.wait_ge(const, 2)
                with pe.Fori(0, E0 // 2) as p:
                    for u in range(2):
                        pe.wait_ge(gathered[u], 16 * CT * (p + 1))
                        for j in range(CT):
                            ins = nc.tensor.transpose(bank[u][0][:, j * P:(j + 1) * P], rows[u][:, j, 0:D],
                                                      keep.ident[:, :])
                        ins.then_inc(turned[u], 1)
                    for u in range(2):
                        pe.wait_ge(xT_ready[u], p + 1)
                        pe.wait_ge(w_loaded[u], 16 * (NCH + 2) * (p + 1))
                        for c, (lo, n) in enumerate(CHUNKS):
                            dst = bank[u][1 + c // 2][0:n, (c % 2) * CAP:(c % 2 + 1) * CAP]
                            ins = nc.tensor.matmul(dst, w_up[u][:, lo:lo + n], xT[u][:, :], start=True, stop=True)
                        ins.then_inc(up_done[u], 1)
                    for u in range(2):
                        pe.wait_ge(hidden_ready[u], START + NCH * (p + 1))
                        pe.wait_ge(y_ready[u], START + CT * p)
                        for j in range(CT):
                            dst = bank[u][3][:, j * P:(j + 1) * P]
                            for c, (lo, n) in enumerate(CHUNKS):
                                nc.tensor.matmul(dst, hidden[u][0:n, c, j * P:(j + 1) * P], w_down[u][0:n, c, :],
                                                 start=(c == 0), stop=False)
                            ins = nc.tensor.matmul(dst, ones[:, :], b_down[u][:, :], start=False, stop=True)
                        ins.then_inc(down_done[u], 1)

            @block.scalar
            def _(act):
                act.wait_ge(weights, 16 * NCH)
                with act.Fori(0, E0 // 2) as p:
                    for u in range(2):
                        act.wait_ge(up_done[u], p + 1)
                        act.wait_ge(bias_ready[u], p + 1)
                        for c, (lo, n) in enumerate(CHUNKS):
                            src = bank[u][1 + c // 2][0:n, (c % 2) * CAP:(c % 2 + 1) * CAP]
                            nc.scalar.activation(hidden[u][0:n, c, :], src, ACT.Silu, bias=bias[u][0:n, c:c + 1])\
                                .then_inc(hidden_ready[u], 1)

            @block.vector
            def _(dve):
                dve.wait_ge(weights, 16 * NCH)
                with dve.Fori(0, E0 // 2) as p:
                    for u in range(2):
                        dve.wait_ge(hidden_ready[u], START + NCH * p)
                        stand_alone(dve, dve_seen)
                        for c, (lo, n) in enumerate(CHUNKS):
                            ins = nc.vector.tensor_copy(bias[u][0:n, c:c + 1],
                                                        b_up[0:n, c, bass.ds(p // (GROUP // 2), 1)])
                        ins.then_inc(bias_ready[u], 1)
                        dve.wait_ge(turned[u], p + 1)
                        nc.vector.tensor_copy(xT[u][:, :], bank[u][0][:, 0:CAP]).then_inc(xT_ready[u], 1)
                    for u in range(2):
                        dve.wait_ge(down_done[u], START + p + 1)
                        dve.wait_ge(col_ready[u], p + 1)
                        for j in range(CT):
                            nc.vector.tensor_scalar(y[u][:, j, :], bank[u][3][:, j * P:(j + 1) * P],
                                                    rows[u][:, j, bass.ds(2 * p + (D + u), 1)], None, ALU.mult)\
                                .then_inc(y_ready[u], 1)
                with dve.Fori(0, PAIRS) as p:
                    for u in range(2):
                        dve.wait_ge(added_loaded[u], 32 * (p + 1))
                        nc.vector.tensor_tensor(keep.h[:, 2 * p + u, :, :], keep.h[:, 2 * p + u, :, :],
                                                add_up[u][:, :, :], ALU.add).then_inc(added[u], 1)
        nc.clear_and_free_semaphores(sems)
        nc.all_engine_barrier()


LEVELS = 7


def delta_rule(nc, dram, keep):
    sems = []
    with ExitStack() as ctx:
        def sb(name, shape, dt=F32):
            return ctx.enter_context(nc.sbuf_tensor("d_" + name, shape, dt))

        def two(name, shape, dt=F32):
            return [sb(f"{name}{u}", shape, dt) for u in range(2)]

        def sem(name):
            sems.append(nc.alloc_semaphore("d_" + name))
            return sems[-1]

        def sem2(name):
            return [sem(f"{name}{u}") for u in range(2)]

        wT = sb("wT", [P, D])
        eta = sb("eta", [P, 1])
        minus_eta = sb("minus_eta", [P, 1])
        lam = sb("lam", [P, 1])
        gain = sb("gain", [P, D])
        shift = sb("shift", [P, D])
        half_neg = sb("half_neg", [P, PT])
        eps = sb("eps", [P, PT])
        spike = sb("spike", [P, LP])
        decay = sb("decay", [P, LP])
        decay_low = sb("decay_low", [P, P])
        own_i = sb("own_i", [P, P], I32)
        other_i = sb("other_i", [P, P], I32)
        level_i = sb("level_i", [P, P], I32)
        level_mask = sb("level_mask", [P, LEVELS, P])
        low = sb("low", [P, LEVELS - 1, P])
        first = sb("first", [P, 2, P])
        unit2 = sb("unit2", [P, 2, P])

        stats = two("stats", [P, PT, 6])
        mean_var = two("mean_var", [P, PT, 2])
        rstd = two("rstd", [P, PT])
        offset = two("offset", [P, PT])
        k_sb = two("k", [P, PT, D])
        kT = two("kT", [P, LP])
        v_sb = two("v", [P, PT, D])
        eta_v = two("eta_v", [P, PT, D])
        gT0 = two("gT0", [P, LP])
        gT1 = two("gT1", [P, P])
        g_low = two("g_low", [P, PT, LEVELS - 1, P])
        g_first = two("g_first", [P, PT, 2, P])
        inv = two("inv", [P, PT, 2, P])
        mid = two("mid", [P, PT, P])
        rest = two("rest", [P, D])
        err = two("err", [P, PT, D])
        y = two("y", [P, PT, D])
        h_shift = two("h_shift", [P, PT, D])

        bank = [[ctx.enter_context(nc.psum_tensor(f"d_bank{u}{k}", [P, 512], F32)) for k in range(4)]
                for u in range(2)]

        weights = sem("weights")
        const = sem("const")
        dve_seen = sem("dve_seen")
        pool_seen = sem("pool_seen")
        lam_ready, decay_ready, decay_turned, low_ready, set_up, level_ready = map(
            sem, ("lam_ready", "decay_ready", "decay_turned", "low_ready", "set_up", "level_ready"))
        ln_stats, ln_var, ln_eps, ln_root, offset_ready, k_ready = map(
            sem2, ("ln_stats", "ln_var", "ln_eps", "ln_root", "offset_ready", "k_ready"))
        k_turned, kT_ready, v_done, gram_done, v_ready, eta_v_ready = map(
            sem2, ("k_turned", "kT_ready", "v_done", "gram_done", "v_ready", "eta_v_ready"))
        gram_ready, first_ready, inv_ready, mid_done, mid_ready, inv_done = map(
            sem2, ("gram_ready", "first_ready", "inv_ready", "mid_done", "mid_ready", "inv_done"))
        err_done, err_ready, before_done, rest_ready, o_done, y_ready = map(
            sem2, ("err_done", "err_ready", "before_done", "rest_ready", "o_done", "y_ready"))
        normed, gained, shifted, h_ready = map(sem2, ("normed", "gained", "shifted", "h_ready"))

        loads = [(wT[:, :], dram["WT"]), (eta[:, :], dram["eta"].partition_broadcast(P)),
                 (lam[:, :], dram["lam_logit"].partition_broadcast(P)),
                 (gain[:, :], dram["ln_gamma"].partition_broadcast(P)),
                 (shift[:, :], dram["ln_beta"].partition_broadcast(P))]
        ALL_WEIGHTS = 16 * len(loads)
        CONSTS = 6
        GRAM = 4

        start_counts(nc, [*err_ready, *y_ready, *k_turned, *h_ready])

        with nc.Block() as block:
            @block.sync
            def _(sp):
                for dst, src in loads:
                    sp.dma_start(dst, src).then_inc(weights, 16)
                sp.wait_ge(weights, ALL_WEIGHTS)

            @block.gpsimd
            def _(pool):
                nc.gpsimd.memset(half_neg[:, :], -0.5).then_inc(const, 1)
                nc.gpsimd.memset(eps[:, :], LN_EPS).then_inc(const, 1)
                nc.gpsimd.memset(spike[:, P:], 0.0).then_inc(const, 1)
                nc.gpsimd.tensor_copy(spike[:, 0:P], keep.ident[:, :]).then_inc(const, 1)
                nc.gpsimd.iota(own_i[:, :], pattern=[[0, P]], base=0, channel_multiplier=1).then_inc(const, 1)
                nc.gpsimd.iota(other_i[:, :], pattern=[[1, P]], base=0, channel_multiplier=0)\
                    .then_inc(const, 1)
                with pool.Fori(0, PAIRS) as p:
                    for n in range(2):
                        for u in range(2):
                            pool.wait_ge(ln_var[u], PT * (2 * p + n + 1))
                            nc.gpsimd.tensor_tensor(rstd[u][:, :], mean_var[u][:, :, 1], eps[:, :],
                                                    ALU.add).then_inc(ln_eps[u], 1)
                            pool.wait_ge(ln_eps[u], 2 * p + n + 1)
                            nc.gpsimd.tensor_tensor(rstd[u][:, :], rstd[u][:, :], half_neg[:, :],
                                                    ALU.pow).then_inc(ln_root[u], 1)
                        if n == 0:
                            for u in range(2):
                                nc.gpsimd.tensor_tensor(h_shift[u][:, :, :], keep.h[:, 2 * p + u, :, :],
                                                        shift[:, :].unsqueeze(1).broadcast_to([P, PT, D]),
                                                        ALU.add).then_inc(shifted[u], 1)
                    for u in range(2):
                        pool.wait_ge(normed[u], PT * (p + 1))
                        nc.gpsimd.tensor_tensor(y[u][:, :, :], y[u][:, :, :],
                                                gain[:, :].unsqueeze(1).broadcast_to([P, PT, D]),
                                                ALU.mult).then_inc(gained[u], 1)
                        pool.wait_ge(gained[u], p + 1)
                        pool.wait_ge(shifted[u], p + 1)
                        stand_alone(pool, pool_seen)
                        nc.gpsimd.tensor_tensor(keep.h[:, 2 * p + u, :, :], y[u][:, :, :], h_shift[u][:, :, :],
                                                ALU.add).then_inc(h_ready[u], 1)

            @block.tensor
            def _(pe):
                pe.wait_ge(decay_ready, 1)
                nc.tensor.transpose(bank[0][0][:, 0:P], decay[:, 0:P], keep.ident[:, :]).then_inc(decay_turned, 1)
                pe.wait_ge(low_ready, 1)
                pe.wait_ge(weights, ALL_WEIGHTS)
                with pe.Fori(0, PAIRS) as p:
                    for u in range(2):
                        pe.wait_ge(k_ready[u], PT * (p + 1))
                        pe.wait_ge(err_ready[u], START + PT * p)
                        for t in range(PT):
                            ins = nc.tensor.transpose(bank[u][0][:, t * P:(t + 1) * P], k_sb[u][:, t, :],
                                                      keep.ident[:, :])
                        ins.then_inc(k_turned[u], 1)
                    for u in range(2):
                        pe.wait_ge(kT_ready[u], p + 1)
                        tile = [kT[u][:, t * P:(t + 1) * P] for t in range(PT)]
                        nc.tensor.matmul(bank[u][2][:, 0:LP], tile[0], kT[u][:, :], start=True, stop=True)
                        nc.tensor.matmul(bank[u][2][:, LP:LP + P], tile[1], tile[1], start=True, stop=True)\
                            .then_inc(gram_done[u], 1)
                        pe.wait_ge(y_ready[u], START + p)
                        for t in range(PT):
                            ins = nc.tensor.matmul(bank[u][3][:, t * D:(t + 1) * D], tile[t], wT[:, :], start=True,
                                                   stop=True)
                        ins.then_inc(v_done[u], 1)
                    for l in range(1, LEVELS):
                        for u in range(2):
                            pe.wait_ge(inv_ready[u], LEVELS * p + l)
                            for t in range(PT):
                                ins = nc.tensor.matmul(bank[u][0][:, t * P:(t + 1) * P],
                                                       g_low[u][:, t, l - 1, :], inv[u][:, t, 0, :], start=True,
                                                       stop=True)
                            ins.then_inc(mid_done[u], 1)
                        for u in range(2):
                            pe.wait_ge(mid_ready[u], (LEVELS - 1) * p + l)
                            for t in range(PT):
                                lo = 2 * t * P
                                ins = nc.tensor.matmul(bank[u][1][:, lo:lo + P], inv[u][:, t, 1, :],
                                                       mid[u][:, t, :], start=True, stop=True)
                                if l < LEVELS - 1:
                                    ins = nc.tensor.matmul(bank[u][1][:, lo + P:lo + 2 * P], mid[u][:, t, :],
                                                           inv[u][:, t, 1, :], start=True, stop=True)
                            ins.then_inc(inv_done[u], 1)
                    for u in range(2):
                        pe.wait_ge(inv_ready[u], LEVELS * (p + 1))
                        pe.wait_ge(eta_v_ready[u], p + 1)
                        nc.tensor.matmul(bank[u][0][:, 0:D], inv[u][:, 0, 0, :], eta_v[u][:, 0, :], start=True,
                                         stop=True).then_inc(err_done[u], 1)
                    for u in range(2):
                        pe.wait_ge(err_ready[u], START + PT * p + 1)
                        pe.wait_ge(gram_ready[u], GRAM * (p + 1))
                        nc.tensor.matmul(bank[u][2][:, 0:D], gT0[u][:, P:], err[u][:, 0, :], start=True, stop=True)\
                            .then_inc(before_done[u], 1)
                        nc.tensor.matmul(bank[u][3][:, 0:D], gT0[u][:, 0:P], err[u][:, 0, :], start=True, stop=True)
                    for u in range(2):
                        pe.wait_ge(rest_ready[u], p + 1)
                        nc.tensor.matmul(bank[u][0][:, D:2 * D], inv[u][:, 1, 0, :], rest[u][:, :], start=True,
                                         stop=True).then_inc(err_done[u], 1)
                    for u in range(2):
                        pe.wait_ge(err_ready[u], START + PT * (p + 1))
                        nc.tensor.matmul(bank[u][3][:, D:2 * D], gT0[u][:, P:], err[u][:, 0, :], start=True,
                                         stop=False)
                        nc.tensor.matmul(bank[u][3][:, D:2 * D], gT1[u][:, :], err[u][:, 1, :], start=False,
                                         stop=True).then_inc(o_done[u], 1)

            @block.scalar
            def _(act):
                act.wait_ge(weights, ALL_WEIGHTS)
                nc.scalar.activation(lam[:, :], lam[:, :], ACT.Sigmoid).then_inc(lam_ready, 1)
                with act.Fori(0, PAIRS) as p:
                    for u in range(2):
                        act.wait_ge(offset_ready[u], p + 1)
                        act.wait_ge(k_turned[u], START + p)
                        for t in range(PT):
                            nc.scalar.activation(k_sb[u][:, t, :], keep.h[:, 2 * p + u, t, :], ACT.Tanh,
                                                 bias=offset[u][:, t:t + 1], scale=rstd[u][:, t:t + 1])\
                                .then_inc(k_ready[u], 1)
                    for u in range(2):
                        act.wait_ge(k_turned[u], START + p + 1)
                        nc.scalar.copy(kT[u][:, :], bank[u][0][:, 0:LP]).then_inc(kT_ready[u], 1)
                    for u in range(2):
                        act.wait_ge(v_done[u], p + 1)
                        nc.scalar.copy(v_sb[u][:, :, :].rearrange("p t d -> p (t d)"),
                                       bank[u][3][:, 0:PT * D]).then_inc(v_ready[u], 1)
                    for l in range(1, LEVELS):
                        for u in range(2):
                            act.wait_ge(mid_done[u], (LEVELS - 1) * p + l)
                            nc.scalar.copy(mid[u][:, :, :].rearrange("p t d -> p (t d)"),
                                           bank[u][0][:, 0:PT * P]).then_inc(mid_ready[u], 1)
                    for t in range(PT):
                        for u in range(2):
                            act.wait_ge(err_done[u], PT * p + t + 1)
                            nc.scalar.copy(err[u][:, t, :], bank[u][0][:, t * D:(t + 1) * D])\
                                .then_inc(err_ready[u], 1)

            @block.vector
            def _(dve):
                dve.wait_ge(const, CONSTS)
                dve.wait_ge(lam_ready, 1)
                nc.vector.tensor_tensor_scan(decay[:, :], lam[:, 0:1].broadcast_to([P, LP]), spike[:, :], 0.0,
                                             ALU.mult, ALU.add).then_inc(decay_ready, 1)
                nc.vector.tensor_tensor(own_i[:, :], own_i[:, :], other_i[:, :], ALU.bitwise_xor)\
                    .then_inc(level_ready, 1)
                dve.wait_ge(level_ready, 1)
                for l in range(LEVELS):
                    nc.vector.tensor_scalar(level_i[:, :], own_i[:, :], l, None, ALU.logical_shift_right)\
                        .then_inc(level_ready, 1)
                    dve.wait_ge(level_ready, 2 * l + 2)
                    nc.vector.tensor_scalar(level_mask[:, l, :], level_i[:, :], 1.0, None, ALU.is_equal)\
                        .then_inc(level_ready, 1)
                    dve.wait_ge(level_ready, 2 * l + 3)
                dve.wait_ge(decay_turned, 1)
                nc.vector.tensor_copy(decay_low[:, :], bank[0][0][:, 0:P]).then_inc(low_ready, 1)
                dve.wait_ge(low_ready, 1)
                nc.vector.tensor_scalar(minus_eta[:, :], eta[:, :], -1.0, None, ALU.mult).then_inc(set_up, 1)
                nc.vector.scalar_tensor_tensor(
                    out=low[:, :, :], in0=level_mask[:, 1:, :], scalar=eta[:, 0:1],
                    in1=decay_low[:, :].unsqueeze(1).broadcast_to([P, LEVELS - 1, P]), op0=ALU.mult,
                    op1=ALU.mult).then_inc(set_up, 1)
                nc.vector.scalar_tensor_tensor(out=first[:, 0, :], in0=level_mask[:, 0, :], scalar=eta[:, 0:1],
                                               in1=decay[:, 0:P], op0=ALU.mult, op1=ALU.mult).then_inc(set_up, 1)
                nc.vector.scalar_tensor_tensor(out=first[:, 1, :], in0=level_mask[:, 0, :], scalar=eta[:, 0:1],
                                               in1=decay_low[:, :], op0=ALU.mult, op1=ALU.mult)\
                    .then_inc(set_up, 1)
                nc.vector.tensor_copy(unit2[:, :, :], keep.ident[:, :].unsqueeze(1).broadcast_to([P, 2, P]))\
                    .then_inc(set_up, 1)
                dve.wait_ge(set_up, 5)
                dve.wait_ge(weights, ALL_WEIGHTS)

                def layer_norm(u, n, src):
                    for t in range(PT):
                        nc.vector.bn_stats(stats[u][:, t, :], src(t)).then_inc(ln_stats[u], 1)
                    dve.wait_ge(ln_stats[u], PT * (n + 1))
                    stand_alone(dve, dve_seen)
                    for t in range(PT):
                        nc.vector.bn_aggr(mean_var[u][:, t, :], stats[u][:, t, :]).then_inc(ln_var[u], 1)

                with dve.Fori(0, PAIRS) as p:
                    for u in range(2):
                        layer_norm(u, 2 * p, lambda t: keep.h[:, 2 * p + u, t, :])
                    for u in range(2):
                        dve.wait_ge(ln_root[u], 2 * p + 1)
                        nc.vector.scalar_tensor_tensor(out=offset[u][:, :], in0=mean_var[u][:, :, 0], scalar=-1.0,
                                                       in1=rstd[u][:, :], op0=ALU.mult, op1=ALU.mult)\
                            .then_inc(offset_ready[u], 1)
                    for u in range(2):
                        dve.wait_ge(gram_done[u], p + 1)
                        own = [bank[u][2][:, 0:P], bank[u][2][:, LP:LP + P]]
                        for t in range(PT):
                            nc.vector.tensor_tensor(g_first[u][:, t, :, :],
                                                    own[t].unsqueeze(1).broadcast_to([P, 2, P]), first[:, :, :],
                                                    ALU.mult).then_inc(first_ready[u], 1)
                        dve.wait_ge(first_ready[u], PT * (p + 1))
                        for t in range(PT):
                            ins = nc.vector.tensor_tensor(inv[u][:, t, :, :], unit2[:, :, :],
                                                          g_first[u][:, t, :, :], ALU.subtract)
                        for t in range(PT):
                            nc.vector.tensor_tensor(g_low[u][:, t, :, :],
                                                    own[t].unsqueeze(1).broadcast_to([P, LEVELS - 1, P]),
                                                    low[:, :, :], ALU.mult).then_inc(gram_ready[u], 1)
                        dve.wait_ge(gram_ready[u], GRAM * p + 2)
                        nc.vector.tensor_tensor(gT0[u][:, :], bank[u][2][:, 0:LP], decay[:, :], ALU.mult)\
                            .then_inc(gram_ready[u], 1)
                        nc.vector.tensor_tensor(gT1[u][:, :], own[1], decay[:, 0:P], ALU.mult)\
                            .then_inc(gram_ready[u], 1)
                        dve.wait_ge(gram_ready[u], GRAM * (p + 1))
                        dve.sem_inc(inv_ready[u], 1)
                    for u in range(2):
                        dve.wait_ge(v_ready[u], p + 1)
                        nc.vector.tensor_scalar(eta_v[u][:, :, :], v_sb[u][:, :, :], eta[:, 0:1], None, ALU.mult)\
                            .then_inc(eta_v_ready[u], 1)
                    for l in range(1, LEVELS):
                        for u in range(2):
                            dve.wait_ge(inv_done[u], (LEVELS - 1) * p + l)
                            done = bank[u][1][:, :].rearrange("p (t i c) -> p t i c", t=PT, i=2)
                            if l < LEVELS - 1:
                                nc.vector.tensor_tensor(inv[u][:, :, :, :], inv[u][:, :, :, :], done,
                                                        ALU.subtract).then_inc(inv_ready[u], 1)
                            else:
                                nc.vector.tensor_tensor(inv[u][:, :, 0, :], inv[u][:, :, 0, :], done[:, :, 0, :],
                                                        ALU.subtract).then_inc(inv_ready[u], 1)
                    for u in range(2):
                        dve.wait_ge(before_done[u], p + 1)
                        nc.vector.scalar_tensor_tensor(out=rest[u][:, :], in0=bank[u][2][:, 0:D],
                                                       scalar=minus_eta[:, 0:1], in1=eta_v[u][:, 1, :],
                                                       op0=ALU.mult, op1=ALU.add).then_inc(rest_ready[u], 1)
                    for u in range(2):
                        dve.wait_ge(o_done[u], p + 1)
                        dve.wait_ge(h_ready[u], START + p)
                        nc.vector.tensor_tensor(y[u][:, :, :],
                                                bank[u][3][:, 0:PT * D].rearrange("p (t d) -> p t d", t=PT),
                                                v_sb[u][:, :, :], ALU.add).then_inc(y_ready[u], 1)
                    for u in range(2):
                        dve.wait_ge(y_ready[u], START + p + 1)
                        layer_norm(u, 2 * p + 1, lambda t: y[u][:, t, :])
                    for u in range(2):
                        dve.wait_ge(ln_root[u], 2 * p + 2)
                        for t in range(PT):
                            nc.vector.tensor_scalar(y[u][:, t, :], y[u][:, t, :], mean_var[u][:, t, 0:1],
                                                    rstd[u][:, t:t + 1], ALU.subtract, ALU.mult)\
                                .then_inc(normed[u], 1)
        nc.clear_and_free_semaphores(sems)
        nc.all_engine_barrier()


F32R = mybir.dt.float32r
E1 = 64
TOP_K = 6
LEAST = -3.0e38
HIGH_BITS = -4096
GT = 4
GROUP_TOKENS = GT * P
GROUPS1 = B * LP // GROUP_TOKENS
ROUTED = E1 * 64 // P
SHARED = 256 // P
CH = ROUTED + SHARED


def expert_ffn(nc, dram, keep):
    sems = []
    with ExitStack() as ctx:
        def sb(name, shape, dt=F32):
            return ctx.enter_context(nc.sbuf_tensor("f_" + name, shape, dt))

        def two(name, shape, dt=F32):
            return [sb(f"{name}{u}", shape, dt) for u in range(2)]

        def sem(name):
            sems.append(nc.alloc_semaphore("f_" + name))
            return sems[-1]

        w1 = [sb("w1_hi", [P, CH, P], F32R), sb("w1_lo", [P, CH, P], F32R)]
        w3 = [sb("w3_hi", [P, CH, P], F32R), sb("w3_lo", [P, CH, P], F32R)]
        w2 = sb("w2", [P, CH, D])
        gate = sb("gate", [P, E1])
        spread = sb("spread", [P, ROUTED, P], F32R)
        half_neg = sb("half_neg", [P, GT])
        eps = sb("eps", [P, GT])

        own_i = sb("own_i", [P, 1], I32)
        own = sb("own", [P, 1])
        expert_i = sb("expert_i", [P, E1], I32)
        expert = sb("expert", [P, E1])

        stats = sb("stats", [P, GT, 6])
        mean_var = sb("mean_var", [P, GT, 2])
        rstd = sb("rstd", [P, GT])
        n_sb = sb("n", [P, GT, D])
        nT = sb("nT", [P, GROUP_TOKENS])
        nT_part = [[sb(f"nT_{part}{u}", [P, GROUP_TOKENS], F32R) for part in ("hi", "lo")] for u in range(2)]
        score = sb("score", [P, GT, E1 + 2])
        best = sb("best", [P, GT, 8])
        marked = sb("marked", [P, GT, E1 + 2])
        chosen = sb("chosen", [P, GT, E1])
        power = sb("power", [P, GT, E1])
        total = sb("total", [P, GT])
        comb = sb("comb", [P, GT, 2, E1], F32R)
        combT = two("combT", [P, GROUP_TOKENS], F32R)
        silu = two("silu", [P, GROUP_TOKENS])
        gated = two("gated", [P, GROUP_TOKENS])
        hidden = two("hidden", [P, GROUP_TOKENS])
        outT = sb("outT", [P, GROUP_TOKENS])
        result = two("result", [P, GT, D])

        def bank(name):
            return ctx.enter_context(nc.psum_tensor("f_" + name, [P, 512], F32))

        ps1 = [bank("ps1_0"), bank("ps1_1")]
        ps3 = [bank("ps3_0"), bank("ps3_1")]
        ps_comb = [bank("ps_comb0"), bank("ps_comb1")]
        ps_out = bank("ps_out")
        ps_turn = bank("ps_turn")

        gate_loaded, const, dve_seen, numbers, spread_ready, split_hi = map(
            sem, ("gate_loaded", "const", "dve_seen", "numbers", "spread_ready", "split_hi"))
        weights = [sem("weights0"), sem("weights1")]
        split = [sem("split0"), sem("split1")]
        (ln_stats, ln_var, ln_eps, ln_root, n_ready, n_turned, nT_ready, nT_hi, parts_ready) = map(
            sem, ("ln_stats", "ln_var", "ln_eps", "ln_root", "n_ready", "n_turned", "nT_ready", "nT_hi",
                  "parts_ready"))
        (scores_done, score_ready, best_ready, best_cut, marked_ready, chosen_ready, below_ready, power_ready,
         power_cut, total_ready, share_ready, comb_full, comb_hi, comb_ready, comb_turned, combT_ready) = map(
            sem, ("scores_done", "score_ready", "best_ready", "best_cut", "marked_ready", "chosen_ready",
                  "below_ready", "power_ready", "power_cut", "total_ready", "share_ready", "comb_full",
                  "comb_hi", "comb_ready", "comb_turned", "combT_ready"))
        x1_done, x3_done, spread_done, silu_ready, gated_ready, hidden_ready, hidden_used = map(
            sem, ("x1_done", "x3_done", "spread_done", "silu_ready", "gated_ready", "hidden_ready",
                  "hidden_used"))
        outT_ready, out_turned, result_ready = map(sem, ("outT_ready", "out_turned", "result_ready"))
        stored = [sem("stored0"), sem("stored1")]

        def plain(ap):
            return ap.bitcast(F32)

        def chunks(name):
            return dram[name].rearrange("d (c m) -> d c m", m=P)

        half = [slice(0, CH // 2), slice(CH // 2, CH)]

        def pieces(routed, shared, k):
            lo, hi = half[k].start, half[k].stop
            found = [(w2[:, lo:min(hi, ROUTED), :], routed[:, lo:min(hi, ROUTED), :])]
            if hi > ROUTED:
                found.append((w2[:, ROUTED:, :], shared))
            return found

        rows = {name: dram[name].rearrange("(c m) d -> m c d", m=P) for name in ("w2", "w_sdT")}
        sources = [(chunks("w1T"), chunks("w_sgT")), (chunks("w3T"), chunks("w_suT")), (rows["w2"], rows["w_sdT"])]
        PIECES = [1, 2]
        CONSTS = 5
        out_d = dram["out"].rearrange("(g t p) d -> g p t d", t=GT, p=P)

        def tile_of(g, t):
            return keep.h[:, (GT // PT) * g + t // PT, t % PT, :]

        STATS, VAR, NORM, TURN, COPY_N, PARTS, SCORES = 4, 6, 8, 10, 11, 12, 12
        CHOOSE = 14
        POWER, TURN_COMB, COPY_COMB = CHOOSE + 3, CHOOSE + 12, CHOOSE + 13
        COPY_OUT, TURN_OUT, ADD_OUT = 1, 4, 5
        LAG = 2
        AHEAD = 2

        start_counts(nc, [*stored, outT_ready, scores_done, parts_ready, out_turned, n_turned, comb_turned])

        with nc.Block() as block:
            @block.sync
            def _(sp):
                sp.dma_start(gate[:, :], dram["w_gateT"]).then_inc(gate_loaded, 16)
                for n, (routed, shared) in enumerate(sources):
                    for k in range(2):
                        if n > 0:
                            sp.wait_ge(split[k], n)
                        for dst, src in pieces(routed, shared, k):
                            sp.dma_start(dst, src).then_inc(weights[k], 16)
                with sp.Fori(0, GROUPS1 // 2) as p:
                    for u in range(2):
                        sp.wait_ge(result_ready, 2 * p + u + 1)
                        sp.dma_start(out_d[2 * p + u], result[u][:, :, :]).then_inc(stored[u], 16)
                for u in range(2):
                    sp.wait_ge(stored[u], START + 16 * (GROUPS1 // 2))

            @block.gpsimd
            def _(pool):
                nc.gpsimd.memset(half_neg[:, :], -0.5).then_inc(const, 1)
                nc.gpsimd.memset(eps[:, :], LN_EPS).then_inc(const, 1)
                nc.gpsimd.memset(score[:, :, E1:], LEAST).then_inc(const, 1)
                nc.gpsimd.iota(own_i[:, :], pattern=[[0, 1]], base=0, channel_multiplier=1).then_inc(const, 1)
                nc.gpsimd.iota(expert_i[:, :], pattern=[[1, E1]], base=0, channel_multiplier=0)\
                    .then_inc(const, 1)
                def inverse_deviation(g):
                    pool.wait_ge(ln_var, GT * (g + 1))
                    nc.gpsimd.tensor_tensor(rstd[:, :], mean_var[:, :, 1], eps[:, :], ALU.add).then_inc(ln_eps, 1)
                    pool.wait_ge(ln_eps, g + 1)
                    nc.gpsimd.tensor_tensor(rstd[:, :], rstd[:, :], half_neg[:, :], ALU.pow).then_inc(ln_root, 1)

                inverse_deviation(0)
                with pool.Fori(1, GROUPS1) as g:
                    inverse_deviation(g)

            @block.tensor
            def _(pe):
                def turn_n(g, first):
                    pe.wait_ge(n_ready, GT * (g + 1))
                    if not first:
                        pe.wait_ge(result_ready, g - 1)
                    for t in range(GT):
                        ins = nc.tensor.transpose(ps_turn[:, t * P:(t + 1) * P], n_sb[:, t, :], keep.ident[:, :])
                    ins.then_inc(n_turned, 1)

                def score_tokens(g):
                    pe.wait_ge(nT_ready, g + 1)
                    for t in range(GT):
                        ins = nc.tensor.matmul(ps_turn[:, t * E1:(t + 1) * E1], nT[:, t * P:(t + 1) * P],
                                               gate[:, :], start=True, stop=True)
                    ins.then_inc(scores_done, 1)

                def turn_comb(g):
                    pe.wait_ge(comb_ready, g + 1)
                    for t in range(GT):
                        ins = nc.tensor.transpose(ps_turn[:, t * P:(t + 1) * P],
                                                  plain(comb[:, t, :, :]).rearrange("p i e -> p (i e)"),
                                                  keep.ident[:, :])
                    ins.then_inc(comb_turned, 1)

                def turn_out(g, last):
                    pe.wait_ge(outT_ready, START + g + 1)
                    if not last:
                        pe.wait_ge(combT_ready, g + 2)
                    for t in range(GT):
                        ins = nc.tensor.transpose(ps_turn[:, t * P:(t + 1) * P], outT[:, t * P:(t + 1) * P],
                                                  keep.ident[:, :])
                    ins.then_inc(out_turned, 1)

                def in_parts(dst, w, x, c):
                    nc.tensor.matmul(dst, w[0][:, c, :], x[0][:, :], start=True, stop=False)
                    nc.tensor.matmul(dst, w[0][:, c, :], x[1][:, :], start=False, stop=False)
                    return nc.tensor.matmul(dst, w[1][:, c, :], x[0][:, :], start=False, stop=True)

                def up(g, u, c):
                    n = CH * g + c
                    pe.wait_ge(silu_ready, n + 1)
                    in_parts(ps1[c % 2][:, :], w1, nT_part[u], c).then_inc(x1_done, 1)
                    pe.wait_ge(gated_ready, n + 1)
                    in_parts(ps3[c % 2][:, :], w3, nT_part[u], c).then_inc(x3_done, 1)
                    if c < ROUTED:
                        pe.wait_ge(hidden_ready, n + 1)
                        nc.tensor.matmul(ps_comb[c % 2][:, :], spread[:, c, :], combT[u][:, :],
                                         start=True, stop=True).then_inc(spread_done, 1)

                def down(g, c):
                    pe.wait_ge(hidden_ready, CH * g + c + AHEAD + 1)
                    if c == 0:
                        pe.wait_ge(outT_ready, START + g)
                    nc.tensor.matmul(ps_out[:, :], w2[:, c, :], hidden[c % 2][:, :], start=(c == 0),
                                     stop=(c == CH - 1)).then_inc(hidden_used, 1)

                def group(g, u, first, last):
                    pe.wait_ge(parts_ready, START + g + 1)
                    pe.wait_ge(combT_ready, g + 1)
                    for c in range(CH + LAG):
                        if c < CH:
                            up(g, u, c)
                        if c >= LAG:
                            down(g, c - LAG)
                        if c == TURN_OUT and not first:
                            turn_out(g - 1, False)
                        if c == TURN and not last:
                            turn_n(g + 1, first)
                        if c == SCORES and not last:
                            score_tokens(g + 1)
                        if c == TURN_COMB and not last:
                            turn_comb(g + 1)

                pe.wait_ge(gate_loaded, 16)
                pe.sem_inc(hidden_used, AHEAD)
                turn_n(0, True)
                score_tokens(0)
                turn_comb(0)
                pe.wait_ge(spread_ready, 1)
                for k in range(2):
                    pe.wait_ge(split[k], 2)
                    pe.wait_ge(weights[k], 16 * PIECES[k] * 3)
                group(0, 0, True, False)
                with pe.Fori(0, GROUPS1 // 2 - 1) as p:
                    group(2 * p + 1, 1, False, False)
                    group(2 * p + 2, 0, False, False)
                group(GROUPS1 - 1, 1, False, True)
                turn_out(GROUPS1 - 1, True)

            @block.scalar
            def _(act):
                def copy_nT(g):
                    act.wait_ge(n_turned, START + g + 1)
                    act.wait_ge(scores_done, START + g)
                    act.wait_ge(parts_ready, START + g)
                    nc.scalar.copy(nT[:, :], ps_turn[:, :]).then_inc(nT_ready, 1)

                def raise_power(g):
                    act.wait_ge(below_ready, g + 1)
                    nc.scalar.activation(power[:, :, :].rearrange("p t e -> p (t e)"),
                                         power[:, :, :].rearrange("p t e -> p (t e)"),
                                         ACT.Exp).then_inc(power_ready, 1)

                def copy_combT(g, u, first):
                    act.wait_ge(comb_turned, START + g + 1)
                    if not first:
                        act.wait_ge(spread_done, ROUTED * (g - 1))
                    nc.scalar.copy(combT[u][:, :], ps_turn[:, :]).then_inc(combT_ready, 1)

                def copy_out(g):
                    act.wait_ge(hidden_used, CH * (g + 1) + AHEAD)
                    act.wait_ge(out_turned, START + g)
                    nc.scalar.copy(outT[:, :], ps_out[:, :]).then_inc(outT_ready, 1)

                def group(g, u, first, last):
                    for c in range(CH):
                        n = CH * g + c
                        act.wait_ge(x1_done, n + 1)
                        act.wait_ge(gated_ready, n + 1)
                        nc.scalar.activation(silu[c % 2][:, :], ps1[c % 2][:, :], ACT.Silu)\
                            .then_inc(silu_ready, 1)
                        if c == COPY_OUT and not first:
                            copy_out(g - 1)
                        if c == COPY_N and not last:
                            copy_nT(g + 1)
                        if c == POWER and not last:
                            raise_power(g + 1)
                        if c == COPY_COMB and not last:
                            copy_combT(g + 1, 1 - u, False)

                act.sem_inc(silu_ready, AHEAD)
                copy_nT(0)
                raise_power(0)
                copy_combT(0, 0, True)
                group(0, 0, True, False)
                with act.Fori(0, GROUPS1 // 2 - 1) as p:
                    group(2 * p + 1, 1, False, False)
                    group(2 * p + 2, 0, False, False)
                group(GROUPS1 - 1, 1, False, True)
                copy_out(GROUPS1 - 1)

            @block.vector
            def _(dve):
                def statistics(g):
                    for t in range(GT):
                        nc.vector.bn_stats(stats[:, t, :], tile_of(g, t)).then_inc(ln_stats, 1)

                def mean_variance(g):
                    dve.wait_ge(ln_stats, GT * (g + 1))
                    stand_alone(dve, dve_seen)
                    for t in range(GT):
                        nc.vector.bn_aggr(mean_var[:, t, :], stats[:, t, :]).then_inc(ln_var, 1)

                def normalise(g):
                    dve.wait_ge(ln_root, g + 1)
                    dve.wait_ge(n_turned, START + g)
                    for t in range(GT):
                        nc.vector.tensor_scalar(n_sb[:, t, :], tile_of(g, t), mean_var[:, t, 0:1], rstd[:, t:t + 1],
                                                ALU.subtract, ALU.mult).then_inc(n_ready, 1)

                def part_nT(g, u, first):
                    hi, lo = nT_part[u]
                    dve.wait_ge(nT_ready, g + 1)
                    if not first:
                        dve.wait_ge(x3_done, CH * (g - 1))
                    nc.vector.tensor_copy(hi[:, :], nT[:, :]).then_inc(nT_hi, 1)
                    dve.wait_ge(nT_hi, g + 1)
                    nc.vector.tensor_tensor(lo[:, :], nT[:, :], plain(hi[:, :]), ALU.subtract).then_inc(parts_ready, 1)

                def copy_scores(g):
                    dve.wait_ge(scores_done, START + g + 1)
                    nc.vector.tensor_copy(score[:, :, 0:E1],
                                          ps_turn[:, 0:GT * E1].rearrange("p (t e) -> p t e", e=E1))\
                        .then_inc(score_ready, 1)

                def eight_best(g):
                    dve.wait_ge(score_ready, g + 1)
                    stand_alone(dve, dve_seen)
                    for t in range(GT):
                        nc.vector.max(best[:, t, :], score[:, t, :]).then_inc(best_ready, 1)

                def below_best(g):
                    dve.wait_ge(best_ready, GT * (g + 1))
                    nc.vector.tensor_tensor(power[:, :, :], score[:, :, 0:E1],
                                            best[:, :, 0:1].broadcast_to([P, GT, E1]), ALU.subtract)\
                        .then_inc(below_ready, 1)
                    nc.vector.memset(best[:, :, TOP_K:], LEAST).then_inc(best_cut, 1)

                def mark_best(g):
                    dve.wait_ge(best_cut, g + 1)
                    stand_alone(dve, dve_seen)
                    for t in range(GT):
                        nc.vector.match_replace(marked[:, t, :], best[:, t, :], score[:, t, :], LEAST)\
                            .then_inc(marked_ready, 1)

                def find_chosen(g):
                    dve.wait_ge(marked_ready, GT * (g + 1))
                    nc.vector.tensor_tensor(chosen[:, :, :], marked[:, :, 0:E1], score[:, :, 0:E1], ALU.is_lt)\
                        .then_inc(chosen_ready, 1)

                def cut_power(g):
                    dve.wait_ge(chosen_ready, g + 1)
                    dve.wait_ge(power_ready, g + 1)
                    nc.vector.tensor_tensor(power[:, :, :], power[:, :, :], chosen[:, :, :], ALU.mult)\
                        .then_inc(power_cut, 1)

                def add_power(g):
                    dve.wait_ge(power_cut, g + 1)
                    nc.vector.tensor_reduce(total[:, :], power[:, :, :], AX.X, ALU.add).then_inc(total_ready, 1)

                def invert_total(g):
                    dve.wait_ge(total_ready, g + 1)
                    nc.vector.reciprocal(total[:, :], total[:, :]).then_inc(share_ready, 1)

                def divide(g):
                    dve.wait_ge(share_ready, g + 1)
                    nc.vector.tensor_tensor(power[:, :, :], power[:, :, :],
                                            total[:, :].unsqueeze(2).broadcast_to([P, GT, E1]), ALU.mult)\
                        .then_inc(comb_full, 1)

                def comb_high(g):
                    dve.wait_ge(comb_full, g + 1)
                    dve.wait_ge(comb_turned, START + g)
                    nc.vector.tensor_copy(comb[:, :, 0, :], power[:, :, :]).then_inc(comb_hi, 1)

                def comb_low(g):
                    dve.wait_ge(comb_hi, g + 1)
                    nc.vector.tensor_tensor(comb[:, :, 1, :], power[:, :, :], plain(comb[:, :, 0, :]), ALU.subtract)\
                        .then_inc(comb_ready, 1)

                def add_out(g, u, turn):
                    dve.wait_ge(out_turned, START + g + 1)
                    dve.wait_ge(stored[u], START + 16 * turn)
                    for s in range(GT // PT):
                        ins = nc.vector.tensor_tensor(
                            result[u][:, s * PT:(s + 1) * PT, :], keep.h[:, (GT // PT) * g + s, :, :],
                            ps_turn[:, s * PT * D:(s + 1) * PT * D].rearrange("p (t d) -> p t d", t=PT), ALU.add)
                    ins.then_inc(result_ready, 1)

                def group(g, u, turn, first, last):
                    for c in range(CH):
                        n = CH * g + c
                        dve.wait_ge(silu_ready, n + AHEAD + 1)
                        dve.wait_ge(x3_done, n + 1)
                        if c < ROUTED:
                            nc.vector.tensor_tensor(gated[c % 2][:, :], silu[c % 2][:, :], ps3[c % 2][:, :],
                                                    ALU.mult).then_inc(gated_ready, 1)
                            dve.wait_ge(gated_ready, n + AHEAD + 1)
                            dve.wait_ge(spread_done, ROUTED * g + c + 1)
                            dve.wait_ge(hidden_used, n + 1)
                            nc.vector.tensor_tensor(hidden[c % 2][:, :], gated[c % 2][:, :], ps_comb[c % 2][:, :],
                                                    ALU.mult).then_inc(hidden_ready, 1)
                        else:
                            dve.wait_ge(hidden_used, n + 1)
                            nc.vector.tensor_tensor(hidden[c % 2][:, :], silu[c % 2][:, :], ps3[c % 2][:, :],
                                                    ALU.mult).then_inc(gated_ready, 1)
                            dve.wait_ge(gated_ready, n + AHEAD + 1)
                            dve.sem_inc(hidden_ready, 1)
                        if c == ADD_OUT and not first:
                            add_out(g - 1, 1 - u, turn)
                        if not last:
                            if c == PARTS:
                                part_nT(g + 1, 1 - u, False)
                            if c in at:
                                at[c](g + 1)

                steps = [copy_scores, eight_best, below_best, mark_best, find_chosen, cut_power, add_power,
                         invert_total, divide, comb_high, comb_low]
                at = {STATS: statistics, VAR: mean_variance, NORM: normalise}
                at.update({CHOOSE + i: step for i, step in enumerate(steps)})
                dve.sem_inc(gated_ready, AHEAD)
                dve.sem_inc(hidden_ready, AHEAD)
                dve.wait_ge(const, CONSTS)
                statistics(0)
                mean_variance(0)
                normalise(0)
                part_nT(0, 0, True)
                for step in steps:
                    step(0)
                nc.vector.tensor_scalar(own_i[:, :], own_i[:, :], E1 - 1, None, ALU.bitwise_and)\
                    .then_inc(numbers, 1)
                dve.wait_ge(numbers, 1)
                nc.vector.tensor_copy(own[:, :], own_i[:, :]).then_inc(numbers, 1)
                nc.vector.tensor_copy(expert[:, :], expert_i[:, :]).then_inc(numbers, 1)
                dve.wait_ge(numbers, 3)
                nc.vector.tensor_scalar(spread[:, :, :].rearrange("p c (j i) -> p (c j) i", i=P // 2),
                                        expert[:, :].unsqueeze(2).broadcast_to([P, E1, P // 2]), own[:, 0:1], None,
                                        ALU.is_equal).then_inc(spread_ready, 1)
                for n, w in enumerate((w1, w3)):
                    for k in range(2):
                        dve.wait_ge(weights[k], 16 * PIECES[k] * (n + 1))
                        nc.vector.tensor_copy(w[0][:, half[k], :], w2[:, half[k], :]).then_inc(split_hi, 1)
                        dve.wait_ge(split_hi, 2 * n + k + 1)
                        nc.vector.tensor_tensor(w[1][:, half[k], :], w2[:, half[k], :], plain(w[0][:, half[k], :]),
                                                ALU.subtract).then_inc(split[k], 1)
                group(0, 0, 0, True, False)
                with dve.Fori(0, GROUPS1 // 2 - 1) as p:
                    group(2 * p + 1, 1, p, False, False)
                    group(2 * p + 2, 0, p, False, False)
                group(GROUPS1 - 1, 1, GROUPS1 // 2 - 1, False, True)
                add_out(GROUPS1 - 1, 1, GROUPS1 // 2 - 1)
        nc.clear_and_free_semaphores(sems)
        nc.all_engine_barrier()


def initialise(nc, keep):
    zeroed, ready, spare_ready = (nc.alloc_semaphore(n) for n in ("i_zeroed", "i_ready", "i_spare_ready"))
    with nc.Block() as block:
        @block.gpsimd
        def _(pool):
            make_identity(nc, pool, keep.ident, zeroed, ready)
            nc.gpsimd.memset(keep.tokens[:, E0 * CT:], 0).then_inc(spare_ready, 1)
    nc.clear_and_free_semaphores([zeroed, ready, spare_ready])
    nc.all_engine_barrier()


class Keep:

    def __init__(self, nc, ctx):
        def sb(name, shape, dt=F32):
            return ctx.enter_context(nc.sbuf_tensor("keep_" + name, shape, dt))

        self.ident = sb("ident", [P, P])
        self.h = sb("h", [P, B, PT, D])
        self.top_f32 = sb("top_f32", [P, B * H0])
        self.top_row = sb("top_row", [P, (B + 2) * H0], I32)
        self.tokens = sb("tokens", [P, (E0 + 2) * CT], I32)


def build(nc, dram, out):
    def scratch(name, shape):
        return nc.dram_tensor(name, shape, F32, kind="Internal").ap()

    def part(prefix, **more):
        found = {name[len(prefix):]: ap for name, ap in dram.items() if name.startswith(prefix)}
        found.update(more)
        return found

    q_rows = scratch("q_rows", (B * L * H0, HD0))
    token_rows = scratch("token_rows", (TOK, ROW))
    with ExitStack() as ctx:
        keep = Keep(nc, ctx)
        initialise(nc, keep)
        tok = part("L0_tok_", x=dram["x"], xT=dram["xT"], q_rows=q_rows)
        select_queries(nc, tok, keep)
        token_layer(nc, tok, keep)
        windowed_attention(nc, part("L0_attn_"), keep)
        ffn = part("L0_ffn_", token_rows=token_rows, lists=scratch("lists", (TOK,)),
                   sum0=scratch("sum0", (TOK, D)), sum1=scratch("sum1", (TOK, D)))
        route(nc, ffn, keep)
        experts(nc, ffn, keep)
        delta_rule(nc, part("L1_attn_"), keep)
        expert_ffn(nc, part("L1_ffn_", out=out.rearrange("b l d -> (b l) d")), keep)


def lay_out(inputs):
    x = dict(inputs)
    x["xT"] = x["x"].transpose(0, 2, 1)
    x["L0_tok_f1_b"] = x["L0_tok_f1_b"].reshape(FC, P).T
    x["L0_tok_conv_w"] = x["L0_tok_conv_w"].transpose(1, 2, 0)
    x["L0_ffn_b_upT"] = x.pop("L0_ffn_b_up").T
    x["L1_attn_WT"] = x.pop("L1_attn_W").T
    for name in ("L1_attn_eta", "L1_attn_lam_logit"):
        x[name] = x[name].reshape(1)
    for name in ("w_gate", "w_sg", "w_su", "w_sd"):
        x[f"L1_ffn_{name}T"] = x.pop(f"L1_ffn_{name}").T
    for name in ("w1", "w3"):
        x[f"L1_ffn_{name}T"] = x.pop(f"L1_ffn_{name}").reshape(-1, D).T
    x["L1_ffn_w2"] = x["L1_ffn_w2"].reshape(-1, D)
    return x


def kernel(**inputs):
    import numpy as np
    import concourse.bacc as bacc
    from concourse.bass_utils import run_bass_kernel_spmd

    nc = bacc.Bacc("TRN2", target_bir_lowering=False, num_devices=1)
    arrays, dram = {}, {}
    for name, a in lay_out({name: np.asarray(a) for name, a in inputs.items()}).items():
        a = np.ascontiguousarray(a).reshape(a.shape)
        arrays[f"in_{name}"] = a
        dram[name] = nc.dram_tensor(f"in_{name}", a.shape, mybir.dt.from_np(a.dtype), kind="ExternalInput").ap()
    out = nc.dram_tensor("out", (B, LP, D), F32, kind="ExternalOutput").ap()
    build(nc, dram, out)
    return run_bass_kernel_spmd(nc, [arrays], core_ids=[0]).results[0]["out"]
```

```python
from contextlib import ExitStack

import concourse.bass as bass
from concourse import mybir

ALU = mybir.AluOpType
ACT = mybir.ActivationFunctionType
F32 = mybir.dt.float32
F32R = mybir.dt.float32r
BF16 = mybir.dt.bfloat16
F16 = mybir.dt.float16
I32 = mybir.dt.int32
U32 = mybir.dt.uint32
AX = mybir.AxisListType

P = 128
B, L, D = 32, 512, 128
LT = L // P
H0, HD0 = 8, 16
TOP = int(L * 0.2)
LN_EPS = 1e-5
START = 2
PAIRS = B // 2


def stand_alone(eng, seen):
    eng.sem_inc(seen, 1)


def start_counts(nc, sems):
    with nc.Block() as block:
        @block.sync
        def _(sp):
            for s in sems:
                sp.sem_inc(s, START)
    nc.all_engine_barrier()


def make_identity(nc, pool, ident, zeroed, ready):
    nc.gpsimd.memset(ident[:, :], 0.0).then_inc(zeroed, 1)
    pool.wait_ge(zeroed, 1)
    nc.gpsimd.affine_select(out=ident[:, :], in_=ident[:, :], compare_op=ALU.not_equal, fill=1.0, base=0,
                            pattern=[[-1, P]], channel_multiplier=1).then_inc(ready, 1)


def select_queries(nc, dram, keep):
    GROUPS = 2
    GB = B // GROUPS
    ROUNDS = -(-TOP // 8)
    sems = []
    with ExitStack() as ctx:
        def sb(name, shape, dt=F32):
            return ctx.enter_context(nc.sbuf_tensor(name, shape, dt))

        def two(name, shape, dt=F32):
            return [sb(f"{name}{u}", shape, dt) for u in range(2)]

        def ps(name, shape):
            return ctx.enter_context(nc.psum_tensor(name, shape, F32))

        def sem(name):
            sems.append(nc.alloc_semaphore("q_" + name))
            return sems[-1]

        def sem2(name):
            return [sem(f"{name}{u}") for u in range(2)]

        xT = two("q1_xT", [P, L])
        q_sb = two("q1_q", [P, LT, D])
        sq = two("q1_sq", [P, LT, H0, HD0])
        wq = sb("q1_wq", [P, D])
        qb = sb("q1_qb", [P, D])
        norms = sb("q1_norms", [P, LT, B, H0])
        rows = two("q1_rows", [P, L])
        best = two("q1_best", [P, 8])
        found = two("q1_found", [P, ROUNDS * 8], U32)
        found_f = two("q1_found_f", [P, ROUNDS * 8])
        base = sb("q1_base", [P, B, H0], I32)
        base_f = sb("q1_base_f", [P, B * H0])
        psT = [ps(f"q1_psT{u}", [P, L]) for u in range(2)]
        psQ = [ps(f"q1_psQ{u}", [P, LT, D]) for u in range(2)]
        psR = [ps(f"q1_psR{u}", [P, L]) for u in range(2)]

        weights = sem("weights")
        xT_loaded = sem2("xT_loaded")
        q_done = sem2("q_done")
        q_ready = sem2("q_ready")
        q_squared = sem2("q_squared")
        q_stored = sem2("q_stored")
        norms_ready = sem2("norms_ready")
        rows_turned = sem("rows_turned")
        rows_ready = sem("rows_ready")
        best_ready = sem2("best_ready")
        found_ready = sem2("found_ready")
        row_marked = sem2("row_marked")
        found_cast = sem("found_cast")
        found_turned = sem("found_turned")
        top_ready = sem("top_ready")
        spare_ready = sem("spare_ready")
        base_ready = sem("base_ready")
        base_cast = sem("base_cast")

        q_d = dram["q_rows"].rearrange("(b t p h) c -> b p t (h c)", b=B, t=LT, h=H0)

        start_counts(nc, [*q_ready, *norms_ready, *q_stored, *q_squared])

        with nc.Block() as block:
            @block.sync
            def _(sp):
                sp.dma_start(wq[:, :], dram["q_w"]).then_inc(weights, 16)
                sp.dma_start(qb[:, :], dram["q_b"].partition_broadcast(P)).then_inc(weights, 16)
                for u in range(2):
                    sp.dma_start(xT[u][:, :], dram["xT"][u]).then_inc(xT_loaded[u], 16)
                with sp.Fori(0, PAIRS - 1) as p:
                    for u in range(2):
                        sp.wait_ge(q_done[u], p + 1)
                        sp.dma_start(xT[u][:, :], dram["xT"][2 * p + 2 + u]).then_inc(xT_loaded[u], 16)
                        sp.wait_ge(q_ready[u], START + p + 1)
                        sp.dma_start(q_d[2 * p + u], q_sb[u][:, :, :]).then_inc(q_stored[u], 16)
                for u in range(2):
                    sp.wait_ge(q_ready[u], START + PAIRS)
                    sp.dma_start(q_d[2 * (PAIRS - 1) + u], q_sb[u][:, :, :]).then_inc(q_stored[u], 16)
                for u in range(2):
                    sp.wait_ge(q_stored[u], START + 16 * PAIRS)

            @block.gpsimd
            def _(pool):
                nc.gpsimd.memset(keep.top_row[0:TOP, B * H0:], 0).then_inc(spare_ready, 1)
                nc.gpsimd.iota(base[:, :, :], pattern=[[L * H0, B], [1, H0]], base=0,
                               channel_multiplier=0).then_inc(base_ready, 1)

            @block.tensor
            def _(pe):
                pe.wait_ge(weights, 32)
                with pe.Fori(0, PAIRS) as p:
                    for u in range(2):
                        pe.wait_ge(xT_loaded[u], 16 * p + 16)
                        pe.wait_ge(q_ready[u], START + p)
                        for t in range(LT):
                            ins = nc.tensor.matmul(psQ[u][:, t, :], xT[u][:, t * P:(t + 1) * P], wq[:, :],
                                                   start=True, stop=True)
                        ins.then_inc(q_done[u], 1)
                for u in range(2):
                    pe.wait_ge(norms_ready[u], START + PAIRS)
                for g in range(GROUPS):
                    for t in range(LT):
                        ins = nc.tensor.transpose(psR[g][:, t * P:(t + 1) * P],
                                                  norms[:, t, g * GB:(g + 1) * GB, :].rearrange("p b h -> p (b h)"),
                                                  keep.ident[:, :])
                    ins.then_inc(rows_turned, 1)
                for g in range(GROUPS):
                    pe.wait_ge(found_cast, g + 1)
                    nc.tensor.transpose(psT[g][0:TOP, 0:P], found_f[g][:, 0:TOP],
                                        keep.ident[:, :]).then_inc(found_turned, 1)

            @block.scalar
            def _(act):
                with act.Fori(0, PAIRS) as p:
                    for u in range(2):
                        act.wait_ge(q_ready[u], START + p + 1)
                        act.wait_ge(norms_ready[u], START + p)
                        nc.scalar.activation(sq[u][:, :, :, :].rearrange("p t h c -> p (t h c)"),
                                             q_sb[u][:, :, :].rearrange("p t d -> p (t d)"),
                                             ACT.Square).then_inc(q_squared[u], 1)

            @block.vector
            def _(dve):
                dve.wait_ge(weights, 32)
                with dve.Fori(0, PAIRS) as p:
                    for u in range(2):
                        dve.wait_ge(q_done[u], p + 1)
                        dve.wait_ge(q_stored[u], START + 16 * p)
                        dve.wait_ge(q_squared[u], START + p)
                        nc.vector.tensor_tensor(q_sb[u][:, :, :], psQ[u][:, :, :],
                                                qb[:, :].unsqueeze(1).broadcast_to([P, LT, D]),
                                                ALU.add).then_inc(q_ready[u], 1)
                    for u in range(2):
                        dve.wait_ge(q_squared[u], START + p + 1)
                        nc.vector.tensor_reduce(norms[:, :, 2 * p + u, :], sq[u][:, :, :, :], AX.X,
                                                ALU.add).then_inc(norms_ready[u], 1)
                for g in range(GROUPS):
                    dve.wait_ge(rows_turned, g + 1)
                    nc.vector.tensor_copy(rows[g][:, :], psR[g][:, :]).then_inc(rows_ready, 1)
                for r in range(ROUNDS):
                    for g in range(GROUPS):
                        if r == 0:
                            dve.wait_ge(rows_ready, g + 1)
                        else:
                            dve.wait_ge(row_marked[g], r)
                        nc.vector.max(best[g][:, :], rows[g][:, :]).then_inc(best_ready[g], 1)
                    for g in range(GROUPS):
                        dve.wait_ge(best_ready[g], r + 1)
                        nc.vector.max_index(found[g][:, 8 * r:8 * r + 8], best[g][:, :],
                                            rows[g][:, :]).then_inc(found_ready[g], 1)
                    for g in range(GROUPS):
                        dve.wait_ge(found_ready[g], r + 1)
                        nc.vector.match_replace(rows[g][:, :], best[g][:, :], rows[g][:, :],
                                                -1.0).then_inc(row_marked[g], 1)
                for g in range(GROUPS):
                    dve.wait_ge(found_ready[g], ROUNDS)
                    nc.vector.tensor_copy(found_f[g][:, :], found[g][:, :]).then_inc(found_cast, 1)
                dve.wait_ge(base_ready, 1)
                nc.vector.tensor_copy(base_f[:, :], base[:, :, :].rearrange("p b h -> p (b h)"))\
                    .then_inc(base_cast, 1)
                dve.wait_ge(base_cast, 1)
                for g in range(GROUPS):
                    dve.wait_ge(found_turned, g + 1)
                    cols = slice(g * P, (g + 1) * P)
                    nc.vector.tensor_copy(keep.top_f32[0:TOP, cols], psT[g][0:TOP, 0:P]).then_inc(top_ready, 1)
                    dve.wait_ge(top_ready, 2 * g + 1)
                    nc.vector.scalar_tensor_tensor(out=keep.top_row[0:TOP, cols], in0=keep.top_f32[0:TOP, cols],
                                                   scalar=float(H0), in1=base_f[0:TOP, cols], op0=ALU.mult,
                                                   op1=ALU.add).then_inc(top_ready, 1)
        nc.clear_and_free_semaphores(sems)
        nc.all_engine_barrier()


LP = L // 2
PT = LP // P
FF = 512
FC = FF // P


def turns(eng, turn):
    turn((0, 0), None)
    turn((1, 0), (0, 0))
    with eng.Fori(0, PAIRS - 1) as p:
        turn((0, p + 1), (1, p))
        turn((1, p + 1), (0, p + 1))
    turn(None, (1, PAIRS - 1))


def token_layer(nc, dram, keep):
    sems = []
    with ExitStack() as ctx:
        def sb(name, shape, dt=F32):
            return ctx.enter_context(nc.sbuf_tensor("t_" + name, shape, dt))

        def two(name, shape, dt=F32):
            return [sb(f"{name}{u}", shape, dt) for u in range(2)]

        def sem(name):
            sems.append(nc.alloc_semaphore("t_" + name))
            return sems[-1]

        def sem2(name):
            return [sem(f"{name}{u}") for u in range(2)]

        w_small = {n: sb(n, [P, D]) for n in ("k_w", "v_w", "o_w")}
        rows = {n: sb(n, [P, D]) for n in ("v_b", "o_b", "ln1_g", "ln1_b", "ln2_g", "ln2_b", "f2_b")}
        cols = {n: sb(n, [P, 1]) for n in ("k_b", "conv_b")}
        f1_w = sb("f1_w", [P, FF])
        f1_b = sb("f1_b", [P, FC])
        f2_w = sb("f2_w", [P, FC, D])
        conv_w = sb("conv_w", [P, 3, D])
        out_shift = sb("out_shift", [P, D])
        head_mask = sb("head_mask", [P, H0])
        mean_w = sb("mean_w", [P, P])
        half_neg = sb("half_neg", [P, LT])
        eps = sb("eps", [P, LT])
        iota_i = sb("iota_i", [P, L], I32)
        iota_h = sb("iota_h", [P, L], F16)

        x_sb = two("x", [P, LT, D])
        x_shift = two("x_shift", [P, LT, D])
        xT = two("xT", [P, L])
        kT = two("kT", [P, L])
        v1 = two("v1", [P, LT, H0, HD0 + 1])
        top_col = two("top_col", [P, H0], I32)
        q_top = two("q_top", [P, D])
        q_diag = two("q_diag", [P, H0, TOP])
        v_mean = two("v_mean", [P, D])
        low = two("low", [P, H0])
        probs = two("probs", [P, 2, L])
        probsT = two("probsT", [P, 2, LT, TOP])
        place = two("place", [P, H0, L], BF16)
        o_scale = two("o_scale", [P, H0])
        o_top = two("o_top", [P, H0, HD0])
        o_rest = two("o_rest", [P, H0, HD0])
        o_part = two("o_part", [P, 3, D], BF16)
        attn = two("attn", [P, LT, D])
        attnT = two("attnT", [P, L])
        ao_shift = two("ao_shift", [P, LT, D])
        z = two("z", [P, LT, D])
        stats = two("stats", [P, LT, 6])
        mean_var = two("mean_var", [P, LT, 2])
        rstd = two("rstd", [P, LT])
        h1 = two("h1", [P, LT, D])
        h1T = two("h1T", [P, L])
        ff = two("ff", [P, FC, L])
        fusedT = two("fusedT", [P, L + 2])
        pooled = two("pooled", [P, LP])
        yT = two("yT", [P, LP])

        bank = [[ctx.enter_context(nc.psum_tensor(f"t_bank{u}{k}", [P, 512], F32)) for k in range(4)]
                for u in range(2)]

        def tiles(ap, n=LT):
            return ap.rearrange("p (t d) -> p t d", t=n)

        def per_tile(row, n=LT):
            return row[:, :].unsqueeze(1).broadcast_to([P, n, D])

        weights = sem("weights")
        const = sem("const")
        dve_seen = sem("dve_seen")
        pool_seen = sem("pool_seen")
        shift_ready = sem("shift_ready")
        iota_ready = sem("iota_ready")
        x_loaded, xT_loaded, x_shifted = map(sem2, ("x_loaded", "xT_loaded", "x_shifted"))
        kT_done, kT_ready, v_done, v_ready = map(sem2, ("kT_done", "kT_ready", "v_done", "v_ready"))
        col_ready, q_gathered, qT_done, q_diag_ready = map(
            sem2, ("col_ready", "q_gathered", "qT_done", "q_diag_ready"))
        mean_done, mean_ready, place_ready = map(sem2, ("mean_done", "mean_ready", "place_ready"))
        scores_done, low_ready, probs_ready = map(sem2, ("scores_done", "low_ready", "probs_ready"))
        probs_turned, probsT_ready, o_done = map(sem2, ("probs_turned", "probsT_ready", "o_done"))
        o_rest_ready = sem2("o_rest_ready")
        o_step, o_placed, attn_ready, attn_turned, attnT_ready = map(
            sem2, ("o_step", "o_placed", "attn_ready", "attn_turned", "attnT_ready"))
        ao_done, ao_ready, z_ready = map(sem2, ("ao_done", "ao_ready", "z_ready"))
        ln_stats, ln_var, ln_eps, ln_root, ln_norm, ln_gain = map(
            sem2, ("ln_stats", "ln_var", "ln_eps", "ln_root", "ln_norm", "ln_gain"))
        h1_ready, h1_turned, h1T_ready, h1_shifted = map(sem2, ("h1_ready", "h1_turned", "h1T_ready", "h1_shifted"))
        ff_done, ff_act, ff_dve, y_done, z2_ready = map(sem2, ("ff_done", "ff_act", "ff_dve", "y_done", "z2_ready"))
        fused_ready, fused_turned, fusedT_ready = map(sem2, ("fused_ready", "fused_turned", "fusedT_ready"))
        conv_done, pooled_ready, yT_ready, y_turned, h_ready = map(
            sem2, ("conv_done", "pooled_ready", "yT_ready", "y_turned", "h_ready"))

        x_d = dram["x"].rearrange("b (t p) d -> b p t d", p=P)
        top_f32 = keep.top_f32[:, :].rearrange("p (b h) -> p b h", h=H0)
        top_row = keep.top_row[:, :].rearrange("p (b h) -> p b h", h=H0)

        loads = [(w_small[n][:, :], dram[n]) for n in w_small]
        loads += [(rows[n][:, :], dram[n].partition_broadcast(P)) for n in rows]
        loads += [(cols[n][:, :], dram[n].unsqueeze(1)) for n in cols]
        loads += [(f1_w[:, :], dram["f1_w"]),
                  (f1_b[:, :], dram["f1_b"]),
                  (f2_w[:, :, :], dram["f2_w"].rearrange("(c p) d -> p c d", p=P)),
                  (conv_w[:, :, :], dram["conv_w"])]
        ALL_WEIGHTS = 16 * len(loads)
        CONSTS = 10

        start_counts(nc, [*z_ready, *h_ready, *probs_ready, *probsT_ready, *probs_turned, *o_done,
                          *fused_ready, *fused_turned])

        FF_BANK = (0, 2, 3, 1)
        TURN_H1, FF_LOW, FF_HIGH, FF_DOWN, ADD_H1, NORM2_STATS, NORM2 = 1, 2, 3, 4, 5, 6, 7

        with nc.Block() as block:
            @block.sync
            def _(sp):
                for dst, src in loads:
                    sp.dma_start(dst, src).then_inc(weights, 16)
                for u in range(2):
                    sp.dma_start(xT[u][:, :], dram["xT"][u]).then_inc(xT_loaded[u], 16)
                    sp.dma_start(x_sb[u][:, :, :], x_d[u]).then_inc(x_loaded[u], 16)
                with sp.Fori(0, PAIRS - 1) as p:
                    for u in range(2):
                        sp.wait_ge(v_done[u], p + 1)
                        sp.dma_start(xT[u][:, :], dram["xT"][2 * p + 2 + u]).then_inc(xT_loaded[u], 16)
                        sp.wait_ge(x_shifted[u], p + 1)
                        sp.dma_start(x_sb[u][:, :, :], x_d[2 * p + 2 + u]).then_inc(x_loaded[u], 16)

            @block.gpsimd
            def _(pool):
                nc.gpsimd.memset(mean_w[:, :], 1.0 / L).then_inc(const, 1)
                nc.gpsimd.memset(half_neg[:, :], -0.5).then_inc(const, 1)
                nc.gpsimd.memset(eps[:, :], LN_EPS).then_inc(const, 1)
                for u in range(2):
                    nc.gpsimd.memset(v1[u][:, :, :, HD0:HD0 + 1], 1.0).then_inc(const, 1)
                    nc.gpsimd.memset(fusedT[u][:, 0:L + 2:L + 1], 0.0).then_inc(const, 1)
                nc.gpsimd.iota(iota_i[:, :], pattern=[[1, L]], base=0, channel_multiplier=0)\
                    .then_inc(iota_ready, 1)
                nc.gpsimd.memset(head_mask[:, :], -(float(HD0) ** -0.5)).then_inc(const, 1)
                pool.wait_ge(const, 8)
                nc.gpsimd.affine_select(out=head_mask[:, :], in_=head_mask[:, :], compare_op=ALU.is_ge,
                                        fill=0.0, base=0, pattern=[[-HD0, H0]],
                                        channel_multiplier=1).then_inc(const, 1)
                pool.wait_ge(const, 9)
                nc.gpsimd.affine_select(out=head_mask[:, :], in_=head_mask[:, :], compare_op=ALU.is_ge,
                                        fill=0.0, base=HD0 - 1, pattern=[[HD0, H0]],
                                        channel_multiplier=-1).then_inc(const, 1)
                pool.wait_ge(weights, ALL_WEIGHTS)
                nc.gpsimd.tensor_tensor(out_shift[:, :], rows["o_b"][:, :], rows["ln2_b"][:, :],
                                        ALU.add).then_inc(shift_ready, 1)

                def gather(u):
                    for h in range(H0):
                        pool.indirect_dma_start(
                            out=q_top[u][0:TOP, h * HD0:(h + 1) * HD0], out_offset=None, in_=dram["q_rows"],
                            in_offset=bass.IndirectOffsetOnAxis(ap=top_col[u][0:TOP, h:h + 1], axis=0),
                        ).then_inc(q_gathered[u], 16)

                def inverse_root(u, n):
                    pool.wait_ge(ln_var[u], LT * (n + 1))
                    nc.gpsimd.tensor_tensor(rstd[u][:, :], mean_var[u][:, :, 1], eps[:, :],
                                            ALU.add).then_inc(ln_eps[u], 1)
                    pool.wait_ge(ln_eps[u], n + 1)
                    nc.gpsimd.tensor_tensor(rstd[u][:, :], rstd[u][:, :], half_neg[:, :],
                                            ALU.pow).then_inc(ln_root[u], 1)

                def shift_x(u, p):
                    pool.wait_ge(x_loaded[u], 16 * p + 16)
                    pool.wait_ge(z_ready[u], START + p)
                    nc.gpsimd.tensor_tensor(x_shift[u][:, :, :], x_sb[u][:, :, :], per_tile(rows["o_b"]),
                                            ALU.add).then_inc(x_shifted[u], 1)

                def gather_next(u, p):
                    pool.wait_ge(q_gathered[u], 16 * H0 * (p + 1))
                    nc.gpsimd.tensor_copy(top_col[u][0:TOP, :], top_row[0:TOP, 2 * p + 2 + u, :])\
                        .then_inc(col_ready[u], 1)
                    pool.wait_ge(qT_done[u], p + 1)
                    pool.wait_ge(col_ready[u], p + 2)
                    stand_alone(pool, pool_seen)
                    gather(u)

                def gain_shift_1(u, p):
                    pool.wait_ge(ln_norm[u], LT * (2 * p + 1))
                    nc.gpsimd.tensor_tensor(h1[u][:, :, :], h1[u][:, :, :], per_tile(rows["ln1_g"]),
                                            ALU.mult).then_inc(ln_gain[u], 1)
                    pool.wait_ge(ln_gain[u], 2 * p + 1)
                    nc.gpsimd.tensor_tensor(h1[u][:, :, :], h1[u][:, :, :], per_tile(rows["ln1_b"]),
                                            ALU.add).then_inc(h1_ready[u], 1)

                def shift_h1(u, p):
                    pool.wait_ge(h1_ready[u], p + 1)
                    nc.gpsimd.tensor_tensor(z[u][:, :, :], h1[u][:, :, :], per_tile(rows["f2_b"]),
                                            ALU.add).then_inc(h1_shifted[u], 1)

                def gain_shift_2(u, p):
                    pool.wait_ge(ln_norm[u], LT * (2 * p + 2))
                    pool.wait_ge(h1_turned[u], p + 1)
                    nc.gpsimd.tensor_tensor(h1[u][:, :, :], h1[u][:, :, :], per_tile(rows["ln2_g"]),
                                            ALU.mult).then_inc(ln_gain[u], 1)
                    pool.wait_ge(ln_gain[u], 2 * p + 2)
                    nc.gpsimd.tensor_tensor(h1[u][:, :, :], h1[u][:, :, :], ao_shift[u][:, :, :],
                                            ALU.add).then_inc(fused_ready[u], 1)

                def turn(a, b):
                    if a:
                        shift_x(*a)
                    if b:
                        inverse_root(b[0], 2 * b[1])
                        gain_shift_1(*b)
                        shift_h1(*b)
                    if a:
                        gather_next(*a)
                    if b:
                        inverse_root(b[0], 2 * b[1] + 1)
                        gain_shift_2(*b)

                for u in range(2):
                    nc.gpsimd.tensor_copy(top_col[u][0:TOP, :], top_row[0:TOP, u, :]).then_inc(col_ready[u], 1)
                for u in range(2):
                    pool.wait_ge(col_ready[u], 1)
                    gather(u)
                turns(pool, turn)
                for u in range(2):
                    pool.wait_ge(q_gathered[u], 16 * H0 * (PAIRS + 1))

            @block.tensor
            def _(pe):
                def transpose(dst, src, n=LT):
                    for t in range(n):
                        ins = nc.tensor.transpose(dst[:, t * P:(t + 1) * P], src[:, t, :], keep.ident[:, :])
                    return ins

                def project(u, p):
                    pe.wait_ge(xT_loaded[u], 16 * p + 16)
                    nc.tensor.matmul(bank[u][1][:, :], w_small["k_w"][:, :], xT[u][:, :], start=True,
                                     stop=True).then_inc(kT_done[u], 1)
                    for t in range(LT):
                        ins = nc.tensor.matmul(bank[u][2][:, t * P:(t + 1) * P], xT[u][:, t * P:(t + 1) * P],
                                               w_small["v_w"][:, :], start=True, stop=True)
                    ins.then_inc(v_done[u], 1)

                def turn_queries(u, p):
                    pe.wait_ge(q_gathered[u], 16 * H0 * (p + 1))
                    nc.tensor.transpose(bank[u][0][:, 0:TOP], q_top[u][0:TOP, :],
                                        keep.ident[0:TOP, 0:TOP]).then_inc(qT_done[u], 1)

                def mean_value(u, p):
                    pe.wait_ge(v_ready[u], p + 1)
                    pe.wait_ge(h_ready[u], START + p)
                    for t in range(LT):
                        ins = nc.tensor.matmul(bank[u][3][:, 0:D], mean_w[:, :], v1[u][:, t, :, 0:HD0],
                                               start=(t == 0), stop=(t == LT - 1))
                    ins.then_inc(mean_done[u], 1)

                def score(u, p, h):
                    if h == 0:
                        pe.wait_ge(q_diag_ready[u], p + 1)
                        pe.wait_ge(kT_ready[u], p + 1)
                    if h >= 2:
                        pe.wait_ge(probs_ready[u], START + H0 * p + h - 1)
                    nc.tensor.matmul(bank[u][h % 2][0:TOP, :], q_diag[u][:, h, :], kT[u][:, :],
                                     start=True, stop=True).then_inc(scores_done[u], 1)

                def turn_probs(u, p, h):
                    pe.wait_ge(probs_ready[u], START + H0 * p + h + 1)
                    if h:
                        pe.wait_ge(probsT_ready[u], START + H0 * p + h)
                    for t in range(LT):
                        ins = nc.tensor.transpose(bank[u][2][:, t * TOP:(t + 1) * TOP],
                                                  probs[u][0:TOP, h % 2, t * P:(t + 1) * P],
                                                  keep.ident[0:TOP, 0:TOP])
                    ins.then_inc(probs_turned[u], 1)

                def sum_values(u, p, h):
                    if h == 0:
                        pe.wait_ge(mean_ready[u], p + 1)
                    pe.wait_ge(probsT_ready[u], START + H0 * p + h + 1)
                    for t in range(LT):
                        ins = nc.tensor.matmul(bank[u][3][0:TOP, h * (HD0 + 1):(h + 1) * (HD0 + 1)],
                                               probsT[u][:, h % 2, t, :], v1[u][:, t, h, :],
                                               start=(t == 0), stop=(t == LT - 1))
                    ins.then_inc(o_done[u], 1)

                def place_outputs(u, p):
                    pe.wait_ge(place_ready[u], H0 * (p + 1))
                    pe.wait_ge(o_step[u], 6 * (p + 1))
                    for t in range(LT):
                        for h in range(H0):
                            for k in range(3):
                                ins = nc.tensor.matmul(
                                    bank[u][0][:, t * P + h * HD0:t * P + (h + 1) * HD0],
                                    place[u][0:TOP, h, t * P:(t + 1) * P],
                                    o_part[u][0:TOP, k, h * HD0:(h + 1) * HD0], start=(k == 0), stop=(k == 2))
                    ins.then_inc(o_placed[u], 1)

                def turn_attention(u, p):
                    pe.wait_ge(attn_ready[u], p + 1)
                    transpose(bank[u][1], attn[u]).then_inc(attn_turned[u], 1)

                def project_out(u, p):
                    pe.wait_ge(attnT_ready[u], p + 1)
                    for t in range(LT):
                        ins = nc.tensor.matmul(bank[u][2][:, t * P:(t + 1) * P], attnT[u][:, t * P:(t + 1) * P],
                                               w_small["o_w"][:, :], start=True, stop=True)
                    ins.then_inc(ao_done[u], 1)

                def turn_h1(u, p):
                    pe.wait_ge(h1_ready[u], p + 1)
                    transpose(bank[u][1], h1[u]).then_inc(h1_turned[u], 1)

                def up(u, p, chunks):
                    pe.wait_ge(h1T_ready[u], p + 1)
                    for c in chunks:
                        nc.tensor.matmul(bank[u][FF_BANK[c]][:, :], f1_w[:, c * P:(c + 1) * P], h1T[u][:, :],
                                         start=True, stop=True).then_inc(ff_done[u], 1)

                def down(u, p):
                    pe.wait_ge(ff_act[u], 2 * p + 2)
                    pe.wait_ge(ff_dve[u], 2 * p + 2)
                    for t in range(LT):
                        for c in range(FC):
                            ins = nc.tensor.matmul(bank[u][0][:, t * P:(t + 1) * P],
                                                   ff[u][:, c, t * P:(t + 1) * P], f2_w[:, c, :],
                                                   start=(c == 0), stop=(c == FC - 1))
                    ins.then_inc(y_done[u], 1)

                def turn_fused(u, p):
                    pe.wait_ge(fused_ready[u], START + p + 1)
                    transpose(bank[u][2], h1[u]).then_inc(fused_turned[u], 1)

                def convolve(u, p):
                    pe.wait_ge(fusedT_ready[u], p + 1)
                    for k in range(3):
                        ins = nc.tensor.matmul(bank[u][3][:, :], conv_w[:, k, :], fusedT[u][:, k:k + L],
                                               start=(k == 0), stop=(k == 2))
                    ins.then_inc(conv_done[u], 1)

                def turn_pooled(u, p):
                    pe.wait_ge(yT_ready[u], p + 1)
                    for t in range(PT):
                        ins = nc.tensor.transpose(bank[u][3][:, t * P:(t + 1) * P],
                                                  yT[u][:, t * P:(t + 1) * P], keep.ident[:, :])
                    ins.then_inc(y_turned[u], 1)

                def turn(a, b):
                    if a:
                        turn_queries(*a)
                        project(*a)
                    for s in range(H0 + 2):
                        if a and s < H0:
                            score(*a, s)
                        if a and s == 1:
                            mean_value(*a)
                        if a and 1 <= s <= H0:
                            turn_probs(*a, s - 1)
                        if a and s >= 2:
                            sum_values(*a, s - 2)
                        if b and s == TURN_H1:
                            turn_h1(*b)
                        if b and s == FF_LOW:
                            up(*b, (0, 1))
                        if b and s == FF_HIGH:
                            up(*b, (2, 3))
                        if b and s == FF_DOWN:
                            down(*b)
                    if a:
                        place_outputs(*a)
                    if b:
                        turn_fused(*b)
                    if a:
                        turn_attention(*a)
                    if b:
                        convolve(*b)
                    if a:
                        project_out(*a)
                    if b:
                        turn_pooled(*b)

                pe.wait_ge(weights, ALL_WEIGHTS)
                pe.wait_ge(const, CONSTS)
                turns(pe, turn)

            @block.scalar
            def _(act):
                def copy_kT(u, p):
                    act.wait_ge(kT_done[u], p + 1)
                    nc.scalar.activation(kT[u][:, :], bank[u][1][:, :], ACT.Identity,
                                         bias=cols["k_b"][:, 0:1]).then_inc(kT_ready[u], 1)

                def copy_mean(u, p):
                    act.wait_ge(mean_done[u], p + 1)
                    nc.scalar.copy(v_mean[u][:, :], bank[u][3][:, 0:D]).then_inc(mean_ready[u], 1)

                def raise_scores(u, p, h):
                    act.wait_ge(low_ready[u], H0 * p + h + 1)
                    if h >= 2:
                        act.wait_ge(probs_turned[u], START + H0 * p + h - 1)
                    nc.scalar.activation(probs[u][0:TOP, h % 2, :], bank[u][h % 2][0:TOP, :], ACT.Exp,
                                         bias=low[u][0:TOP, h:h + 1], scale=-1.0).then_inc(probs_ready[u], 1)

                def copy_probsT(u, p, h):
                    act.wait_ge(probs_turned[u], START + H0 * p + h + 1)
                    if h >= 2:
                        act.wait_ge(o_done[u], START + H0 * p + h - 1)
                    nc.scalar.copy(probsT[u][:, h % 2, :, :].rearrange("p t r -> p (t r)"),
                                   bank[u][2][:, 0:LT * TOP]).then_inc(probsT_ready[u], 1)

                def copy_attnT(u, p):
                    act.wait_ge(attn_turned[u], p + 1)
                    nc.scalar.copy(attnT[u][:, :], bank[u][1][:, :]).then_inc(attnT_ready[u], 1)

                def copy_h1T(u, p):
                    act.wait_ge(h1_turned[u], p + 1)
                    nc.scalar.copy(h1T[u][:, :], bank[u][1][:, :]).then_inc(h1T_ready[u], 1)

                def rectify(u, p, c):
                    act.wait_ge(ff_done[u], FC * p + c + 1)
                    nc.scalar.activation(ff[u][:, c, :], bank[u][FF_BANK[c]][:, :], ACT.Relu,
                                         bias=f1_b[:, c:c + 1]).then_inc(ff_act[u], 1)

                def copy_fusedT(u, p):
                    act.wait_ge(fused_turned[u], START + p + 1)
                    nc.scalar.copy(fusedT[u][:, 1:L + 1], bank[u][2][:, :]).then_inc(fusedT_ready[u], 1)

                def rectify_pooled(u, p):
                    act.wait_ge(pooled_ready[u], p + 1)
                    nc.scalar.activation(yT[u][:, :], pooled[u][:, :], ACT.Relu,
                                         bias=cols["conv_b"][:, 0:1]).then_inc(yT_ready[u], 1)

                def copy_h(u, p):
                    act.wait_ge(y_turned[u], p + 1)
                    nc.scalar.copy(keep.h[:, 2 * p + u, :, :].rearrange("p t d -> p (t d)"),
                                   bank[u][3][:, 0:LP]).then_inc(h_ready[u], 1)

                def turn(a, b):
                    if a:
                        copy_kT(*a)
                    for s in range(H0 + 1):
                        if a and s < H0:
                            raise_scores(*a, s)
                        if a and s == 1:
                            copy_mean(*a)
                        if a and s >= 1:
                            copy_probsT(*a, s - 1)
                        if b and s == TURN_H1:
                            copy_h1T(*b)
                        if b and s == FF_LOW:
                            rectify(*b, 0)
                        if b and s == FF_HIGH:
                            rectify(*b, 2)
                    if b:
                        copy_fusedT(*b)
                    if a:
                        copy_attnT(*a)
                    if b:
                        rectify_pooled(*b)
                    if b:
                        copy_h(*b)

                act.wait_ge(weights, ALL_WEIGHTS)
                turns(act, turn)

            @block.vector
            def _(dve):
                def statistics(u, n):
                    for t in range(LT):
                        nc.vector.bn_stats(stats[u][:, t, :], z[u][:, t, :]).then_inc(ln_stats[u], 1)

                def mean_variance(u, n):
                    dve.wait_ge(ln_stats[u], LT * (n + 1))
                    stand_alone(dve, dve_seen)
                    for t in range(LT):
                        nc.vector.bn_aggr(mean_var[u][:, t, :], stats[u][:, t, :]).then_inc(ln_var[u], 1)

                def normalize(u, n):
                    dve.wait_ge(ln_root[u], n + 1)
                    for t in range(LT):
                        nc.vector.tensor_scalar(h1[u][:, t, :], z[u][:, t, :], mean_var[u][:, t, 0:1],
                                                rstd[u][:, t:t + 1], ALU.subtract, ALU.mult)\
                            .then_inc(ln_norm[u], 1)

                def mark_place(u, p, h):
                    nc.vector.tensor_scalar(place[u][0:TOP, h, :], iota_h[0:TOP, :],
                                            top_f32[0:TOP, 2 * p + u, h:h + 1], None,
                                            ALU.is_equal).then_inc(place_ready[u], 1)

                def shift_v(u, p):
                    dve.wait_ge(v_done[u], p + 1)
                    nc.vector.tensor_tensor(
                        v1[u][:, :, :, 0:HD0],
                        bank[u][2][:, :].rearrange("p (t h c) -> p t h c", t=LT, h=H0),
                        rows["v_b"][:, :].rearrange("p (h c) -> p h c", h=H0).unsqueeze(1)
                        .broadcast_to([P, LT, H0, HD0]), ALU.add).then_inc(v_ready[u], 1)

                def spread_queries(u, p):
                    dve.wait_ge(qT_done[u], p + 1)
                    nc.vector.tensor_tensor(
                        q_diag[u][:, :, :], bank[u][0][:, 0:TOP].unsqueeze(1).broadcast_to([P, H0, TOP]),
                        head_mask[:, :].unsqueeze(2).broadcast_to([P, H0, TOP]),
                        ALU.mult).then_inc(q_diag_ready[u], 1)

                def least_score(u, p, h):
                    dve.wait_ge(scores_done[u], H0 * p + h + 1)
                    nc.vector.tensor_reduce(low[u][0:TOP, h:h + 1], bank[u][h % 2][0:TOP, :], AX.X,
                                            ALU.min).then_inc(low_ready[u], 1)

                def divide(u, p):
                    sums = bank[u][3][0:TOP, 0:H0 * (HD0 + 1)].rearrange("p (h c) -> p h c", h=H0)
                    top3 = o_top[u][0:TOP, :, :]
                    rest3 = o_rest[u][0:TOP, :, :]

                    def part(k):
                        return o_part[u][0:TOP, k, :].rearrange("p (h c) -> p h c", h=H0)

                    dve.wait_ge(o_done[u], START + H0 * (p + 1))
                    nc.vector.reciprocal(o_scale[u][0:TOP, :], sums[:, :, HD0]).then_inc(o_step[u], 1)
                    dve.wait_ge(o_step[u], 6 * p + 1)
                    nc.vector.tensor_tensor(top3, sums[:, :, 0:HD0],
                                            o_scale[u][0:TOP, :].unsqueeze(2).broadcast_to([TOP, H0, HD0]),
                                            ALU.mult).then_inc(o_step[u], 1)
                    dve.wait_ge(o_step[u], 6 * p + 2)
                    dve.wait_ge(mean_ready[u], p + 1)
                    nc.vector.tensor_tensor(top3, top3,
                                            v_mean[u][0:TOP, :].rearrange("p (h c) -> p h c", h=H0),
                                            ALU.subtract).then_inc(o_step[u], 1)
                    dve.wait_ge(o_step[u], 6 * p + 3)
                    nc.vector.tensor_copy(part(0), top3).then_inc(o_step[u], 1)
                    dve.wait_ge(o_step[u], 6 * p + 4)
                    nc.vector.tensor_tensor(rest3, top3, part(0), ALU.subtract).then_inc(o_rest_ready[u], 1)
                    dve.wait_ge(o_rest_ready[u], p + 1)
                    nc.vector.tensor_copy(part(1), rest3).then_inc(o_step[u], 1)
                    dve.wait_ge(o_step[u], 6 * p + 5)
                    nc.vector.tensor_tensor(part(2), rest3, part(1), ALU.subtract).then_inc(o_step[u], 1)

                def add_mean(u, p):
                    dve.wait_ge(o_placed[u], p + 1)
                    nc.vector.tensor_tensor(attn[u][:, :, :], tiles(bank[u][0][:, :]), per_tile(v_mean[u]),
                                            ALU.add).then_inc(attn_ready[u], 1)

                def add_x(u, p):
                    dve.wait_ge(ao_done[u], p + 1)
                    dve.wait_ge(x_shifted[u], p + 1)
                    nc.vector.tensor_tensor(z[u][:, :, :], tiles(bank[u][2][:, :]), x_shift[u][:, :, :],
                                            ALU.add).then_inc(z_ready[u], 1)
                    dve.wait_ge(fused_ready[u], START + p)
                    nc.vector.tensor_tensor(ao_shift[u][:, :, :], tiles(bank[u][2][:, :]), per_tile(out_shift),
                                            ALU.add).then_inc(ao_ready[u], 1)

                def rectify(u, p, c):
                    dve.wait_ge(ff_done[u], FC * p + c + 1)
                    nc.vector.tensor_scalar(ff[u][:, c, :], bank[u][FF_BANK[c]][:, :], f1_b[:, c:c + 1], 0.0,
                                            ALU.add, ALU.max).then_inc(ff_dve[u], 1)

                def add_h1(u, p):
                    dve.wait_ge(y_done[u], p + 1)
                    dve.wait_ge(h1_shifted[u], p + 1)
                    nc.vector.tensor_tensor(z[u][:, :, :], tiles(bank[u][0][:, :]), z[u][:, :, :],
                                            ALU.add).then_inc(z2_ready[u], 1)

                def pool_pairs(u, p):
                    dve.wait_ge(conv_done[u], p + 1)
                    nc.vector.tensor_reduce(pooled[u][:, :], bank[u][3][:, :].rearrange("p (l a) -> p l a", a=2),
                                            AX.X, ALU.max).then_inc(pooled_ready[u], 1)

                def turn(a, b):
                    if b:
                        dve.wait_ge(z_ready[b[0]], START + b[1] + 1)
                        statistics(b[0], 2 * b[1])
                        mean_variance(b[0], 2 * b[1])
                    if a:
                        spread_queries(*a)
                        shift_v(*a)
                    if b:
                        dve.wait_ge(fused_turned[b[0]], START + b[1])
                        normalize(b[0], 2 * b[1])
                    for s in range(H0 + 1):
                        if a and s < H0:
                            least_score(*a, s)
                            mark_place(*a, s)
                        if b and s == FF_LOW:
                            rectify(*b, 1)
                        if b and s == FF_HIGH:
                            rectify(*b, 3)
                        if b and s == ADD_H1:
                            add_h1(*b)
                        if b and s == NORM2_STATS:
                            dve.wait_ge(z2_ready[b[0]], b[1] + 1)
                            statistics(b[0], 2 * b[1] + 1)
                            mean_variance(b[0], 2 * b[1] + 1)
                        if b and s == NORM2:
                            normalize(b[0], 2 * b[1] + 1)
                    if a:
                        divide(*a)
                    if a:
                        add_mean(*a)
                    if b:
                        pool_pairs(*b)
                    if a:
                        add_x(*a)

                dve.wait_ge(iota_ready, 1)
                nc.vector.tensor_copy(iota_h[:, :], iota_i[:, :]).then_inc(iota_ready, 1)
                dve.wait_ge(iota_ready, 2)
                dve.wait_ge(weights, ALL_WEIGHTS)
                dve.wait_ge(shift_ready, 1)
                dve.wait_ge(const, CONSTS)
                turns(dve, turn)
        nc.clear_and_free_semaphores(sems)
        nc.all_engine_barrier()


H1, HD1 = 8, 64
HALF = HD1 // 2
W1 = H1 * HD1
WC = W1 // P
WIN = 128
RMS_EPS = 1e-6
MASKED = -1e30
LEAST = -3e38


def windowed_attention(nc, dram, keep):
    sems = []
    with ExitStack() as ctx:
        def sb(name, shape, dt=F32):
            return ctx.enter_context(nc.sbuf_tensor("w_" + name, shape, dt))

        def two(name, shape, dt=F32):
            return [sb(f"{name}{u}", shape, dt) for u in range(2)]

        def sem(name):
            sems.append(nc.alloc_semaphore("w_" + name))
            return sems[-1]

        def sem2(name):
            return [sem(f"{name}{u}") for u in range(2)]

        w_qkv = [sb(n, [P, W1]) for n in ("W_q", "W_k", "W_v")]
        w_out = sb("W_o", [P, WC, D])
        rope = sb("rope", [P, 2, PT, HD1])
        norm_w = sb("norm_w", [P, 2, HD1])
        cos_w = sb("cos_w", [P, 2, PT, HD1])
        sin_w = sb("sin_w", [P, 2, PT, HD1])
        win_mask = sb("win_mask", [P, 3 * P])
        half_neg = sb("half_neg", [P, 4 * H1])
        eps = sb("eps", [P, PT])
        rms_eps = sb("rms_eps", [P, 4 * H1])

        stats = two("stats", [P, PT, 6])
        mean_var = two("mean_var", [P, PT, 2])
        rstd = two("rstd", [P, PT])
        hn = two("hn", [P, PT, D])
        hnT = two("hnT", [P, LP])
        v_sb = two("v", [P, PT, W1])
        squares = two("squares", [P, 2, H1, HD1])
        sum_sq = two("sum_sq", [P, PT, 2, H1])
        root = two("root", [P, PT, 2, H1])
        t1 = two("t1", [P, 2, H1, HD1])
        t2 = two("t2", [P, 2, H1, HD1])
        qk = two("qk", [P, PT, 2, W1])
        qkT = two("qkT", [P, 2, WC, LP])
        masked = two("masked", [P, 2, 3 * P])
        top = two("top", [P, H1, PT])
        bias = two("bias", [P, H1, PT])
        probs = two("probs", [P, 2, 3 * P])
        probsT = two("probsT", [P, 2, 3 * P])
        total = two("total", [P, PT, H1])
        scale = two("scale", [P, PT, H1])
        o_sb = two("o", [P, PT, W1])
        oT = two("oT", [P, PT, WC, P])

        bank = [[ctx.enter_context(nc.psum_tensor(f"w_bank{u}{k}", [P, 512], F32)) for k in range(4)]
                for u in range(2)]

        weights = sem("weights")
        const = sem("const")
        dve_seen = sem("dve_seen")
        tables = sem("tables")
        ln_stats, ln_var, ln_eps, ln_root, hn_ready = map(
            sem2, ("ln_stats", "ln_var", "ln_eps", "ln_root", "hn_ready"))
        hn_turned, hnT_ready, qkv_done, v_copied = map(sem2, ("hn_turned", "hnT_ready", "qkv_done", "v_copied"))
        squared, summed, rotated, added, root_eps, root_ready, k_scaled = map(
            sem2, ("squared", "summed", "rotated", "added", "root_eps", "root_ready", "k_scaled"))
        qk_turned, qkT_ready = map(sem2, ("qk_turned", "qkT_ready"))
        scores_done, masked_ready, bias_ready, probs_ready = map(
            sem2, ("scores_done", "masked_ready", "bias_ready", "probs_ready"))
        probs_turned, probsT_ready, o_done = map(sem2, ("probs_turned", "probsT_ready", "o_done"))
        scale_ready, o_ready, o_turned, oT_ready, out_done, h_ready = map(
            sem2, ("scale_ready", "o_ready", "o_turned", "oT_ready", "out_done", "h_ready"))

        loads = [(w[:, :], dram[n]) for w, n in zip(w_qkv, ("W_q", "W_k", "W_v"))]
        loads += [(w_out[:, :, :], dram["W_o"].rearrange("(c p) d -> p c d", p=P))]
        loads += [(rope[:, i, :, :], dram[n][0:LP, :].rearrange("(t p) c -> p t c", p=P))
                  for i, n in enumerate(("rope_cos", "rope_sin"))]
        loads += [(norm_w[:, i, :], dram[n].partition_broadcast(P))
                  for i, n in enumerate(("q_norm_w", "k_norm_w"))]
        ALL_WEIGHTS = 16 * len(loads)
        CONSTS = 7
        TABLES = 7
        PRODUCTS = ((0, 0, 1), (0, 1, 2), (0, 2, 3), (1, 0, 0), (1, 1, 1), (1, 2, 2))
        QK = [(n, t, w, k) for n, (t, w, k) in enumerate(PRODUCTS) if w < 2]

        start_counts(nc, [*h_ready, *masked_ready, *probsT_ready, *summed, *probs_turned, *o_done, *added,
                          *probs_ready])

        NORM, TURN_HN = 0, 1
        PRODUCTS_AT = (2, 2, 3, 3, 5, 6)
        SQUARES_AT = (2, 3, 3, 4, 5, 6)
        ROTARY_AT = (3, 4, 5, 6)
        TURN_Q = 8

        with nc.Block() as block:
            @block.sync
            def _(sp):
                for dst, src in loads:
                    sp.dma_start(dst, src).then_inc(weights, 16)
                sp.wait_ge(weights, ALL_WEIGHTS)

            @block.gpsimd
            def _(pool):
                nc.gpsimd.memset(half_neg[:, :], -0.5).then_inc(const, 1)
                nc.gpsimd.memset(eps[:, :], LN_EPS).then_inc(const, 1)
                nc.gpsimd.memset(rms_eps[:, :], HD1 * RMS_EPS).then_inc(const, 1)
                nc.gpsimd.memset(win_mask[:, :], 0.0).then_inc(const, 1)
                pool.wait_ge(const, 4)
                nc.gpsimd.affine_select(out=win_mask[:, 0:P], in_=win_mask[:, 0:P], compare_op=ALU.is_ge,
                                        fill=MASKED, base=0, pattern=[[-1, P]],
                                        channel_multiplier=1).then_inc(const, 1)
                nc.gpsimd.affine_select(out=win_mask[:, P:], in_=win_mask[:, P:], compare_op=ALU.is_ge,
                                        fill=MASKED, base=P, pattern=[[-1, 2 * P]],
                                        channel_multiplier=1).then_inc(const, 1)
                pool.wait_ge(const, 6)
                nc.gpsimd.affine_select(out=win_mask[:, P:], in_=win_mask[:, P:], compare_op=ALU.is_ge,
                                        fill=MASKED, base=WIN - 1 - P, pattern=[[1, 2 * P]],
                                        channel_multiplier=-1).then_inc(const, 1)
                pool.wait_ge(weights, ALL_WEIGHTS)
                nc.gpsimd.tensor_scalar(norm_w[:, 1, :], norm_w[:, 1, :], float(HD1) ** 0.5, 1.0, ALU.mult,
                                        ALU.mult).then_inc(tables, 1)
                pool.wait_ge(tables, 1)
                for i in range(2):
                    def over_tiles(lo, hi):
                        return norm_w[:, i, lo:hi].unsqueeze(1).broadcast_to([P, PT, hi - lo])

                    nc.gpsimd.tensor_tensor(cos_w[:, i, :, :], rope[:, 0, :, :], over_tiles(0, HD1),
                                            ALU.mult).then_inc(tables, 1)
                    nc.gpsimd.tensor_tensor(sin_w[:, i, :, 0:HALF], rope[:, 1, :, 0:HALF], over_tiles(HALF, HD1),
                                            ALU.mult).then_inc(tables, 1)
                    nc.gpsimd.tensor_tensor(sin_w[:, i, :, HALF:], rope[:, 1, :, HALF:], over_tiles(0, HALF),
                                            ALU.mult).then_inc(tables, 1)
                pool.wait_ge(tables, TABLES)
                nc.gpsimd.tensor_scalar(sin_w[:, :, :, 0:HALF], sin_w[:, :, :, 0:HALF], -1.0, 1.0, ALU.mult,
                                        ALU.mult).then_inc(tables, 1)
                def inverse_deviation(u, p):
                    pool.wait_ge(ln_var[u], PT * (p + 1))
                    nc.gpsimd.tensor_tensor(rstd[u][:, :], mean_var[u][:, :, 1], eps[:, :],
                                            ALU.add).then_inc(ln_eps[u], 1)
                    pool.wait_ge(ln_eps[u], p + 1)
                    nc.gpsimd.tensor_tensor(rstd[u][:, :], rstd[u][:, :], half_neg[:, 0:PT],
                                            ALU.pow).then_inc(ln_root[u], 1)

                def add_rotated(u, p, i):
                    _, t, w, _ = QK[i]
                    pool.wait_ge(rotated[u], 12 * p + 3 * i + 3)
                    nc.gpsimd.tensor_tensor(
                        qk[u][:, t, w, :], t1[u][:, i % 2, :, :].rearrange("p h c -> p (h c)"),
                        t2[u][:, i % 2, :, :].rearrange("p h c -> p (h c)"), ALU.add).then_inc(added[u], 1)

                def inverse_norms(u, p):
                    pool.wait_ge(summed[u], START + 4 * (p + 1))
                    nc.gpsimd.tensor_tensor(
                        root[u][:, :, :, :].rearrange("p t w h -> p (t w h)"),
                        sum_sq[u][:, :, :, :].rearrange("p t w h -> p (t w h)"), rms_eps[:, :],
                        ALU.add).then_inc(root_eps[u], 1)
                    pool.wait_ge(root_eps[u], p + 1)
                    nc.gpsimd.tensor_tensor(
                        root[u][:, :, :, :].rearrange("p t w h -> p (t w h)"),
                        root[u][:, :, :, :].rearrange("p t w h -> p (t w h)"), half_neg[:, :],
                        ALU.pow).then_inc(root_ready[u], 1)

                def turn(a, b):
                    if a:
                        inverse_deviation(*a)
                        for i in range(4):
                            add_rotated(*a, i)
                        inverse_norms(*a)

                turns(pool, turn)

            @block.tensor
            def _(pe):
                def turn_hn(u, p):
                    pe.wait_ge(hn_ready[u], PT * (p + 1))
                    for t in range(PT):
                        ins = nc.tensor.transpose(bank[u][0][:, t * P:(t + 1) * P], hn[u][:, t, :],
                                                  keep.ident[:, :])
                    ins.then_inc(hn_turned[u], 1)

                def project(u, p, n):
                    t, w, k = PRODUCTS[n]
                    if n == 0:
                        pe.wait_ge(hnT_ready[u], p + 1)
                        pe.wait_ge(h_ready[u], START + p)
                    if n == 4:
                        pe.wait_ge(rotated[u], 12 * p + 3)
                        pe.wait_ge(squared[u], 4 * p + 1)
                    if n == 5:
                        pe.wait_ge(rotated[u], 12 * p + 6)
                        pe.wait_ge(squared[u], 4 * p + 2)
                    nc.tensor.matmul(bank[u][k][:, :], hnT[u][:, t * P:(t + 1) * P], w_qkv[w][:, :],
                                     start=True, stop=True).then_inc(qkv_done[u], 1)

                def turn_qk(u, p, i):
                    t, w = i % 2, i // 2
                    if i == 0:
                        pe.wait_ge(added[u], START + 4 * (p + 1))
                        pe.wait_ge(squared[u], 4 * (p + 1))
                        pe.wait_ge(v_copied[u], 2 * (p + 1))
                    if w == 1:
                        pe.wait_ge(k_scaled[u], 2 * p + t + 1)
                    for c in range(WC):
                        ins = nc.tensor.transpose(bank[u][i][:, c * P:(c + 1) * P],
                                                  qk[u][:, t, w, c * P:(c + 1) * P], keep.ident[:, :])
                    ins.then_inc(qk_turned[u], 1)

                def score(u, p, h):
                    if h == 0:
                        pe.wait_ge(qkT_ready[u], 4 * (p + 1))
                    else:
                        pe.wait_ge(masked_ready[u], START + 2 * (H1 * p + h))
                    c, lo = h // 2, HD1 * (h % 2)
                    q, k = (qkT[u][lo:lo + HD1, w, c, :] for w in range(2))
                    nc.tensor.matmul(bank[u][0][:, 0:P], q[:, 0:P], k[:, 0:P], start=True, stop=True)
                    nc.tensor.matmul(bank[u][0][:, P:3 * P], q[:, P:], k[:, :], start=True,
                                     stop=True).then_inc(scores_done[u], 1)

                def turn_probs(u, p, h):
                    pe.wait_ge(probs_ready[u], START + 2 * (H1 * p + h + 1))
                    if h:
                        pe.wait_ge(probsT_ready[u], START + H1 * p + h)
                    for j in range(3):
                        ins = nc.tensor.transpose(bank[u][1][:, j * P:(j + 1) * P],
                                                  probs[u][:, h % 2, j * P:(j + 1) * P], keep.ident[:, :])
                    ins.then_inc(probs_turned[u], 1)

                def sum_values(u, p, h):
                    pe.wait_ge(probsT_ready[u], START + H1 * p + h + 1)
                    cols = slice(h * HD1, (h + 1) * HD1)
                    for j, (t, kt) in enumerate(((0, 0), (1, 0), (1, 1))):
                        ins = nc.tensor.matmul(bank[u][2 + t][:, cols], probsT[u][:, h % 2, j * P:(j + 1) * P],
                                               v_sb[u][:, kt, cols], start=(kt == 0), stop=(j != 1))
                    ins.then_inc(o_done[u], 1)

                def turn_outputs(u, p, t):
                    pe.wait_ge(o_ready[u], PT * p + t + 1)
                    for c in range(WC):
                        ins = nc.tensor.transpose(bank[u][t][:, c * P:(c + 1) * P],
                                                  o_sb[u][:, t, c * P:(c + 1) * P], keep.ident[:, :])
                    ins.then_inc(o_turned[u], 1)

                def project_out(u, p):
                    pe.wait_ge(oT_ready[u], PT * (p + 1))
                    for t in range(PT):
                        for c in range(WC):
                            ins = nc.tensor.matmul(bank[u][2][:, t * P:(t + 1) * P], oT[u][:, t, c, :],
                                                   w_out[:, c, :], start=(c == 0), stop=(c == WC - 1))
                    ins.then_inc(out_done[u], 1)

                def turn(a, b):
                    for s in range(H1 + 2):
                        if b and s < H1:
                            score(*b, s)
                        if b and 1 <= s <= H1:
                            turn_probs(*b, s - 1)
                        if b and s >= 2:
                            sum_values(*b, s - 2)
                        if a and s == TURN_HN:
                            turn_hn(*a)
                        for n in range(len(PRODUCTS)):
                            if a and s == PRODUCTS_AT[n]:
                                project(*a, n)
                        if a and s == TURN_Q:
                            turn_qk(*a, 0)
                            turn_qk(*a, 1)
                    if b:
                        turn_outputs(*b, 0)
                        turn_outputs(*b, 1)
                    if a:
                        turn_qk(*a, 2)
                        turn_qk(*a, 3)
                    if b:
                        project_out(*b)

                pe.wait_ge(weights, ALL_WEIGHTS)
                turns(pe, turn)

            @block.scalar
            def _(act):
                def copy_hnT(u, p):
                    act.wait_ge(hn_turned[u], p + 1)
                    nc.scalar.copy(hnT[u][:, :], bank[u][0][:, 0:LP]).then_inc(hnT_ready[u], 1)

                def square_or_copy(u, p, n):
                    t, w, k = PRODUCTS[n]
                    act.wait_ge(qkv_done[u], 6 * p + n + 1)
                    if w == 2:
                        nc.scalar.copy(v_sb[u][:, t, :], bank[u][k][:, :]).then_inc(v_copied[u], 1)
                    else:
                        i = PT * t + w
                        if i >= 2:
                            act.wait_ge(summed[u], START + 4 * p + i - 1)
                        nc.scalar.activation(squares[u][:, i % 2, :, :].rearrange("p h c -> p (h c)"),
                                             bank[u][k][:, :], ACT.Square).then_inc(squared[u], 1)

                def copy_qkT(u, p, i):
                    t, w = i % 2, i // 2
                    act.wait_ge(qk_turned[u], 4 * p + i + 1)
                    nc.scalar.copy(qkT[u][:, w, :, t * P:(t + 1) * P],
                                   bank[u][i][:, :].rearrange("p (c l) -> p c l", c=WC)).then_inc(qkT_ready[u], 1)

                def raise_scores(u, p, h):
                    act.wait_ge(bias_ready[u], H1 * p + h + 1)
                    if h >= 2:
                        act.wait_ge(probs_turned[u], START + H1 * p + h - 1)
                    for t, cols in enumerate((slice(0, P), slice(P, 3 * P))):
                        nc.scalar.activation(probs[u][:, h % 2, cols], masked[u][:, h % 2, cols], ACT.Exp,
                                             bias=bias[u][:, h, t:t + 1], scale=root[u][:, t, 0, h:h + 1],
                                             accum_out=total[u][:, t, h:h + 1]).then_inc(probs_ready[u], 1)

                def copy_probsT(u, p, h):
                    act.wait_ge(probs_turned[u], START + H1 * p + h + 1)
                    if h >= 2:
                        act.wait_ge(o_done[u], START + H1 * p + h - 1)
                    nc.scalar.copy(probsT[u][:, h % 2, :], bank[u][1][:, 0:3 * P]).then_inc(probsT_ready[u], 1)

                def copy_oT(u, p, t):
                    act.wait_ge(o_turned[u], PT * p + t + 1)
                    nc.scalar.copy(oT[u][:, t, :, :].rearrange("p c l -> p (c l)"),
                                   bank[u][t][:, :]).then_inc(oT_ready[u], 1)

                def turn(a, b):
                    for s in range(H1 + 1):
                        if b and s < H1:
                            raise_scores(*b, s)
                        if b and s >= 1:
                            copy_probsT(*b, s - 1)
                        if a and s == TURN_HN:
                            copy_hnT(*a)
                        for n in range(len(PRODUCTS)):
                            if a and s == SQUARES_AT[n]:
                                square_or_copy(*a, n)
                        if a and s == TURN_Q:
                            copy_qkT(*a, 0)
                            copy_qkT(*a, 1)
                    if b:
                        copy_oT(*b, 0)
                        copy_oT(*b, 1)
                    if a:
                        copy_qkT(*a, 2)
                        copy_qkT(*a, 3)

                act.wait_ge(weights, ALL_WEIGHTS)
                turns(act, turn)

            @block.vector
            def _(dve):
                def statistics(u, p):
                    for t in range(PT):
                        nc.vector.bn_stats(stats[u][:, t, :], keep.h[:, 2 * p + u, t, :]).then_inc(ln_stats[u], 1)
                    dve.wait_ge(ln_stats[u], PT * (p + 1))
                    stand_alone(dve, dve_seen)
                    for t in range(PT):
                        nc.vector.bn_aggr(mean_var[u][:, t, :], stats[u][:, t, :]).then_inc(ln_var[u], 1)

                def normalize(u, p):
                    dve.wait_ge(ln_root[u], p + 1)
                    for t in range(PT):
                        nc.vector.tensor_scalar(hn[u][:, t, :], keep.h[:, 2 * p + u, t, :],
                                                mean_var[u][:, t, 0:1], rstd[u][:, t:t + 1],
                                                ALU.subtract, ALU.mult).then_inc(hn_ready[u], 1)

                def rotate(u, p, i):
                    _, t, w, k = QK[i]
                    x = bank[u][k][:, :].rearrange("p (h c) -> p h c", h=H1)

                    def over_heads(table, lo, hi):
                        return table[:, w, t, lo:hi].unsqueeze(1).broadcast_to([P, H1, hi - lo])

                    dve.wait_ge(squared[u], 4 * p + i + 1)
                    if i >= 2:
                        dve.wait_ge(added[u], START + 4 * p + i - 1)
                    nc.vector.tensor_tensor(t1[u][:, i % 2, :, :], x, over_heads(cos_w, 0, HD1),
                                            ALU.mult).then_inc(rotated[u], 1)
                    nc.vector.tensor_tensor(t2[u][:, i % 2, :, 0:HALF], x[:, :, HALF:],
                                            over_heads(sin_w, 0, HALF), ALU.mult).then_inc(rotated[u], 1)
                    nc.vector.tensor_tensor(t2[u][:, i % 2, :, HALF:], x[:, :, 0:HALF],
                                            over_heads(sin_w, HALF, HD1), ALU.mult).then_inc(rotated[u], 1)
                    nc.vector.tensor_reduce(sum_sq[u][:, t, w, :], squares[u][:, i % 2, :, :], AX.X,
                                            ALU.add).then_inc(summed[u], 1)

                def scale_keys(u, p):
                    dve.wait_ge(root_ready[u], p + 1)
                    dve.wait_ge(added[u], START + 4 * (p + 1))
                    for t in range(PT):
                        k3 = qk[u][:, t, 1, :].rearrange("p (h c) -> p h c", h=H1)
                        nc.vector.tensor_tensor(k3, k3, root[u][:, t, 1, :].unsqueeze(2)
                                                .broadcast_to([P, H1, HD1]), ALU.mult).then_inc(k_scaled[u], 1)

                def mask_scores(u, p, h):
                    dve.wait_ge(scores_done[u], H1 * p + h + 1)
                    if h >= 2:
                        dve.wait_ge(probs_ready[u], START + 2 * (H1 * p + h - 1))
                    stand_alone(dve, dve_seen)
                    for t, cols in enumerate((slice(0, P), slice(P, 3 * P))):
                        nc.vector.tensor_tensor_reduce(
                            masked[u][:, h % 2, cols], bank[u][0][:, cols], win_mask[:, cols], 1.0,
                            LEAST, ALU.add, ALU.max, top[u][:, h, t:t + 1]).then_inc(masked_ready[u], 1)
                    dve.wait_ge(masked_ready[u], START + 2 * (H1 * p + h + 1))
                    nc.vector.scalar_tensor_tensor(out=bias[u][:, h, :], in0=top[u][:, h, :], scalar=-1.0,
                                                   in1=root[u][:, :, 0, h], op0=ALU.mult,
                                                   op1=ALU.mult).then_inc(bias_ready[u], 1)

                def divide(u, p):
                    dve.wait_ge(probs_ready[u], START + 2 * H1 * (p + 1))
                    nc.vector.reciprocal(scale[u][:, :, :], total[u][:, :, :]).then_inc(scale_ready[u], 1)
                    dve.wait_ge(scale_ready[u], p + 1)
                    dve.wait_ge(o_done[u], START + H1 * (p + 1))
                    for t in range(PT):
                        nc.vector.tensor_tensor(
                            o_sb[u][:, t, :].rearrange("p (h c) -> p h c", h=H1),
                            bank[u][2 + t][:, :].rearrange("p (h c) -> p h c", h=H1),
                            scale[u][:, t, :].unsqueeze(2).broadcast_to([P, H1, HD1]),
                            ALU.mult).then_inc(o_ready[u], 1)

                def add_out(u, p):
                    dve.wait_ge(out_done[u], p + 1)
                    nc.vector.tensor_tensor(keep.h[:, 2 * p + u, :, :], keep.h[:, 2 * p + u, :, :],
                                            bank[u][2][:, 0:LP].rearrange("p (t d) -> p t d", t=PT),
                                            ALU.add).then_inc(h_ready[u], 1)

                def turn(a, b):
                    if a:
                        statistics(*a)
                    for s in range(H1 + 1):
                        if b and s < H1:
                            mask_scores(*b, s)
                        if a and s == NORM:
                            normalize(*a)
                        for i in range(4):
                            if a and s == ROTARY_AT[i]:
                                rotate(*a, i)
                    if b:
                        divide(*b)
                    if a:
                        scale_keys(*a)
                    if b:
                        add_out(*b)

                dve.wait_ge(tables, TABLES + 1)
                dve.wait_ge(const, CONSTS)
                turns(dve, turn)
        nc.clear_and_free_semaphores(sems)
        nc.all_engine_barrier()


E0 = 32
NT = B * PT
TOK = NT * P
CAP = TOK // E0
CT = CAP // P
ROW = D + E0
TG = P // E0
NG = NT // TG
DIGIT = 16
EG = P // DIGIT
LISTS = E0 // EG


def route(nc, dram, keep):
    sems = []
    with ExitStack() as ctx:
        def sb(name, shape, dt=F32):
            return ctx.enter_context(nc.sbuf_tensor("r_" + name, shape, dt))

        def two(name, shape, dt=F32):
            return [sb(f"{name}{u}", shape, dt) for u in range(2)]

        def sem(name):
            sems.append(nc.alloc_semaphore("r_" + name))
            return sems[-1]

        def sem2(name):
            return [sem(f"{name}{u}") for u in range(2)]

        w_router = sb("w_router", [P, E0])
        b_router = sb("b_router", [P, E0])
        half_neg = sb("half_neg", [P, PT])
        eps = sb("eps", [P, PT])
        ident_h = sb("ident_h", [P, P], BF16)
        before = sb("before", [P, P], BF16)
        ones = sb("ones", [P, P], BF16)
        same_expert = sb("same_expert", [P, P])
        own_list = sb("own_list", [P, EG])
        digits_i = sb("digits_i", [P, DIGIT], I32)
        digits = sb("digits", [P, DIGIT], BF16)
        lane_i = sb("lane_i", [P, 1], I32)
        lane = sb("lane", [P, 1])
        not_first = sb("not_first", [P, E0, NT])

        stats = two("stats", [P, PT, 6])
        mean_var = two("mean_var", [P, PT, 2])
        rstd = two("rstd", [P, PT])
        hn = two("hn", [P, PT, D])
        hnT = two("hnT", [P, LP])
        prob = sb("prob", [P, NT, E0])
        high = sb("high", [P, NT])
        total = sb("total", [P, NT])
        probT = sb("probT", [P, NG, P])
        hits = sb("hits", [P, NG * P], BF16)
        count = sb("count", [P, 1])
        ZERO_LOTS = 8
        zeros = sb("zeros", [P, NT // ZERO_LOTS * D])
        bit = sb("bit", [P, 1], I32)
        least = sb("least", [P, 1], I32)
        tried = sb("tried", [P, 1], I32)
        gain = sb("gain", [P, 1], I32)
        aboveT = sb("aboveT", [P, NG, P], BF16)
        levelT = sb("levelT", [P, NG, P], BF16)
        above = sb("above", [P, NT, E0], BF16)
        level = sb("level", [P, NT, E0], BF16)
        chosen = sb("chosen", [P, NT, E0], BF16)
        inside = sb("inside", [P, NT, E0])
        per_tile = sb("per_tile", [P, E0, NT])
        upto = sb("upto", [P, E0, NT])
        wanted = sb("wanted", [P, E0])
        pos_i = sb("pos_i", [P, NT, E0], I32)
        digit_i = sb("digit_i", [P, NT, E0], I32)
        digit_a = sb("digit_a", [P, NT, E0], BF16)
        digit_b = sb("digit_b", [P, NT, E0], BF16)
        hot_a = [sb(f"hot_a{k}", [P, E0, DIGIT], BF16) for k in range(2)]
        hot_b = [sb(f"hot_b{k}", [P, E0, DIGIT], BF16) for k in range(2)]
        tile_b = [sb(f"tile_b{k}", [P, E0, DIGIT], BF16) for k in range(2)]
        lane_b = [sb(f"lane_b{k}", [P, E0, DIGIT], BF16) for k in range(2)]
        picked = sb("picked", [P, EG, DIGIT])
        half = sb("half", [P, LISTS, 2, DIGIT])
        lists = sb("lists", [P, LISTS, DIGIT])
        lists_r = sb("lists_r", [E0 * CT, P])

        bank = [ctx.enter_context(nc.psum_tensor(f"r_bank{k}", [P, 512], F32)) for k in range(8)]

        zeros_ready, zero_stored = sem("zeros_ready"), sem("zero_stored")
        weights = sem("weights")
        const = sem("const")
        dve_seen = sem("dve_seen")
        cast = sem("cast")
        ln_stats, ln_var, ln_eps, ln_root, hn_ready = map(
            sem2, ("ln_stats", "ln_var", "ln_eps", "ln_root", "hn_ready"))
        hn_turned, hnT_ready, logits_done, logits_ready, row_stored = map(
            sem2, ("hn_turned", "hnT_ready", "logits_done", "logits_ready", "row_stored"))
        softmax_step, exp_done, prob_stored = sem("softmax_step"), sem("exp_done"), sem("prob_stored")
        prob_turned, probT_ready = sem("prob_turned"), sem("probT_ready")
        start_ready, tried_ready, counted, summed, gained, least_ready, bit_ready = map(
            sem, ("start_ready", "tried_ready", "counted", "summed", "gained", "least_ready", "bit_ready"))
        markT_ready, mark_turned, mark_ready = map(sem, ("markT_ready", "mark_turned", "mark_ready"))
        inside_done, inside_ready, tiles_done, tiles_ready = map(
            sem, ("inside_done", "inside_ready", "tiles_done", "tiles_ready"))
        step = sem("step")
        listed = sem("listed")
        a_ready, b_ready, tile_b_ready, lane_b_ready = map(sem, ("a_ready", "b_ready", "tile_b_ready", "lane_b_ready"))
        half_ready, lists_ready = sem("half_ready"), sem("lists_ready")
        list_step, list_stored, list_loaded, list_turned, tokens_ready = map(
            sem, ("list_step", "list_stored", "list_loaded", "list_turned", "tokens_ready"))

        rows_d = dram["token_rows"]
        feat_d = rows_d[:, 0:D].rearrange("(n t p) d -> n p t d", t=PT, p=P)
        prob_d = rows_d[:, D:ROW].rearrange("(t p) e -> p t e", p=P)
        sum_d = [dram[f"sum{u}"].rearrange("(n t p) d -> n p t d", n=ZERO_LOTS, p=P) for u in range(2)]
        CONSTS = 12

        start_counts(nc, [*logits_ready, tiles_ready, *row_stored, *hn_turned, least_ready, bit_ready])

        with nc.Block() as block:
            @block.sync
            def _(sp):
                sp.dma_start(w_router[:, :], dram["W_router"]).then_inc(weights, 16)
                sp.dma_start(b_router[:, :], dram["b_router"].partition_broadcast(P)).then_inc(weights, 16)
                with sp.Fori(0, PAIRS) as p:
                    for u in range(2):
                        sp.wait_ge(hn_ready[u], PT * (p + 1))
                        sp.dma_start(feat_d[2 * p + u], hn[u][:, :, :]).then_inc(row_stored[u], 16)
                sp.wait_ge(softmax_step, 5)
                sp.dma_start(prob_d, prob[:, :, :]).then_inc(prob_stored, 16)
                sp.wait_ge(zeros_ready, 1)
                for total_d in sum_d:
                    for lot in range(ZERO_LOTS):
                        sp.dma_start(total_d[lot], zeros[:, :].rearrange("p (t d) -> p t d", d=D))\
                            .then_inc(zero_stored, 16)
                sp.wait_ge(zero_stored, 16 * 2 * ZERO_LOTS)
                sp.wait_ge(lists_ready, LISTS)
                flat = dram["lists"]
                sp.dma_start(flat.rearrange("(g p b) -> p g b", g=LISTS, p=P), lists[:, :, :])\
                    .then_inc(list_stored, 16)
                sp.wait_ge(list_stored, 16)
                sp.dma_start(lists_r[:, :], flat.rearrange("(c r) -> c r", r=P)).then_inc(list_loaded, 16)
                for u in range(2):
                    sp.wait_ge(row_stored[u], START + 16 * PAIRS)
                sp.wait_ge(prob_stored, 16)

            @block.gpsimd
            def _(pool):
                nc.gpsimd.memset(zeros[:, :], 0.0).then_inc(zeros_ready, 1)
                nc.gpsimd.memset(half_neg[:, :], -0.5).then_inc(const, 1)
                nc.gpsimd.memset(eps[:, :], LN_EPS).then_inc(const, 1)
                nc.gpsimd.memset(before[:, :], 1.0).then_inc(const, 1)
                nc.gpsimd.memset(ones[:, :], 1.0).then_inc(const, 1)
                nc.gpsimd.memset(same_expert[:, :], 0.0).then_inc(const, 1)
                nc.gpsimd.memset(own_list[:, :], 1.0).then_inc(const, 1)
                nc.gpsimd.memset(not_first[:, :, :], 1.0).then_inc(const, 1)
                nc.gpsimd.iota(digits_i[:, :], pattern=[[1, DIGIT]], base=0, channel_multiplier=0)\
                    .then_inc(const, 1)
                nc.gpsimd.iota(lane_i[:, :], pattern=[[1, 1]], base=0, channel_multiplier=1).then_inc(const, 1)
                pool.wait_ge(const, 9)
                nc.gpsimd.memset(not_first[:, :, 0:1], 0.0).then_inc(const, 1)
                nc.gpsimd.affine_select(out=before[:, :], in_=before[:, :], compare_op=ALU.is_ge, fill=0.0,
                                        base=-1, pattern=[[1, P]], channel_multiplier=-1).then_inc(const, 1)
                nc.gpsimd.affine_select(out=own_list[:, :], in_=own_list[:, :], compare_op=ALU.is_ge, fill=0.0,
                                        base=0, pattern=[[-DIGIT, EG]], channel_multiplier=1).then_inc(const, 1)
                pool.wait_ge(const, 12)
                nc.gpsimd.affine_select(out=own_list[:, :], in_=own_list[:, :], compare_op=ALU.is_ge, fill=0.0,
                                        base=DIGIT - 1, pattern=[[DIGIT, EG]], channel_multiplier=-1)\
                    .then_inc(cast, 1)
                for n, off in enumerate(range(-P + E0, P, E0)):
                    pool.wait_ge(cast, 1 + n)
                    nc.gpsimd.affine_select(out=same_expert[:, :], in_=same_expert[:, :],
                                            compare_op=ALU.not_equal, fill=1.0, base=off, pattern=[[-1, P]],
                                            channel_multiplier=1).then_inc(cast, 1)
                pool.wait_ge(cast, 2 * TG)
                nc.gpsimd.tensor_copy(ident_h[:, :], keep.ident[:, :]).then_inc(cast, 1)
                nc.gpsimd.tensor_copy(digits[:, :], digits_i[:, :]).then_inc(cast, 1)
                nc.gpsimd.tensor_copy(lane[:, :], lane_i[:, :]).then_inc(cast, 1)
                with pool.Fori(0, PAIRS) as p:
                    for u in range(2):
                        pool.wait_ge(ln_var[u], PT * (p + 1))
                        nc.gpsimd.tensor_tensor(rstd[u][:, :], mean_var[u][:, :, 1], eps[:, :],
                                                ALU.add).then_inc(ln_eps[u], 1)
                        pool.wait_ge(ln_eps[u], p + 1)
                        nc.gpsimd.tensor_tensor(rstd[u][:, :], rstd[u][:, :], half_neg[:, :],
                                                ALU.pow).then_inc(ln_root[u], 1)

            CASTS = 2 * TG + 3

            @block.tensor
            def _(pe):
                pe.wait_ge(weights, 32)
                with pe.Fori(0, PAIRS) as p:
                    for u in range(2):
                        pe.wait_ge(hn_ready[u], PT * (p + 1))
                        for t in range(PT):
                            ins = nc.tensor.transpose(bank[u][:, t * P:(t + 1) * P], hn[u][:, t, :],
                                                      keep.ident[:, :])
                        ins.then_inc(hn_turned[u], 1)
                    for u in range(2):
                        pe.wait_ge(hnT_ready[u], p + 1)
                        pe.wait_ge(logits_ready[u], START + p)
                        for t in range(PT):
                            ins = nc.tensor.matmul(bank[2 + u][:, t * E0:(t + 1) * E0],
                                                   hnT[u][:, t * P:(t + 1) * P], w_router[:, :], start=True,
                                                   stop=True)
                        ins.then_inc(logits_done[u], 1)
                pe.wait_ge(softmax_step, 5)
                for g in range(NG):
                    k = 4 + g % 4
                    if g >= 4:
                        pe.wait_ge(probT_ready, g - 3)
                    nc.tensor.transpose(bank[k][:, 0:P],
                                        prob[:, TG * g:TG * (g + 1), :].rearrange("p t e -> p (t e)"),
                                        keep.ident[:, :]).then_inc(prob_turned, 1)
                pe.wait_ge(cast, CASTS)
                with pe.Fori(0, 30) as r:
                    pe.wait_ge(counted, r + 1)
                    nc.tensor.matmul(bank[0][:, 0:1], same_expert[:, :], count[:, :], start=True, stop=True)\
                        .then_inc(summed, 1)
                for n, src in enumerate((aboveT, levelT)):
                    pe.wait_ge(markT_ready, n + 1)
                    for q in range(4):
                        k = 4 * n + q
                        dst = bank[k][:, :].bitcast(BF16)
                        for j in range(4):
                            ins = nc.tensor.transpose(dst[:, j * P:(j + 1) * P], src[:, 4 * q + j, :],
                                                      ident_h[:, :])
                        ins.then_inc(mark_turned, 1)
                for n, src in enumerate((above, level, chosen)):
                    flat = src[:, :, :].rearrange("p t e -> p (t e)")
                    if n < 2:
                        pe.wait_ge(mark_ready, 8)
                    else:
                        pe.wait_ge(step, 8)
                    if n != 0:
                        for q in range(4):
                            if n == 2:
                                pe.wait_ge(inside_ready, 4)
                            ins = nc.tensor.matmul(bank[q][:, :], before[:, :], flat[:, 512 * q:512 * q + 512],
                                                   start=True, stop=True)
                            ins.then_inc(inside_done, 1)
                    if n:
                        pe.wait_ge(tiles_ready, START + 4 * n)
                    for q in range(4):
                        nc.tensor.matmul(bank[4 + q][:, :], ones[:, :], flat[:, 512 * q:512 * q + 512],
                                         start=True, stop=True).then_inc(tiles_done, 1)
                pe.wait_ge(tiles_ready, START + 12)
                pe.wait_ge(inside_ready, 8)
                for t in range(NT):
                    pe.wait_ge(a_ready, t + 1)
                    pe.wait_ge(tile_b_ready, t + 1)
                    pe.wait_ge(lane_b_ready, t + 1)
                    for g in range(LISTS):
                        cols = slice(g * EG, (g + 1) * EG)
                        for f, src in enumerate((tile_b, lane_b)):
                            ins = nc.tensor.matmul(
                                bank[g][:, f * P:(f + 1) * P],
                                hot_a[t % 2][:, cols, :].rearrange("p e a -> p (e a)"),
                                src[t % 2][:, cols, :].rearrange("p e b -> p (e b)"),
                                start=(t == 0 and f == 0), stop=(t == NT - 1), skip_group_check=True)
                    ins.then_inc(listed, 1)
                pe.wait_ge(list_loaded, 16)
                nc.tensor.transpose(bank[4][:, 0:E0 * CT], lists_r[:, :], keep.ident[0:E0 * CT, 0:E0 * CT])\
                    .then_inc(list_turned, 1)

            @block.scalar
            def _(act):
                with act.Fori(0, PAIRS) as p:
                    for u in range(2):
                        act.wait_ge(hn_turned[u], START + p + 1)
                        nc.scalar.copy(hnT[u][:, :], bank[u][:, 0:LP]).then_inc(hnT_ready[u], 1)
                act.wait_ge(softmax_step, 2)
                nc.scalar.activation(prob[:, :, :].rearrange("p t e -> p (t e)"),
                                     prob[:, :, :].rearrange("p t e -> p (t e)"), ACT.Exp).then_inc(exp_done, 1)
                for g in range(NG):
                    act.wait_ge(prob_turned, g + 1)
                    nc.scalar.copy(probT[:, g, :], bank[4 + g % 4][:, 0:P]).then_inc(probT_ready, 1)
                for t in range(NT):
                    act.wait_ge(b_ready, t + 1)
                    if t >= 2:
                        act.wait_ge(listed, t - 1)
                    nc.scalar.mul(tile_b[t % 2][:, :, :].rearrange("p e b -> p (e b)"),
                                  hot_b[t % 2][:, :, :].rearrange("p e b -> p (e b)"), float(t))\
                        .then_inc(tile_b_ready, 1)

            @block.vector
            def _(dve):
                with dve.Fori(0, PAIRS) as p:
                    for u in range(2):
                        for t in range(PT):
                            nc.vector.bn_stats(stats[u][:, t, :], keep.h[:, 2 * p + u, t, :])\
                                .then_inc(ln_stats[u], 1)
                        dve.wait_ge(ln_stats[u], PT * (p + 1))
                        stand_alone(dve, dve_seen)
                        for t in range(PT):
                            nc.vector.bn_aggr(mean_var[u][:, t, :], stats[u][:, t, :]).then_inc(ln_var[u], 1)
                    for u in range(2):
                        dve.wait_ge(ln_root[u], p + 1)
                        dve.wait_ge(row_stored[u], START + 16 * p)
                        dve.wait_ge(hn_turned[u], START + p)
                        for t in range(PT):
                            nc.vector.tensor_scalar(hn[u][:, t, :], keep.h[:, 2 * p + u, t, :],
                                                    mean_var[u][:, t, 0:1], rstd[u][:, t:t + 1],
                                                    ALU.subtract, ALU.mult).then_inc(hn_ready[u], 1)
                    for u in range(2):
                        dve.wait_ge(logits_done[u], p + 1)
                        if u == 0:
                            dve.wait_ge(weights, 32)
                        nc.vector.tensor_tensor(
                            prob[:, :, :].rearrange("p (n t) e -> p n t e", t=PT)[:, 2 * p + u, :, :],
                            bank[2 + u][:, 0:PT * E0].rearrange("p (t e) -> p t e", t=PT),
                            b_router[:, :].unsqueeze(1).broadcast_to([P, PT, E0]), ALU.add)\
                            .then_inc(logits_ready[u], 1)
                for u in range(2):
                    dve.wait_ge(logits_ready[u], START + PAIRS)

                def over_experts(x):
                    return x[:, :].unsqueeze(2).broadcast_to([P, NT, E0])

                nc.vector.tensor_reduce(high[:, :], prob[:, :, :], AX.X, ALU.max).then_inc(softmax_step, 1)
                dve.wait_ge(softmax_step, 1)
                nc.vector.tensor_tensor(prob[:, :, :], prob[:, :, :], over_experts(high), ALU.subtract)\
                    .then_inc(softmax_step, 1)
                dve.wait_ge(exp_done, 1)
                nc.vector.tensor_reduce(total[:, :], prob[:, :, :], AX.X, ALU.add).then_inc(softmax_step, 1)
                dve.wait_ge(softmax_step, 3)
                nc.vector.reciprocal(total[:, :], total[:, :]).then_inc(softmax_step, 1)
                dve.wait_ge(softmax_step, 4)
                nc.vector.tensor_tensor(prob[:, :, :], prob[:, :, :], over_experts(total), ALU.mult)\
                    .then_inc(softmax_step, 1)

                nc.vector.memset(least[:, :], 0).then_inc(start_ready, 1)
                nc.vector.memset(bit[:, :], 1 << 29).then_inc(start_ready, 1)
                dve.wait_ge(start_ready, 2)
                dve.wait_ge(probT_ready, NG)
                with dve.Fori(0, 30) as r:
                    dve.wait_ge(least_ready, START + r)
                    dve.wait_ge(bit_ready, START + r)
                    nc.vector.tensor_tensor(tried[:, :], least[:, :], bit[:, :], ALU.bitwise_or)\
                        .then_inc(tried_ready, 1)
                    dve.wait_ge(tried_ready, r + 1)
                    nc.vector.tensor_scalar(hits[:, :], probT[:, :, :].rearrange("p g l -> p (g l)"),
                                            tried[:, :].bitcast(F32), None, ALU.is_ge, ALU.add,
                                            accum_out=count[:, :]).then_inc(counted, 1)
                    dve.wait_ge(summed, r + 1)
                    nc.vector.scalar_tensor_tensor(out=gain[:, :], in0=bank[0][:, 0:1], scalar=float(CAP),
                                                   in1=bit[:, :], op0=ALU.is_ge, op1=ALU.mult)\
                        .then_inc(gained, 1)
                    dve.wait_ge(gained, r + 1)
                    nc.vector.tensor_tensor(least[:, :], least[:, :], gain[:, :], ALU.bitwise_or)\
                        .then_inc(least_ready, 1)
                    nc.vector.tensor_scalar(bit[:, :], bit[:, :], 1, None, ALU.logical_shift_right)\
                        .then_inc(bit_ready, 1)
                dve.wait_ge(least_ready, START + 30)
                limit = least[:, :].bitcast(F32)
                flatT = probT[:, :, :].rearrange("p g l -> p (g l)")
                nc.vector.tensor_scalar(aboveT[:, :, :].rearrange("p g l -> p (g l)"), flatT, limit, None,
                                        ALU.is_gt).then_inc(markT_ready, 1)
                nc.vector.tensor_scalar(levelT[:, :, :].rearrange("p g l -> p (g l)"), flatT, limit, None,
                                        ALU.is_equal).then_inc(markT_ready, 1)
                for n, dst in enumerate((above, level)):
                    for q in range(4):
                        dve.wait_ge(mark_turned, 4 * n + q + 1)
                        nc.vector.tensor_copy(
                            dst[:, 16 * q:16 * q + 16, :].rearrange("p t e -> p (t e)"),
                            bank[4 * n + q][:, :].bitcast(BF16)[:, 0:512]).then_inc(mark_ready, 1)

                def take_tiles(n):
                    for q in range(4):
                        dve.wait_ge(tiles_done, 4 * n + q + 1)
                        nc.vector.tensor_copy(per_tile[:, :, 16 * q:16 * q + 16],
                                              bank[4 + q][:, :].rearrange("p (t e) -> p e t", e=E0))\
                            .then_inc(tiles_ready, 1)

                def take_inside(n):
                    for q in range(4):
                        dve.wait_ge(inside_done, 4 * n + q + 1)
                        nc.vector.tensor_copy(inside[:, 16 * q:16 * q + 16, :].rearrange("p t e -> p (t e)"),
                                              bank[q][:, :]).then_inc(inside_ready, 1)

                def flat(x):
                    return x[:, :, :].rearrange("p a b -> p (a b)")

                def scan():
                    nc.vector.tensor_tensor_scan(flat(upto), flat(not_first), flat(per_tile), 0.0, ALU.mult,
                                                 ALU.add).then_inc(step, 1)

                by_tile = upto[:, :, :].rearrange("p e t -> p t e")
                take_tiles(0)
                dve.wait_ge(tiles_ready, START + 4)
                dve.wait_ge(cast, CASTS)
                scan()
                dve.wait_ge(step, 1)
                nc.vector.tensor_scalar(wanted[:, :], upto[:, :, NT - 1], -1.0, float(CAP), ALU.mult, ALU.add)\
                    .then_inc(step, 1)
                take_inside(0)
                take_tiles(1)
                dve.wait_ge(tiles_ready, START + 8)
                dve.wait_ge(step, 2)
                scan()
                dve.wait_ge(step, 3)
                nc.vector.tensor_tensor(flat(upto), flat(upto), flat(per_tile), ALU.subtract).then_inc(step, 1)
                dve.wait_ge(step, 4)
                dve.wait_ge(inside_ready, 4)
                nc.vector.tensor_tensor(inside[:, :, :], inside[:, :, :], by_tile, ALU.add).then_inc(step, 1)
                dve.wait_ge(step, 5)
                nc.vector.tensor_tensor(inside[:, :, :], inside[:, :, :],
                                        wanted[:, :].unsqueeze(1).broadcast_to([P, NT, E0]), ALU.is_lt)\
                    .then_inc(step, 1)
                dve.wait_ge(step, 6)
                nc.vector.tensor_tensor(flat(chosen), flat(inside), flat(level), ALU.mult).then_inc(step, 1)
                dve.wait_ge(step, 7)
                nc.vector.tensor_tensor(flat(chosen), flat(chosen), flat(above), ALU.add).then_inc(step, 1)
                take_inside(1)
                take_tiles(2)
                dve.wait_ge(tiles_ready, START + 12)
                scan()
                dve.wait_ge(step, 9)
                nc.vector.tensor_tensor(flat(upto), flat(upto), flat(per_tile), ALU.subtract).then_inc(step, 1)
                dve.wait_ge(step, 10)
                dve.wait_ge(inside_ready, 8)
                nc.vector.tensor_tensor(inside[:, :, :], inside[:, :, :], by_tile, ALU.add).then_inc(step, 1)
                dve.wait_ge(step, 11)
                nc.vector.scalar_tensor_tensor(out=flat(inside), in0=flat(chosen), scalar=-4096.0,
                                               in1=flat(inside), op0=ALU.mult, op1=ALU.add).then_inc(step, 1)
                dve.wait_ge(step, 12)
                nc.vector.tensor_scalar(flat(pos_i), flat(inside), 4096.0, None, ALU.add).then_inc(step, 1)
                dve.wait_ge(step, 13)
                nc.vector.tensor_scalar(flat(digit_i), flat(pos_i), 4, None, ALU.logical_shift_right)\
                    .then_inc(step, 1)
                dve.wait_ge(step, 14)
                nc.vector.tensor_copy(flat(digit_a), flat(digit_i)).then_inc(step, 1)
                dve.wait_ge(step, 15)
                nc.vector.tensor_scalar(flat(digit_i), flat(pos_i), DIGIT - 1, None, ALU.bitwise_and)\
                    .then_inc(step, 1)
                dve.wait_ge(step, 16)
                nc.vector.tensor_copy(flat(digit_b), flat(digit_i)).then_inc(step, 1)
                dve.wait_ge(step, 17)
                for t in range(NT):
                    if t >= 2:
                        dve.wait_ge(listed, t - 1)
                        dve.wait_ge(tile_b_ready, t - 1)
                    every = digits[:, :].unsqueeze(1).broadcast_to([P, E0, DIGIT])
                    nc.vector.tensor_tensor(hot_b[t % 2][:, :, :], every,
                                            digit_b[:, t, :].unsqueeze(2).broadcast_to([P, E0, DIGIT]),
                                            ALU.is_equal).then_inc(b_ready, 1)
                    nc.vector.tensor_tensor(hot_a[t % 2][:, :, :], every,
                                            digit_a[:, t, :].unsqueeze(2).broadcast_to([P, E0, DIGIT]),
                                            ALU.is_equal).then_inc(a_ready, 1)
                    dve.wait_ge(b_ready, t + 1)
                    nc.vector.tensor_scalar(flat(lane_b[t % 2]), flat(hot_b[t % 2]), lane[:, 0:1], None,
                                            ALU.mult).then_inc(lane_b_ready, 1)
                dve.wait_ge(listed, NT)
                for g in range(LISTS):
                    for f in range(2):
                        block_f = bank[g][:, f * P:(f + 1) * P].rearrange("p (e b) -> p e b", e=EG)
                        if g or f:
                            dve.wait_ge(half_ready, 2 * g + f)
                        nc.vector.tensor_tensor(picked[:, :, :], block_f,
                                                own_list[:, :].unsqueeze(2).broadcast_to([P, EG, DIGIT]),
                                                ALU.mult).then_inc(list_step, 1)
                        dve.wait_ge(list_step, 2 * g + f + 1)
                        nc.vector.tensor_reduce(half[:, g, f, :], picked[:, :, :].rearrange("p e b -> p b e"),
                                                AX.X, ALU.add).then_inc(half_ready, 1)
                    dve.wait_ge(half_ready, 2 * g + 2)
                    nc.vector.scalar_tensor_tensor(out=lists[:, g, :], in0=half[:, g, 0, :], scalar=float(P),
                                                   in1=half[:, g, 1, :], op0=ALU.mult, op1=ALU.add)\
                        .then_inc(lists_ready, 1)
                dve.wait_ge(list_turned, 1)
                nc.vector.tensor_copy(keep.tokens[:, 0:E0 * CT], bank[4][:, 0:E0 * CT]).then_inc(tokens_ready, 1)
        nc.clear_and_free_semaphores(sems)
        nc.all_engine_barrier()


GROUP = 4
F0 = 341
CHUNKS = [(c * P, min(P, F0 - c * P)) for c in range(-(-F0 // P))]


def experts(nc, dram, keep):
    sems = []
    with ExitStack() as ctx:
        def sb(name, shape, dt=F32):
            return ctx.enter_context(nc.sbuf_tensor("e_" + name, shape, dt))

        def two(name, shape, dt=F32):
            return [sb(f"{name}{u}", shape, dt) for u in range(2)]

        def twice(name, shape, dt=F32):
            return [[sb(f"{name}{u}{q}", shape, dt) for q in range(2)] for u in range(2)]

        def sem(name):
            sems.append(nc.alloc_semaphore("e_" + name))
            return sems[-1]

        def sem2(name):
            return [sem(f"{name}{u}") for u in range(2)]

        NCH = len(CHUNKS)
        LOTS = 8
        LOT_TILES = NT // LOTS
        w_up = twice("w_up", [P, F0])
        b_up = sb("b_up", [P, NCH, E0 // GROUP])
        w_down = twice("w_down", [P, NCH, D])
        b_down = twice("b_down", [1, D])
        ones = sb("ones", [1, P])
        token_col = twice("token_col", [P, CT], I32)
        rows = twice("rows", [P, CT, ROW])
        xT = two("xT", [P, CAP])
        bias = two("bias", [P, NCH])
        hidden = two("hidden", [P, NCH, CAP])
        y = two("y", [P, CT, D])
        sums = two("sums", [P, LOT_TILES, D])

        bank = [[ctx.enter_context(nc.psum_tensor(f"e_bank{u}{k}", [P, 512], F32)) for k in range(4)]
                for u in range(2)]

        weights = sem("weights")
        const = sem("const")
        pool_seen = sem("pool_seen")
        dve_seen = sem("dve_seen")
        col_ready, turned, xT_ready, up_done, hidden_ready = map(
            sem2, ("col_ready", "turned", "xT_ready", "up_done", "hidden_ready"))
        down_done, y_ready, scattered, bias_ready = map(sem2, ("down_done", "y_ready", "scattered", "bias_ready"))
        gathered = [[sem(f"gathered{u}{q}") for q in range(2)] for u in range(2)]
        w_loaded = [[sem(f"w_loaded{u}{q}") for q in range(2)] for u in range(2)]
        sum_loaded, added = sem2("sum_loaded"), sem2("added")

        tokens = keep.tokens[:, :].rearrange("p (e j) -> p e j", j=CT)
        sum_d = [dram[f"sum{u}"].rearrange("(n t p) d -> n p t d", t=LOT_TILES, p=P) for u in range(2)]
        up_d = dram["W_up"]
        down_d = dram["W_down"]

        start_counts(nc, [*down_done, *added, *y_ready, *hidden_ready])

        ROUNDS = E0 // GROUP

        with nc.Block() as block:
            @block.sync
            def _(sp):
                for c, (lo, n) in enumerate(CHUNKS):
                    sp.dma_start(b_up[0:n, c, :], dram["b_upT"][lo:lo + n, :]).then_inc(weights, 16)
                with sp.Fori(0, ROUNDS) as r:
                    for q in range(2):
                        p = 2 * r + q
                        for u in range(2):
                            sp.wait_ge(down_done[u], START + p - 1)
                            sp.dma_start(w_up[u][q][:, :], up_d[r]).then_inc(w_loaded[u][q], 16)
                            for c, (lo, n) in enumerate(CHUNKS):
                                sp.dma_start(w_down[u][q][0:n, c, :], down_d[2 * p + u, lo:lo + n, :])\
                                    .then_inc(w_loaded[u][q], 16)
                            sp.dma_start(b_down[u][q][:, :], dram["b_down"][bass.ds(2 * p + u, 1), :])\
                                .then_inc(w_loaded[u][q], 16)
                for u in range(2):
                    sp.wait_ge(scattered[u], 16 * CT * (E0 // 2))
                with sp.Fori(0, LOTS) as n:
                    for u in range(2):
                        sp.wait_ge(added[u], START + n)
                        sp.dma_start(sums[u][:, :, :], sum_d[u][n]).then_inc(sum_loaded[u], 16)

            @block.gpsimd
            def _(pool):
                nc.gpsimd.memset(ones[:, :], 1.0).then_inc(const, 1)
                for q in range(2):
                    for u in range(2):
                        nc.gpsimd.tensor_copy(token_col[u][q][:, :], tokens[:, 2 * q + u, :]).then_inc(col_ready[u], 1)

                def gather(u, q):
                    for j in range(CT):
                        pool.indirect_dma_start(
                            out=rows[u][q][:, j, :], out_offset=None, in_=dram["token_rows"],
                            in_offset=bass.IndirectOffsetOnAxis(ap=token_col[u][q][:, j:j + 1], axis=0),
                        ).then_inc(gathered[u][q], 16)

                for q in range(2):
                    for u in range(2):
                        pool.wait_ge(col_ready[u], 2)
                        gather(u, q)
                with pool.Fori(0, ROUNDS) as r:
                    for q in range(2):
                        p = 2 * r + q
                        for u in range(2):
                            pool.wait_ge(y_ready[u], START + CT * (p + 1))
                            stand_alone(pool, pool_seen)
                            for j in range(CT):
                                pool.indirect_dma_start(
                                    out=dram[f"sum{u}"],
                                    out_offset=bass.IndirectOffsetOnAxis(ap=token_col[u][q][:, j:j + 1], axis=0),
                                    in_=y[u][:, j, :], in_offset=None, compute_op=ALU.add,
                                ).then_inc(scattered[u], 16)
                        for u in range(2):
                            pool.wait_ge(scattered[u], 16 * CT * (p + 1))
                            nc.gpsimd.tensor_copy(token_col[u][q][:, :], tokens[:, 2 * p + 4 + u, :])\
                                .then_inc(col_ready[u], 1)
                            pool.wait_ge(col_ready[u], p + 3)
                            stand_alone(pool, pool_seen)
                            gather(u, q)
                for u in range(2):
                    for q in range(2):
                        pool.wait_ge(gathered[u][q], 16 * CT * (ROUNDS + 1))

            @block.tensor
            def _(pe):
                pe.wait_ge(const, 1)
                with pe.Fori(0, ROUNDS) as r:
                    for q in range(2):
                        p = 2 * r + q
                        for u in range(2):
                            pe.wait_ge(gathered[u][q], 16 * CT * (r + 1))
                            for j in range(CT):
                                ins = nc.tensor.transpose(bank[u][0][:, j * P:(j + 1) * P], rows[u][q][:, j, 0:D],
                                                          keep.ident[:, :])
                            ins.then_inc(turned[u], 1)
                        for u in range(2):
                            pe.wait_ge(xT_ready[u], p + 1)
                            pe.wait_ge(w_loaded[u][q], 16 * (NCH + 2) * (r + 1))
                            for c, (lo, n) in enumerate(CHUNKS):
                                dst = bank[u][1 + c // 2][0:n, (c % 2) * CAP:(c % 2 + 1) * CAP]
                                ins = nc.tensor.matmul(dst, w_up[u][q][:, lo:lo + n], xT[u][:, :], start=True,
                                                       stop=True)
                            ins.then_inc(up_done[u], 1)
                        for u in range(2):
                            pe.wait_ge(hidden_ready[u], START + NCH * (p + 1))
                            pe.wait_ge(y_ready[u], START + CT * p)
                            for j in range(CT):
                                dst = bank[u][3][:, j * P:(j + 1) * P]
                                for c, (lo, n) in enumerate(CHUNKS):
                                    nc.tensor.matmul(dst, hidden[u][0:n, c, j * P:(j + 1) * P],
                                                     w_down[u][q][0:n, c, :], start=(c == 0), stop=False)
                                ins = nc.tensor.matmul(dst, ones[:, :], b_down[u][q][:, :], start=False, stop=True)
                            ins.then_inc(down_done[u], 1)

            @block.scalar
            def _(act):
                act.wait_ge(weights, 16 * NCH)
                with act.Fori(0, E0 // 2) as p:
                    for u in range(2):
                        act.wait_ge(up_done[u], p + 1)
                        act.wait_ge(bias_ready[u], p + 1)
                        for c, (lo, n) in enumerate(CHUNKS):
                            src = bank[u][1 + c // 2][0:n, (c % 2) * CAP:(c % 2 + 1) * CAP]
                            nc.scalar.activation(hidden[u][0:n, c, :], src, ACT.Silu, bias=bias[u][0:n, c:c + 1])\
                                .then_inc(hidden_ready[u], 1)

            @block.vector
            def _(dve):
                dve.wait_ge(weights, 16 * NCH)
                with dve.Fori(0, ROUNDS) as r:
                    for q in range(2):
                        p = 2 * r + q
                        for u in range(2):
                            dve.wait_ge(turned[u], p + 1)
                            nc.vector.tensor_copy(xT[u][:, :], bank[u][0][:, 0:CAP]).then_inc(xT_ready[u], 1)
                            dve.wait_ge(hidden_ready[u], START + NCH * p)
                            stand_alone(dve, dve_seen)
                            for c, (lo, n) in enumerate(CHUNKS):
                                ins = nc.vector.tensor_copy(bias[u][0:n, c:c + 1], b_up[0:n, c, bass.ds(r, 1)])
                            ins.then_inc(bias_ready[u], 1)
                        for u in range(2):
                            dve.wait_ge(down_done[u], START + p + 1)
                            dve.wait_ge(col_ready[u], p + 2)
                            for j in range(CT):
                                nc.vector.tensor_scalar(y[u][:, j, :], bank[u][3][:, j * P:(j + 1) * P],
                                                        rows[u][q][:, j, bass.ds(2 * p + (D + u), 1)], None,
                                                        ALU.mult).then_inc(y_ready[u], 1)
                with dve.Fori(0, LOTS) as n:
                    for u in range(2):
                        lot = keep.h[:, :, :, :].rearrange("p (n b) t d -> p n (b t) d", n=LOTS)[:, n]
                        dve.wait_ge(sum_loaded[u], 16 * (n + 1))
                        if u:
                            dve.wait_ge(added[0], START + n + 1)
                        nc.vector.tensor_tensor(lot, lot, sums[u][:, :, :], ALU.add).then_inc(added[u], 1)
        nc.clear_and_free_semaphores(sems)
        nc.all_engine_barrier()


LEVELS = 7


def delta_rule(nc, dram, keep):
    sems = []
    with ExitStack() as ctx:
        def sb(name, shape, dt=F32):
            return ctx.enter_context(nc.sbuf_tensor("d_" + name, shape, dt))

        def two(name, shape, dt=F32):
            return [sb(f"{name}{u}", shape, dt) for u in range(2)]

        def twice(name, shape):
            return [[sb(f"{name}{u}{q}", shape) for q in range(2)] for u in range(2)]

        def sem(name):
            sems.append(nc.alloc_semaphore("d_" + name))
            return sems[-1]

        def sem2(name):
            return [sem(f"{name}{u}") for u in range(2)]

        wT = sb("wT", [P, D])
        eta = sb("eta", [P, 1])
        minus_eta = sb("minus_eta", [P, 1])
        lam = sb("lam", [P, 1])
        gain = sb("gain", [P, D])
        shift = sb("shift", [P, D])
        half_neg = sb("half_neg", [P, PT])
        eps = sb("eps", [P, PT])
        spike = sb("spike", [P, LP])
        decay = sb("decay", [P, LP])
        decay_low = sb("decay_low", [P, P])
        own_i = sb("own_i", [P, P], I32)
        other_i = sb("other_i", [P, P], I32)
        level_i = sb("level_i", [P, P], I32)
        level_mask = sb("level_mask", [P, LEVELS, P])
        low = sb("low", [P, LEVELS - 1, P])
        first = sb("first", [P, 2, P])
        unit2 = sb("unit2", [P, 2, P])

        stats, mean_var, rstd = ([two(f"{name}{i}_", shape) for i in range(2)] for name, shape in (
            ("stats", [P, PT, 6]), ("mean_var", [P, PT, 2]), ("rstd", [P, PT])))
        offset = two("offset", [P, PT])
        k_sb = two("k", [P, PT, D])
        kT = two("kT", [P, LP])
        v_sb = twice("v", [P, PT, D])
        eta_v = twice("eta_v", [P, PT, D])
        gT0 = twice("gT0", [P, LP])
        gT1 = twice("gT1", [P, P])
        g_low = twice("g_low", [P, PT, LEVELS - 1, P])
        g_first = two("g_first", [P, PT, 2, P])
        inv = twice("inv", [P, PT, 2, P])
        mid = two("mid", [P, PT, P])
        rest = two("rest", [P, D])
        err = two("err", [P, PT, D])
        y = two("y", [P, PT, D])
        h_shift = two("h_shift", [P, PT, D])

        bank = [[ctx.enter_context(nc.psum_tensor(f"d_bank{u}{k}", [P, 512], F32)) for k in range(4)]
                for u in range(2)]

        weights = sem("weights")
        const = sem("const")
        dve_seen = sem("dve_seen")
        pool_seen = sem("pool_seen")
        lam_ready, decay_ready, decay_turned, low_ready, set_up, level_ready = map(
            sem, ("lam_ready", "decay_ready", "decay_turned", "low_ready", "set_up", "level_ready"))
        ln_stats, ln_var, ln_eps, ln_root = ([sem2(f"{name}{i}_") for i in range(2)]
                                             for name in ("ln_stats", "ln_var", "ln_eps", "ln_root"))
        offset_ready, k_ready = sem2("offset_ready"), sem2("k_ready")
        k_turned, kT_ready, v_done, gram_done, v_ready, eta_v_ready = map(
            sem2, ("k_turned", "kT_ready", "v_done", "gram_done", "v_ready", "eta_v_ready"))
        inv_started, gram_left = sem2("inv_started"), sem2("gram_left")
        gram_ready, first_ready, inv_ready, mid_done, mid_ready, inv_done = map(
            sem2, ("gram_ready", "first_ready", "inv_ready", "mid_done", "mid_ready", "inv_done"))
        err_done, err_ready, before_done, rest_ready, o_done, y_ready = map(
            sem2, ("err_done", "err_ready", "before_done", "rest_ready", "o_done", "y_ready"))
        normed, gained, shifted, h_ready = map(sem2, ("normed", "gained", "shifted", "h_ready"))

        loads = [(wT[:, :], dram["WT"]), (eta[:, :], dram["eta"].partition_broadcast(P)),
                 (lam[:, :], dram["lam_logit"].partition_broadcast(P)),
                 (gain[:, :], dram["ln_gamma"].partition_broadcast(P)),
                 (shift[:, :], dram["ln_beta"].partition_broadcast(P))]
        ALL_WEIGHTS = 16 * len(loads)
        CONSTS = 6
        GRAM = 4

        start_counts(nc, [*err_ready, *y_ready, *k_turned, *h_ready, *v_ready, *gram_left])

        OFFSET, TANH, TURN_K, GRAM_V, COPY_V = 1, 2, 2, 3, 4
        START_INVERSE = (4, 5)

        def pair_turns(eng, turn):
            turn(None, (0, 0))
            with eng.Fori(0, PAIRS // 2 - 1) as r:
                turn((2 * r, 0), (2 * r + 1, 1))
                turn((2 * r + 1, 1), (2 * r + 2, 0))
            turn((PAIRS - 2, 0), (PAIRS - 1, 1))
            turn((PAIRS - 1, 1), None)

        with nc.Block() as block:
            @block.sync
            def _(sp):
                for dst, src in loads:
                    sp.dma_start(dst, src).then_inc(weights, 16)
                sp.wait_ge(weights, ALL_WEIGHTS)

            @block.gpsimd
            def _(pool):
                nc.gpsimd.memset(half_neg[:, :], -0.5).then_inc(const, 1)
                nc.gpsimd.memset(eps[:, :], LN_EPS).then_inc(const, 1)
                nc.gpsimd.memset(spike[:, P:], 0.0).then_inc(const, 1)
                nc.gpsimd.tensor_copy(spike[:, 0:P], keep.ident[:, :]).then_inc(const, 1)
                nc.gpsimd.iota(own_i[:, :], pattern=[[0, P]], base=0, channel_multiplier=1).then_inc(const, 1)
                nc.gpsimd.iota(other_i[:, :], pattern=[[1, P]], base=0, channel_multiplier=0)\
                    .then_inc(const, 1)

                def inverse_deviation(i, p):
                    for u in range(2):
                        pool.wait_ge(ln_var[i][u], PT * (p + 1))
                        nc.gpsimd.tensor_tensor(rstd[i][u][:, :], mean_var[i][u][:, :, 1], eps[:, :],
                                                ALU.add).then_inc(ln_eps[i][u], 1)
                        pool.wait_ge(ln_eps[i][u], p + 1)
                        nc.gpsimd.tensor_tensor(rstd[i][u][:, :], rstd[i][u][:, :], half_neg[:, :],
                                                ALU.pow).then_inc(ln_root[i][u], 1)

                def shift_h(p):
                    for u in range(2):
                        pool.wait_ge(h_ready[u], START + p)
                        stand_alone(pool, pool_seen)
                        nc.gpsimd.tensor_tensor(h_shift[u][:, :, :], keep.h[:, 2 * p + u, :, :],
                                                shift[:, :].unsqueeze(1).broadcast_to([P, PT, D]),
                                                ALU.add).then_inc(shifted[u], 1)

                def add_to_h(p):
                    for u in range(2):
                        pool.wait_ge(normed[u], PT * (p + 1))
                        nc.gpsimd.tensor_tensor(y[u][:, :, :], y[u][:, :, :],
                                                gain[:, :].unsqueeze(1).broadcast_to([P, PT, D]),
                                                ALU.mult).then_inc(gained[u], 1)
                        pool.wait_ge(gained[u], p + 1)
                        pool.wait_ge(shifted[u], p + 1)
                        stand_alone(pool, pool_seen)
                        nc.gpsimd.tensor_tensor(keep.h[:, 2 * p + u, :, :], y[u][:, :, :], h_shift[u][:, :, :],
                                                ALU.add).then_inc(h_ready[u], 1)

                def turn(b, a):
                    if a:
                        inverse_deviation(0, a[0])
                    if b:
                        shift_h(b[0])
                        inverse_deviation(1, b[0])
                        add_to_h(b[0])

                pair_turns(pool, turn)

            @block.tensor
            def _(pe):
                pe.wait_ge(decay_ready, 1)
                nc.tensor.transpose(bank[0][0][:, 0:P], decay[:, 0:P], keep.ident[:, :]).then_inc(decay_turned, 1)
                pe.wait_ge(low_ready, 1)
                pe.wait_ge(weights, ALL_WEIGHTS)

                def turn_k(p, q):
                    for u in range(2):
                        pe.wait_ge(k_ready[u], PT * (p + 1))
                        pe.wait_ge(v_ready[u], START + p)
                        for t in range(PT):
                            ins = nc.tensor.transpose(bank[u][3][:, t * P:(t + 1) * P], k_sb[u][:, t, :],
                                                      keep.ident[:, :])
                        ins.then_inc(k_turned[u], 1)

                def gram_and_v(p, q):
                    for u in range(2):
                        pe.wait_ge(kT_ready[u], p + 1)
                        pe.wait_ge(gram_left[u], START + p)
                        tile = [kT[u][:, t * P:(t + 1) * P] for t in range(PT)]
                        nc.tensor.matmul(bank[u][2][:, 0:LP], tile[0], kT[u][:, :], start=True, stop=True)
                        nc.tensor.matmul(bank[u][2][:, LP:LP + P], tile[1], tile[1], start=True, stop=True)\
                            .then_inc(gram_done[u], 1)
                        for t in range(PT):
                            ins = nc.tensor.matmul(bank[u][3][:, LP + t * D:LP + (t + 1) * D], tile[t], wT[:, :],
                                                   start=True, stop=True)
                        ins.then_inc(v_done[u], 1)

                def level(p, q, l):
                    for u in range(2):
                        if l == 1:
                            pe.wait_ge(inv_started[u], p + 1)
                            pe.wait_ge(gram_ready[u], GRAM * (p + 1))
                            pe.wait_ge(err_ready[u], START + PT * p)
                            pe.wait_ge(y_ready[u], START + p)
                        else:
                            pe.wait_ge(inv_ready[u], (LEVELS - 1) * p + l - 1)
                        for t in range(PT):
                            ins = nc.tensor.matmul(bank[u][0][:, t * P:(t + 1) * P],
                                                   g_low[u][q][:, t, l - 1, :], inv[u][q][:, t, 0, :], start=True,
                                                   stop=True)
                        ins.then_inc(mid_done[u], 1)
                    for u in range(2):
                        pe.wait_ge(mid_ready[u], (LEVELS - 1) * p + l)
                        for t in range(PT):
                            lo = 2 * t * P
                            ins = nc.tensor.matmul(bank[u][1][:, lo:lo + P], inv[u][q][:, t, 1, :],
                                                   mid[u][:, t, :], start=True, stop=True)
                            if l < LEVELS - 1:
                                ins = nc.tensor.matmul(bank[u][1][:, lo + P:lo + 2 * P], mid[u][:, t, :],
                                                       inv[u][q][:, t, 1, :], start=True, stop=True)
                        ins.then_inc(inv_done[u], 1)

                def outputs(p, q):
                    for u in range(2):
                        pe.wait_ge(inv_ready[u], (LEVELS - 1) * (p + 1))
                        pe.wait_ge(eta_v_ready[u], p + 1)
                        nc.tensor.matmul(bank[u][0][:, LP:LP + D], inv[u][q][:, 0, 0, :], eta_v[u][q][:, 0, :],
                                         start=True, stop=True).then_inc(err_done[u], 1)
                    for u in range(2):
                        pe.wait_ge(err_ready[u], START + PT * p + 1)
                        nc.tensor.matmul(bank[u][1][:, LP:LP + D], gT0[u][q][:, 0:P], err[u][:, 0, :], start=True,
                                         stop=True)
                        nc.tensor.matmul(bank[u][1][:, 0:D], gT0[u][q][:, P:], err[u][:, 0, :], start=True,
                                         stop=True).then_inc(before_done[u], 1)
                    for u in range(2):
                        pe.wait_ge(rest_ready[u], p + 1)
                        nc.tensor.matmul(bank[u][0][:, LP + D:], inv[u][q][:, 1, 0, :], rest[u][:, :], start=True,
                                         stop=True).then_inc(err_done[u], 1)
                    for u in range(2):
                        pe.wait_ge(err_ready[u], START + PT * (p + 1))
                        nc.tensor.matmul(bank[u][1][:, LP + D:], gT0[u][q][:, P:], err[u][:, 0, :], start=True,
                                         stop=False)
                        nc.tensor.matmul(bank[u][1][:, LP + D:], gT1[u][q][:, :], err[u][:, 1, :], start=False,
                                         stop=True).then_inc(o_done[u], 1)

                def turn(b, a):
                    for l in range(1, LEVELS):
                        if b:
                            level(*b, l)
                        if a and l == TURN_K:
                            turn_k(*a)
                        if a and l == GRAM_V:
                            gram_and_v(*a)
                    if b:
                        outputs(*b)

                pair_turns(pe, turn)

            @block.scalar
            def _(act):
                act.wait_ge(weights, ALL_WEIGHTS)
                nc.scalar.activation(lam[:, :], lam[:, :], ACT.Sigmoid).then_inc(lam_ready, 1)

                def tanh(p, q):
                    for u in range(2):
                        act.wait_ge(offset_ready[u], p + 1)
                        act.wait_ge(k_turned[u], START + p)
                        for t in range(PT):
                            nc.scalar.activation(k_sb[u][:, t, :], keep.h[:, 2 * p + u, t, :], ACT.Tanh,
                                                 bias=offset[u][:, t:t + 1], scale=rstd[0][u][:, t:t + 1])\
                                .then_inc(k_ready[u], 1)

                def copy_kT(p, q):
                    for u in range(2):
                        act.wait_ge(k_turned[u], START + p + 1)
                        nc.scalar.copy(kT[u][:, :], bank[u][3][:, 0:LP]).then_inc(kT_ready[u], 1)

                def copy_v(p, q):
                    for u in range(2):
                        act.wait_ge(v_done[u], p + 1)
                        nc.scalar.copy(v_sb[u][q][:, :, :].rearrange("p t d -> p (t d)"),
                                       bank[u][3][:, LP:]).then_inc(v_ready[u], 1)

                def copy_mid(p, q, l):
                    for u in range(2):
                        act.wait_ge(mid_done[u], (LEVELS - 1) * p + l)
                        nc.scalar.copy(mid[u][:, :, :].rearrange("p t d -> p (t d)"),
                                       bank[u][0][:, 0:PT * P]).then_inc(mid_ready[u], 1)

                def copy_errors(p, q):
                    for t in range(PT):
                        for u in range(2):
                            act.wait_ge(err_done[u], PT * p + t + 1)
                            nc.scalar.copy(err[u][:, t, :], bank[u][0][:, LP + t * D:LP + (t + 1) * D])\
                                .then_inc(err_ready[u], 1)

                def turn(b, a):
                    for l in range(1, LEVELS):
                        if b:
                            copy_mid(*b, l)
                        if a and l == TANH:
                            tanh(*a)
                        if a and l == TURN_K:
                            copy_kT(*a)
                        if a and l == COPY_V:
                            copy_v(*a)
                    if b:
                        copy_errors(*b)

                pair_turns(act, turn)

            @block.vector
            def _(dve):
                dve.wait_ge(const, CONSTS)
                dve.wait_ge(lam_ready, 1)
                nc.vector.tensor_tensor_scan(decay[:, :], lam[:, 0:1].broadcast_to([P, LP]), spike[:, :], 0.0,
                                             ALU.mult, ALU.add).then_inc(decay_ready, 1)
                nc.vector.tensor_tensor(own_i[:, :], own_i[:, :], other_i[:, :], ALU.bitwise_xor)\
                    .then_inc(level_ready, 1)
                dve.wait_ge(level_ready, 1)
                for l in range(LEVELS):
                    nc.vector.tensor_scalar(level_i[:, :], own_i[:, :], l, None, ALU.logical_shift_right)\
                        .then_inc(level_ready, 1)
                    dve.wait_ge(level_ready, 2 * l + 2)
                    nc.vector.tensor_scalar(level_mask[:, l, :], level_i[:, :], 1.0, None, ALU.is_equal)\
                        .then_inc(level_ready, 1)
                    dve.wait_ge(level_ready, 2 * l + 3)
                dve.wait_ge(decay_turned, 1)
                nc.vector.tensor_copy(decay_low[:, :], bank[0][0][:, 0:P]).then_inc(low_ready, 1)
                dve.wait_ge(low_ready, 1)
                nc.vector.tensor_scalar(minus_eta[:, :], eta[:, :], -1.0, None, ALU.mult).then_inc(set_up, 1)
                nc.vector.scalar_tensor_tensor(
                    out=low[:, :, :], in0=level_mask[:, 1:, :], scalar=eta[:, 0:1],
                    in1=decay_low[:, :].unsqueeze(1).broadcast_to([P, LEVELS - 1, P]), op0=ALU.mult,
                    op1=ALU.mult).then_inc(set_up, 1)
                nc.vector.scalar_tensor_tensor(out=first[:, 0, :], in0=level_mask[:, 0, :], scalar=eta[:, 0:1],
                                               in1=decay[:, 0:P], op0=ALU.mult, op1=ALU.mult).then_inc(set_up, 1)
                nc.vector.scalar_tensor_tensor(out=first[:, 1, :], in0=level_mask[:, 0, :], scalar=eta[:, 0:1],
                                               in1=decay_low[:, :], op0=ALU.mult, op1=ALU.mult)\
                    .then_inc(set_up, 1)
                nc.vector.tensor_copy(unit2[:, :, :], keep.ident[:, :].unsqueeze(1).broadcast_to([P, 2, P]))\
                    .then_inc(set_up, 1)
                dve.wait_ge(set_up, 5)
                dve.wait_ge(weights, ALL_WEIGHTS)

                def layer_norm(i, u, p, src):
                    for t in range(PT):
                        nc.vector.bn_stats(stats[i][u][:, t, :], src(t)).then_inc(ln_stats[i][u], 1)
                    dve.wait_ge(ln_stats[i][u], PT * (p + 1))
                    stand_alone(dve, dve_seen)
                    for t in range(PT):
                        nc.vector.bn_aggr(mean_var[i][u][:, t, :], stats[i][u][:, t, :]).then_inc(ln_var[i][u], 1)

                def norm_h(p, q):
                    for u in range(2):
                        dve.wait_ge(k_turned[u], START + p)
                        layer_norm(0, u, p, lambda t: keep.h[:, 2 * p + u, t, :])

                def offsets(p, q):
                    for u in range(2):
                        dve.wait_ge(ln_root[0][u], p + 1)
                        nc.vector.scalar_tensor_tensor(out=offset[u][:, :], in0=mean_var[0][u][:, :, 0],
                                                       scalar=-1.0, in1=rstd[0][u][:, :], op0=ALU.mult,
                                                       op1=ALU.mult).then_inc(offset_ready[u], 1)

                def own(u):
                    return [bank[u][2][:, 0:P], bank[u][2][:, LP:LP + P]]

                def start_inverse(p, q, u):
                    dve.wait_ge(gram_done[u], p + 1)
                    for t in range(PT):
                        nc.vector.tensor_tensor(g_first[u][:, t, :, :],
                                                own(u)[t].unsqueeze(1).broadcast_to([P, 2, P]), first[:, :, :],
                                                ALU.mult).then_inc(first_ready[u], 1)
                    dve.wait_ge(first_ready[u], PT * (p + 1))
                    for t in range(PT):
                        ins = nc.vector.tensor_tensor(inv[u][q][:, t, :, :], unit2[:, :, :],
                                                      g_first[u][:, t, :, :], ALU.subtract)
                    ins.then_inc(inv_started[u], 1)

                def low_levels(p, q, u):
                    for t in range(PT):
                        nc.vector.tensor_tensor(g_low[u][q][:, t, :, :],
                                                own(u)[t].unsqueeze(1).broadcast_to([P, LEVELS - 1, P]),
                                                low[:, :, :], ALU.mult).then_inc(gram_ready[u], 1)

                def decayed(p, q):
                    for u in range(2):
                        nc.vector.tensor_tensor(gT0[u][q][:, :], bank[u][2][:, 0:LP], decay[:, :], ALU.mult)\
                            .then_inc(gram_ready[u], 1)
                        nc.vector.tensor_tensor(gT1[u][q][:, :], own(u)[1], decay[:, 0:P], ALU.mult)\
                            .then_inc(gram_ready[u], 1)
                        dve.wait_ge(gram_ready[u], GRAM * (p + 1))
                        dve.sem_inc(gram_left[u], 1)
                    for u in range(2):
                        dve.wait_ge(v_ready[u], START + p + 1)
                        nc.vector.tensor_scalar(eta_v[u][q][:, :, :], v_sb[u][q][:, :, :], eta[:, 0:1], None,
                                                ALU.mult).then_inc(eta_v_ready[u], 1)

                def subtract_step(p, q, l):
                    for u in range(2):
                        dve.wait_ge(inv_done[u], (LEVELS - 1) * p + l)
                        done = bank[u][1][:, :].rearrange("p (t i c) -> p t i c", t=PT, i=2)
                        if l < LEVELS - 1:
                            nc.vector.tensor_tensor(inv[u][q][:, :, :, :], inv[u][q][:, :, :, :], done,
                                                    ALU.subtract).then_inc(inv_ready[u], 1)
                        else:
                            nc.vector.tensor_tensor(inv[u][q][:, :, 0, :], inv[u][q][:, :, 0, :],
                                                    done[:, :, 0, :], ALU.subtract).then_inc(inv_ready[u], 1)

                def rest_of_v(p, q):
                    for u in range(2):
                        dve.wait_ge(before_done[u], p + 1)
                        nc.vector.scalar_tensor_tensor(out=rest[u][:, :], in0=bank[u][1][:, 0:D],
                                                       scalar=minus_eta[:, 0:1], in1=eta_v[u][q][:, 1, :],
                                                       op0=ALU.mult, op1=ALU.add).then_inc(rest_ready[u], 1)

                def add_v(p, q):
                    for u in range(2):
                        dve.wait_ge(o_done[u], p + 1)
                        dve.wait_ge(h_ready[u], START + p)
                        nc.vector.tensor_tensor(y[u][:, :, :],
                                                bank[u][1][:, LP:].rearrange("p (t d) -> p t d", t=PT),
                                                v_sb[u][q][:, :, :], ALU.add).then_inc(y_ready[u], 1)
                    for u in range(2):
                        dve.wait_ge(y_ready[u], START + p + 1)
                        layer_norm(1, u, p, lambda t: y[u][:, t, :])

                def normalize(p, q):
                    for u in range(2):
                        dve.wait_ge(ln_root[1][u], p + 1)
                        for t in range(PT):
                            nc.vector.tensor_scalar(y[u][:, t, :], y[u][:, t, :], mean_var[1][u][:, t, 0:1],
                                                    rstd[1][u][:, t:t + 1], ALU.subtract, ALU.mult)\
                                .then_inc(normed[u], 1)

                def turn(b, a):
                    if a:
                        norm_h(*a)
                    for l in range(1, LEVELS):
                        if b:
                            subtract_step(*b, l)
                        if a and l == OFFSET:
                            offsets(*a)
                        for u in range(2):
                            if a and l == START_INVERSE[u]:
                                start_inverse(*a, u)
                    if a:
                        low_levels(*a, 0)
                    if b:
                        rest_of_v(*b)
                    if a:
                        low_levels(*a, 1)
                        decayed(*a)
                    if b:
                        add_v(*b)
                    if b:
                        normalize(*b)

                pair_turns(dve, turn)
        nc.clear_and_free_semaphores(sems)
        nc.all_engine_barrier()


E1 = 64
TOP_K = 6
LEAST = -3.0e38

GT = 4
GROUP_TOKENS = GT * P
GROUPS1 = B * LP // GROUP_TOKENS
ROUTED = E1 * 64 // P
SHARED = 256 // P
CH = ROUTED + SHARED


def expert_ffn(nc, dram, keep):
    sems = []
    with ExitStack() as ctx:
        def sb(name, shape, dt=F32):
            return ctx.enter_context(nc.sbuf_tensor("f_" + name, shape, dt))

        def two(name, shape, dt=F32):
            return [sb(f"{name}{u}", shape, dt) for u in range(2)]

        def sem(name):
            sems.append(nc.alloc_semaphore("f_" + name))
            return sems[-1]

        w1 = [sb("w1_hi", [P, CH, P], F32R), sb("w1_lo", [P, CH, P], F32R)]
        w3 = [sb("w3_hi", [P, CH, P], F32R), sb("w3_lo", [P, CH, P], F32R)]
        w2 = [sb("w2_hi", [P, CH, D], F32R), sb("w2_lo", [P, CH, D], F32R)]
        gate = sb("gate", [P, E1])
        spread = sb("spread", [P, ROUTED // 2, P], F32R)
        half_neg = sb("half_neg", [P, GT])
        eps = sb("eps", [P, GT])

        own_i = sb("own_i", [P, 1], I32)
        own = sb("own", [P, 1])
        expert_i = sb("expert_i", [P, E1], I32)
        expert = sb("expert", [P, E1])

        stats = sb("stats", [P, GT, 6])
        mean_var = sb("mean_var", [P, GT, 2])
        rstd = sb("rstd", [P, GT])
        n_sb = sb("n", [P, GT, D])
        nT = sb("nT", [P, GROUP_TOKENS])
        nT_part = [[sb(f"nT_{part}{u}", [P, GROUP_TOKENS], F32R) for part in ("hi", "lo")] for u in range(2)]
        score = sb("score", [P, GT, E1 + 2])
        best = sb("best", [P, GT, 8])
        marked = sb("marked", [P, GT, E1 + 2])
        chosen = sb("chosen", [P, GT, E1])
        power = sb("power", [P, GT, E1])
        total = sb("total", [P, GT])
        comb = sb("comb", [P, GT, 2, 2, E1 // 2], F32R)
        combT = two("combT", [P, GROUP_TOKENS], F32R)
        work = sb("work", [P, 6, GROUP_TOKENS])
        silu, gated, hidden = ([work[:, 2 * i + k, :] for k in range(2)] for i in range(3))
        hidden_part = [[sb(f"hidden_{part}{k}", [P, GROUP_TOKENS], F32R) for part in ("hi", "lo")]
                       for k in range(2)]
        outT = sb("outT", [P, GROUP_TOKENS])
        result = two("result", [P, GT, D])

        def bank(name):
            return ctx.enter_context(nc.psum_tensor("f_" + name, [P, 512], F32))

        ps1 = [bank("ps1_0"), bank("ps1_1")]
        ps3 = [bank("ps3_0"), bank("ps3_1")]
        ps_comb = [bank("ps_comb0"), bank("ps_comb1")]
        ps_out = bank("ps_out")
        ps_turn = bank("ps_turn")

        gate_loaded, const, dve_seen, numbers, spread_ready, split_hi = map(
            sem, ("gate_loaded", "const", "dve_seen", "numbers", "spread_ready", "split_hi"))
        weights_loaded = [sem("weights_loaded0"), sem("weights_loaded1")]
        split_lo = sem("split_lo")
        (ln_stats, ln_var, ln_eps, ln_root, n_ready, n_turned, nT_ready, nT_hi, parts_ready) = map(
            sem, ("ln_stats", "ln_var", "ln_eps", "ln_root", "n_ready", "n_turned", "nT_ready", "nT_hi",
                  "parts_ready"))
        (scores_done, score_ready, best_ready, best_cut, marked_ready, chosen_ready, below_ready, power_ready,
         power_cut, total_ready, share_ready, comb_full, comb_hi, comb_ready, comb_turned, combT_ready) = map(
            sem, ("scores_done", "score_ready", "best_ready", "best_cut", "marked_ready", "chosen_ready",
                  "below_ready", "power_ready", "power_cut", "total_ready", "share_ready", "comb_full",
                  "comb_hi", "comb_ready", "comb_turned", "combT_ready"))
        parts_hi, parts_lo = sem("parts_hi"), sem("parts_lo")
        x1_done, x3_done, spread_done, silu_ready, gated_ready, hidden_ready, hidden_used = map(
            sem, ("x1_done", "x3_done", "spread_done", "silu_ready", "gated_ready", "hidden_ready",
                  "hidden_used"))
        outT_ready, out_turned, result_ready = map(sem, ("outT_ready", "out_turned", "result_ready"))
        stored = [sem("stored0"), sem("stored1")]

        def plain(ap):
            return ap.bitcast(F32)

        def chunks(name):
            return dram[name].rearrange("d (c m) -> d c m", m=P)

        PIECE = 3 * GROUP_TOKENS // P
        stage = [work[:, 3 * k:3 * k + 3, :].rearrange("p i (c m) -> p (i c) m", m=P) for k in range(2)]
        rows = {name: dram[name].rearrange("(c m) d -> m c d", m=P) for name in ("w2", "w_sdT")}
        weights = [(w1, chunks("w1T"), chunks("w_sgT")), (w3, chunks("w3T"), chunks("w_suT")),
                   (w2, rows["w2"], rows["w_sdT"])]
        pieces = [(w, routed, shared, lo, min(lo + PIECE, CH)) for w, routed, shared in weights
                  for lo in range(0, CH, PIECE)]

        def loads_of(n):
            _, routed, shared, lo, hi = pieces[n]
            found = [(stage[n % 2][:, 0:min(hi, ROUTED) - lo, :], routed[:, lo:min(hi, ROUTED), :])]
            if hi > ROUTED:
                found.append((stage[n % 2][:, ROUTED - lo:hi - lo, :], shared))
            return found

        def loaded(n):
            return 16 * sum(len(loads_of(i)) for i in range(n % 2, n + 1, 2))

        CONSTS = 5
        out_d = dram["out"].rearrange("(g t p) d -> g p t d", t=GT, p=P)

        def tile_of(g, t):
            return keep.h[:, (GT // PT) * g + t // PT, t % PT, :]

        STATS, VAR, NORM, TURN, COPY_N, PARTS, SCORES = 4, 6, 8, 10, 11, 12, 12
        CHOOSE = 14
        POWER, TURN_COMB, COPY_COMB = CHOOSE + 3, CHOOSE + 12, CHOOSE + 13
        COPY_OUT, TURN_OUT, ADD_OUT = 2, 4, 5
        LAG = 3
        AHEAD = 2

        start_counts(nc, [*stored, outT_ready, scores_done, parts_ready, out_turned, n_turned, comb_turned])

        with nc.Block() as block:
            @block.sync
            def _(sp):
                sp.dma_start(gate[:, :], dram["w_gateT"]).then_inc(gate_loaded, 16)
                for n in range(len(pieces)):
                    if n >= 2:
                        sp.wait_ge(split_lo, n - 1)
                    for dst, src in loads_of(n):
                        sp.dma_start(dst, src).then_inc(weights_loaded[n % 2], 16)
                with sp.Fori(0, GROUPS1 // 2) as p:
                    for u in range(2):
                        sp.wait_ge(result_ready, 2 * p + u + 1)
                        sp.dma_start(out_d[2 * p + u], result[u][:, :, :]).then_inc(stored[u], 16)
                for u in range(2):
                    sp.wait_ge(stored[u], START + 16 * (GROUPS1 // 2))

            @block.gpsimd
            def _(pool):
                nc.gpsimd.memset(half_neg[:, :], -0.5).then_inc(const, 1)
                nc.gpsimd.memset(eps[:, :], LN_EPS).then_inc(const, 1)
                nc.gpsimd.memset(score[:, :, E1:], LEAST).then_inc(const, 1)
                nc.gpsimd.iota(own_i[:, :], pattern=[[0, 1]], base=0, channel_multiplier=1).then_inc(const, 1)
                nc.gpsimd.iota(expert_i[:, :], pattern=[[1, E1]], base=0, channel_multiplier=0)\
                    .then_inc(const, 1)
                def inverse_deviation(g):
                    pool.wait_ge(ln_var, GT * (g + 1))
                    nc.gpsimd.tensor_tensor(rstd[:, :], mean_var[:, :, 1], eps[:, :], ALU.add).then_inc(ln_eps, 1)
                    pool.wait_ge(ln_eps, g + 1)
                    nc.gpsimd.tensor_tensor(rstd[:, :], rstd[:, :], half_neg[:, :], ALU.pow).then_inc(ln_root, 1)

                inverse_deviation(0)
                with pool.Fori(1, GROUPS1) as g:
                    inverse_deviation(g)

            @block.tensor
            def _(pe):
                def turn_n(g, first):
                    pe.wait_ge(n_ready, GT * (g + 1))
                    if not first:
                        pe.wait_ge(result_ready, g - 1)
                    for t in range(GT):
                        ins = nc.tensor.transpose(ps_turn[:, t * P:(t + 1) * P], n_sb[:, t, :], keep.ident[:, :])
                    ins.then_inc(n_turned, 1)

                def score_tokens(g):
                    pe.wait_ge(nT_ready, g + 1)
                    for t in range(GT):
                        ins = nc.tensor.matmul(ps_turn[:, t * E1:(t + 1) * E1], nT[:, t * P:(t + 1) * P],
                                               gate[:, :], start=True, stop=True)
                    ins.then_inc(scores_done, 1)

                def turn_comb(g):
                    pe.wait_ge(comb_ready, g + 1)
                    for t in range(GT):
                        ins = nc.tensor.transpose(ps_turn[:, t * P:(t + 1) * P],
                                                  plain(comb[:, t, :, :, :]).rearrange("p i k e -> p (i k e)"),
                                                  keep.ident[:, :])
                    ins.then_inc(comb_turned, 1)

                def turn_out(g, last):
                    pe.wait_ge(outT_ready, START + g + 1)
                    if not last:
                        pe.wait_ge(combT_ready, g + 2)
                    for t in range(GT):
                        ins = nc.tensor.transpose(ps_turn[:, t * P:(t + 1) * P], outT[:, t * P:(t + 1) * P],
                                                  keep.ident[:, :])
                    ins.then_inc(out_turned, 1)

                def in_parts(dst, w, x, c, start=True, stop=True):
                    nc.tensor.matmul(dst, w[0][:, c, :], x[0][:, :], start=start, stop=False)
                    nc.tensor.matmul(dst, w[0][:, c, :], x[1][:, :], start=False, stop=False)
                    return nc.tensor.matmul(dst, w[1][:, c, :], x[0][:, :], start=False, stop=stop)

                def up(g, u, c):
                    n = CH * g + c
                    pe.wait_ge(silu_ready, n + 1)
                    in_parts(ps1[c % 2][:, :], w1, nT_part[u], c).then_inc(x1_done, 1)
                    pe.wait_ge(gated_ready, n + 1)
                    in_parts(ps3[c % 2][:, :], w3, nT_part[u], c).then_inc(x3_done, 1)
                    if c < ROUTED:
                        pe.wait_ge(hidden_ready, n + 1)
                        half = slice(0, E1) if c < ROUTED // 2 else slice(E1, P)
                        nc.tensor.matmul(ps_comb[c % 2][:, :], spread[half, c % (ROUTED // 2), :],
                                         combT[u][half, :], start=True, stop=True).then_inc(spread_done, 1)

                def down(g, c):
                    pe.wait_ge(parts_hi, CH * g + c + 1)
                    pe.wait_ge(parts_lo, CH * g + c + 1)
                    if c == 0:
                        pe.wait_ge(outT_ready, START + g)
                    in_parts(ps_out[:, :], w2, hidden_part[c % 2], c, start=(c == 0),
                             stop=(c == CH - 1)).then_inc(hidden_used, 1)

                def group(g, u, first, last):
                    pe.wait_ge(parts_ready, START + g + 1)
                    pe.wait_ge(combT_ready, g + 1)
                    for c in range(CH):
                        up(g, u, c)
                        if c >= LAG:
                            down(g, c - LAG)
                        elif not first:
                            down(g - 1, c - LAG + CH)
                        if c == TURN_OUT and not first:
                            turn_out(g - 1, False)
                        if c == TURN and not last:
                            turn_n(g + 1, first)
                        if c == SCORES and not last:
                            score_tokens(g + 1)
                        if c == TURN_COMB and not last:
                            turn_comb(g + 1)

                pe.wait_ge(gate_loaded, 16)
                pe.sem_inc(hidden_used, AHEAD)
                turn_n(0, True)
                score_tokens(0)
                turn_comb(0)
                pe.wait_ge(spread_ready, 1)
                pe.wait_ge(split_hi, len(pieces))
                pe.wait_ge(split_lo, len(pieces))
                group(0, 0, True, False)
                with pe.Fori(0, GROUPS1 // 2 - 1) as p:
                    group(2 * p + 1, 1, False, False)
                    group(2 * p + 2, 0, False, False)
                group(GROUPS1 - 1, 1, False, True)
                for c in range(CH - LAG, CH):
                    down(GROUPS1 - 1, c)
                turn_out(GROUPS1 - 1, True)

            @block.scalar
            def _(act):
                def copy_nT(g):
                    act.wait_ge(n_turned, START + g + 1)
                    act.wait_ge(scores_done, START + g)
                    act.wait_ge(parts_ready, START + g)
                    nc.scalar.copy(nT[:, :], ps_turn[:, :]).then_inc(nT_ready, 1)

                def weights_high(first, end):
                    for n in range(first, end):
                        w, _, _, lo, hi = pieces[n]
                        act.wait_ge(weights_loaded[n % 2], loaded(n))
                        nc.scalar.copy(w[0][:, lo:hi, :].rearrange("p c m -> p (c m)"),
                                       stage[n % 2][:, 0:hi - lo, :].rearrange("p c m -> p (c m)"))\
                            .then_inc(split_hi, 1)

                def raise_power(g):
                    act.wait_ge(below_ready, g + 1)
                    nc.scalar.activation(power[:, :, :].rearrange("p t e -> p (t e)"),
                                         power[:, :, :].rearrange("p t e -> p (t e)"),
                                         ACT.Exp).then_inc(power_ready, 1)

                def copy_combT(g, u, first):
                    act.wait_ge(comb_turned, START + g + 1)
                    if not first:
                        act.wait_ge(spread_done, ROUTED * (g - 1))
                    nc.scalar.copy(combT[u][:, :], ps_turn[:, :]).then_inc(combT_ready, 1)

                def copy_out(g):
                    act.wait_ge(hidden_used, CH * (g + 1) + AHEAD)
                    act.wait_ge(out_turned, START + g)
                    nc.scalar.copy(outT[:, :], ps_out[:, :]).then_inc(outT_ready, 1)

                def high_part(n, c):
                    act.wait_ge(hidden_ready, n + AHEAD + 1)
                    act.wait_ge(hidden_used, n + 1)
                    nc.scalar.copy(hidden_part[c % 2][0][:, :], hidden[c % 2]).then_inc(parts_hi, 1)

                def group(g, u, first, last):
                    for c in range(CH):
                        n = CH * g + c
                        act.wait_ge(x1_done, n + 1)
                        act.wait_ge(gated_ready, n + 1)
                        nc.scalar.activation(silu[c % 2], ps1[c % 2][:, :], ACT.Silu)\
                            .then_inc(silu_ready, 1)
                        if c or not first:
                            high_part(n - 1, c - 1)
                        if c == COPY_OUT and not first:
                            copy_out(g - 1)
                        if c == COPY_N and not last:
                            copy_nT(g + 1)
                        if c == POWER and not last:
                            raise_power(g + 1)
                        if c == COPY_COMB and not last:
                            copy_combT(g + 1, 1 - u, False)

                act.sem_inc(silu_ready, AHEAD)
                weights_high(0, 4)
                copy_nT(0)
                weights_high(4, 7)
                raise_power(0)
                weights_high(7, len(pieces))
                copy_combT(0, 0, True)
                group(0, 0, True, False)
                with act.Fori(0, GROUPS1 // 2 - 1) as p:
                    group(2 * p + 1, 1, False, False)
                    group(2 * p + 2, 0, False, False)
                group(GROUPS1 - 1, 1, False, True)
                high_part(GROUPS1 * CH - 1, CH - 1)
                copy_out(GROUPS1 - 1)

            @block.vector
            def _(dve):
                def statistics(g):
                    for t in range(GT):
                        nc.vector.bn_stats(stats[:, t, :], tile_of(g, t)).then_inc(ln_stats, 1)

                def mean_variance(g):
                    dve.wait_ge(ln_stats, GT * (g + 1))
                    stand_alone(dve, dve_seen)
                    for t in range(GT):
                        nc.vector.bn_aggr(mean_var[:, t, :], stats[:, t, :]).then_inc(ln_var, 1)

                def normalise(g):
                    dve.wait_ge(ln_root, g + 1)
                    dve.wait_ge(n_turned, START + g)
                    for t in range(GT):
                        nc.vector.tensor_scalar(n_sb[:, t, :], tile_of(g, t), mean_var[:, t, 0:1], rstd[:, t:t + 1],
                                                ALU.subtract, ALU.mult).then_inc(n_ready, 1)

                def part_nT(g, u, first):
                    hi, lo = nT_part[u]
                    dve.wait_ge(nT_ready, g + 1)
                    if not first:
                        dve.wait_ge(x3_done, CH * (g - 1))
                    nc.vector.tensor_copy(hi[:, :], nT[:, :]).then_inc(nT_hi, 1)
                    dve.wait_ge(nT_hi, g + 1)
                    nc.vector.tensor_tensor(lo[:, :], nT[:, :], plain(hi[:, :]), ALU.subtract).then_inc(parts_ready, 1)

                def weights_low(first, end):
                    for n in range(first, end):
                        w, _, _, lo, hi = pieces[n]
                        dve.wait_ge(split_hi, n + 1)
                        nc.vector.tensor_tensor(w[1][:, lo:hi, :], stage[n % 2][:, 0:hi - lo, :],
                                                plain(w[0][:, lo:hi, :]), ALU.subtract).then_inc(split_lo, 1)

                def copy_scores(g):
                    dve.wait_ge(scores_done, START + g + 1)
                    nc.vector.tensor_copy(score[:, :, 0:E1],
                                          ps_turn[:, 0:GT * E1].rearrange("p (t e) -> p t e", e=E1))\
                        .then_inc(score_ready, 1)

                def eight_best(g):
                    dve.wait_ge(score_ready, g + 1)
                    stand_alone(dve, dve_seen)
                    for t in range(GT):
                        nc.vector.max(best[:, t, :], score[:, t, :]).then_inc(best_ready, 1)

                def below_best(g):
                    dve.wait_ge(best_ready, GT * (g + 1))
                    nc.vector.tensor_tensor(power[:, :, :], score[:, :, 0:E1],
                                            best[:, :, 0:1].broadcast_to([P, GT, E1]), ALU.subtract)\
                        .then_inc(below_ready, 1)
                    nc.vector.memset(best[:, :, TOP_K:], LEAST).then_inc(best_cut, 1)

                def mark_best(g):
                    dve.wait_ge(best_cut, g + 1)
                    stand_alone(dve, dve_seen)
                    for t in range(GT):
                        nc.vector.match_replace(marked[:, t, :], best[:, t, :], score[:, t, :], LEAST)\
                            .then_inc(marked_ready, 1)

                def find_chosen(g):
                    dve.wait_ge(marked_ready, GT * (g + 1))
                    nc.vector.tensor_tensor(chosen[:, :, :], marked[:, :, 0:E1], score[:, :, 0:E1], ALU.is_lt)\
                        .then_inc(chosen_ready, 1)

                def cut_power(g):
                    dve.wait_ge(chosen_ready, g + 1)
                    dve.wait_ge(power_ready, g + 1)
                    nc.vector.tensor_tensor(power[:, :, :], power[:, :, :], chosen[:, :, :], ALU.mult)\
                        .then_inc(power_cut, 1)

                def add_power(g):
                    dve.wait_ge(power_cut, g + 1)
                    nc.vector.tensor_reduce(total[:, :], power[:, :, :], AX.X, ALU.add).then_inc(total_ready, 1)

                def invert_total(g):
                    dve.wait_ge(total_ready, g + 1)
                    nc.vector.reciprocal(total[:, :], total[:, :]).then_inc(share_ready, 1)

                def divide(g):
                    dve.wait_ge(share_ready, g + 1)
                    nc.vector.tensor_tensor(power[:, :, :], power[:, :, :],
                                            total[:, :].unsqueeze(2).broadcast_to([P, GT, E1]), ALU.mult)\
                        .then_inc(comb_full, 1)

                def halves(x):
                    return x[:, :, :].rearrange("p t (i e) -> p t i e", i=2)

                def comb_high(g):
                    dve.wait_ge(comb_full, g + 1)
                    dve.wait_ge(comb_turned, START + g)
                    nc.vector.tensor_copy(comb[:, :, :, 0, :], halves(power)).then_inc(comb_hi, 1)

                def comb_low(g):
                    dve.wait_ge(comb_hi, g + 1)
                    nc.vector.tensor_tensor(comb[:, :, :, 1, :], halves(power), plain(comb[:, :, :, 0, :]),
                                            ALU.subtract)\
                        .then_inc(comb_ready, 1)

                def add_out(g, u, turn):
                    dve.wait_ge(out_turned, START + g + 1)
                    dve.wait_ge(stored[u], START + 16 * turn)
                    for s in range(GT // PT):
                        ins = nc.vector.tensor_tensor(
                            result[u][:, s * PT:(s + 1) * PT, :], keep.h[:, (GT // PT) * g + s, :, :],
                            ps_turn[:, s * PT * D:(s + 1) * PT * D].rearrange("p (t d) -> p t d", t=PT), ALU.add)
                    ins.then_inc(result_ready, 1)

                def low_part(n, c):
                    dve.wait_ge(parts_hi, n + 1)
                    dve.wait_ge(hidden_used, n + 1)
                    nc.vector.tensor_tensor(hidden_part[c % 2][1][:, :], hidden[c % 2],
                                            plain(hidden_part[c % 2][0][:, :]), ALU.subtract).then_inc(parts_lo, 1)

                def group(g, u, turn, first, last):
                    for c in range(CH):
                        n = CH * g + c
                        dve.wait_ge(silu_ready, n + AHEAD + 1)
                        dve.wait_ge(x3_done, n + 1)
                        if c < ROUTED:
                            nc.vector.tensor_tensor(gated[c % 2], silu[c % 2], ps3[c % 2][:, :],
                                                    ALU.mult).then_inc(gated_ready, 1)
                            dve.wait_ge(gated_ready, n + AHEAD + 1)
                            dve.wait_ge(spread_done, ROUTED * g + c + 1)
                            nc.vector.tensor_tensor(hidden[c % 2], gated[c % 2], ps_comb[c % 2][:, :],
                                                    ALU.mult).then_inc(hidden_ready, 1)
                        else:
                            dve.wait_ge(parts_lo, n - 1)
                            nc.vector.tensor_tensor(hidden[c % 2], silu[c % 2], ps3[c % 2][:, :],
                                                    ALU.mult).then_inc(gated_ready, 1)
                            dve.wait_ge(gated_ready, n + AHEAD + 1)
                            dve.sem_inc(hidden_ready, 1)
                        if c or not first:
                            low_part(n - 1, c - 1)
                        if c == ADD_OUT and not first:
                            add_out(g - 1, 1 - u, turn)
                        if not last:
                            if c == PARTS:
                                part_nT(g + 1, 1 - u, False)
                            if c in at:
                                at[c](g + 1)

                steps = [copy_scores, eight_best, below_best, mark_best, find_chosen, cut_power, add_power,
                         invert_total, divide, comb_high, comb_low]
                at = {STATS: statistics, VAR: mean_variance, NORM: normalise}
                at.update({CHOOSE + i: step for i, step in enumerate(steps)})
                dve.sem_inc(gated_ready, AHEAD)
                dve.sem_inc(hidden_ready, AHEAD)
                dve.wait_ge(const, CONSTS)
                statistics(0)
                mean_variance(0)
                normalise(0)
                weights_low(0, 4)
                part_nT(0, 0, True)
                for step in steps[:5]:
                    step(0)
                weights_low(4, 7)
                for step in steps[5:]:
                    step(0)
                weights_low(7, len(pieces))
                nc.vector.tensor_scalar(own_i[:, :], own_i[:, :], E1 // 2 - 1, None, ALU.bitwise_and)\
                    .then_inc(numbers, 1)
                dve.wait_ge(numbers, 1)
                nc.vector.tensor_copy(own[:, :], own_i[:, :]).then_inc(numbers, 1)
                nc.vector.tensor_copy(expert[:, :], expert_i[:, :]).then_inc(numbers, 1)
                dve.wait_ge(numbers, 3)
                nc.vector.tensor_scalar(spread[:, :, :].rearrange("p c (j i) -> p (c j) i", i=P // 2),
                                        expert[:, 0:E1 // 2].unsqueeze(2).broadcast_to([P, E1 // 2, P // 2]),
                                        own[:, 0:1], None, ALU.is_equal).then_inc(spread_ready, 1)
                dve.wait_ge(split_lo, len(pieces))
                group(0, 0, 0, True, False)
                with dve.Fori(0, GROUPS1 // 2 - 1) as p:
                    group(2 * p + 1, 1, p, False, False)
                    group(2 * p + 2, 0, p, False, False)
                group(GROUPS1 - 1, 1, GROUPS1 // 2 - 1, False, True)
                low_part(GROUPS1 * CH - 1, CH - 1)
                add_out(GROUPS1 - 1, 1, GROUPS1 // 2 - 1)
        nc.clear_and_free_semaphores(sems)
        nc.all_engine_barrier()


def initialise(nc, keep):
    zeroed, ready, spare_ready = (nc.alloc_semaphore(n) for n in ("i_zeroed", "i_ready", "i_spare_ready"))
    with nc.Block() as block:
        @block.gpsimd
        def _(pool):
            make_identity(nc, pool, keep.ident, zeroed, ready)
            nc.gpsimd.memset(keep.tokens[:, E0 * CT:], 0).then_inc(spare_ready, 1)
    nc.clear_and_free_semaphores([zeroed, ready, spare_ready])
    nc.all_engine_barrier()


class Keep:

    def __init__(self, nc, ctx):
        def sb(name, shape, dt=F32):
            return ctx.enter_context(nc.sbuf_tensor("keep_" + name, shape, dt))

        self.ident = sb("ident", [P, P])
        self.h = sb("h", [P, B, PT, D])
        self.top_f32 = sb("top_f32", [P, B * H0])
        self.top_row = sb("top_row", [P, (B + 2) * H0], I32)
        self.tokens = sb("tokens", [P, (E0 + 4) * CT], I32)


def build(nc, dram, out):
    def scratch(name, shape):
        return nc.dram_tensor(name, shape, F32, kind="Internal").ap()

    def part(prefix, **more):
        found = {name[len(prefix):]: ap for name, ap in dram.items() if name.startswith(prefix)}
        found.update(more)
        return found

    q_rows = scratch("q_rows", (B * L * H0, HD0))
    token_rows = scratch("token_rows", (TOK, ROW))
    with ExitStack() as ctx:
        keep = Keep(nc, ctx)
        initialise(nc, keep)
        tok = part("L0_tok_", x=dram["x"], xT=dram["xT"], q_rows=q_rows)
        select_queries(nc, tok, keep)
        token_layer(nc, tok, keep)
        windowed_attention(nc, part("L0_attn_"), keep)
        ffn = part("L0_ffn_", token_rows=token_rows, lists=scratch("lists", (TOK,)),
                   sum0=scratch("sum0", (TOK, D)), sum1=scratch("sum1", (TOK, D)))
        route(nc, ffn, keep)
        experts(nc, ffn, keep)
        delta_rule(nc, part("L1_attn_"), keep)
        expert_ffn(nc, part("L1_ffn_", out=out.rearrange("b l d -> (b l) d")), keep)


def lay_out(inputs):
    x = dict(inputs)
    x["xT"] = x["x"].transpose(0, 2, 1)
    x["L0_tok_f1_b"] = x["L0_tok_f1_b"].reshape(FC, P).T
    x["L0_tok_conv_w"] = x["L0_tok_conv_w"].transpose(1, 2, 0)
    x["L0_ffn_b_upT"] = x.pop("L0_ffn_b_up").T
    x["L1_attn_WT"] = x.pop("L1_attn_W").T
    for name in ("L1_attn_eta", "L1_attn_lam_logit"):
        x[name] = x[name].reshape(1)
    for name in ("w_gate", "w_sg", "w_su", "w_sd"):
        x[f"L1_ffn_{name}T"] = x.pop(f"L1_ffn_{name}").T
    for name in ("w1", "w3"):
        x[f"L1_ffn_{name}T"] = x.pop(f"L1_ffn_{name}").reshape(-1, D).T
    x["L1_ffn_w2"] = x["L1_ffn_w2"].reshape(-1, D)
    return x


def kernel(**inputs):
    import numpy as np
    import concourse.bacc as bacc
    from concourse.bass_utils import run_bass_kernel_spmd

    nc = bacc.Bacc("TRN2", target_bir_lowering=False, num_devices=1)
    arrays, dram = {}, {}
    for name, a in lay_out({name: np.asarray(a) for name, a in inputs.items()}).items():
        a = np.ascontiguousarray(a).reshape(a.shape)
        arrays[f"in_{name}"] = a
        dram[name] = nc.dram_tensor(f"in_{name}", a.shape, mybir.dt.from_np(a.dtype), kind="ExternalInput").ap()
    out = nc.dram_tensor("out", (B, LP, D), F32, kind="ExternalOutput").ap()
    build(nc, dram, out)
    return run_bass_kernel_spmd(nc, [arrays], core_ids=[0]).results[0]["out"]
```
